# Optimizing a Trainium2 kernel written in Bass

```python
import numpy as np
import jax
import jax.numpy as jnp

def _softmax(x, axis=-1):
    return jax.nn.softmax(x, axis=axis)

def _gelu(x):
    return jax.nn.gelu(x, approximate=True)

def _silu(x):
    return jax.nn.silu(x)

def _sigmoid(x):
    return jax.nn.sigmoid(x)

def _layernorm(x, axis=-1, eps=1e-05):
    m = jnp.mean(x, axis=axis, keepdims=True)
    v = jnp.var(x, axis=axis, keepdims=True)
    return (x - m) / jnp.sqrt(v + eps)

def _scatter_add(tgt, idx, src, axis=0):
    return tgt.at[idx].add(src)

def _segment_sum(src, seg, n):
    return jax.ops.segment_sum(src, seg, n)
kernel_name = 'mk_decoder_postln_d1_seqx_r4_2f5ab5'

def setup_inputs(seed: int=0):
    np.random.seed(seed)
    _w = jnp.asarray

    def _rec_inputs():
        import jax
        import jax.numpy as jnp
        _rk = jax.random.key(seed)
        x = -0.0002928 + 1 * jax.random.normal(jax.random.fold_in(_rk, 1), (8, 256, 256), jnp.float32)
        _lenS = 256 - jax.random.randint(jax.random.fold_in(_rk, 7), (8,), 0, max(1, 256 // 4) + 1, jnp.int32)
        _lenS2 = 256 - jax.random.randint(jax.random.fold_in(_rk, 8), (8,), 0, max(1, 256 // 4) + 1, jnp.int32)
        _ctx_1024P = jax.random.normal(jax.random.fold_in(_rk, 11), (8, 16, 256), jnp.float32)
        _ctx_1024c = jax.random.dirichlet(jax.random.fold_in(_rk, 511), 0.3 * jnp.ones((16,), jnp.float32), (8, 256))
        _ctx_1024t = jnp.einsum('bsk,bkd->bsd', _ctx_1024c, _ctx_1024P)
        _ctx_1024t = _ctx_1024t * jax.lax.rsqrt(jnp.mean(jnp.square(_ctx_1024t)) + 1e-12) * 0.953939
        ctx_1024 = -1.39393e-06 + 0.999914 * (_ctx_1024t + 0.3 * jax.random.normal(jax.random.fold_in(_rk, 611), (8, 256, 256), jnp.float32))
        return (x, ctx_1024)
    x, ctx_1024 = _rec_inputs()

    def _L0_attn_setup():
        import jax, jax.numpy as jnp
        import numpy as np
        B, T, D = (4, 512, 256)
        H = 4
        K = D // H
        V = D // H
        M = 64
        GATE_LOGIT_NORMALIZER = 8.0
        NORM_EPS = 1e-05

        def _swish(x):
            return x * jax.nn.sigmoid(x)

        def _gsa_recurrence(q, k, v, s, g, scale):
            b, t, h, dk = q.shape
            dv = v.shape[-1]
            m = s.shape[-1]

            def step(carry, inp):
                hk, hv = carry
                q_t, k_t, v_t, s_t, g_t = inp
                ge = jnp.exp(g_t)
                hk = hk * ge[:, :, None, :] + k_t[..., :, None] * s_t[..., None, :]
                logits = jnp.einsum('bhk,bhkm->bhm', q_t * scale, hk)
                p = jax.nn.softmax(logits, axis=-1)
                hv = hv * ge[..., :, None] + s_t[..., :, None] * v_t[..., None, :]
                o_t = jnp.einsum('bhm,bhmv->bhv', p, hv)
                return ((hk, hv), o_t)
            init = (jnp.zeros((b, h, dk, m), q.dtype), jnp.zeros((b, h, m, dv), q.dtype))
            xs = tuple((jnp.moveaxis(a, 1, 0) for a in (q, k, v, s, g)))
            _, o = jax.lax.scan(step, init, xs)
            return jnp.moveaxis(o, 0, 1)
        key = jax.random.key(seed)
        ks = jax.random.split(key, 6)
        sc = lambda n: 1.0 / np.sqrt(n)
        return {'x': jax.random.normal(ks[0], (B, T, D), jnp.float32), 'Wq': jax.random.normal(ks[1], (D, H * K), jnp.float32) * sc(D), 'Wk': jax.random.normal(ks[2], (D, H * K), jnp.float32) * sc(D), 'Wv': jax.random.normal(ks[3], (D, H * V), jnp.float32) * sc(D), 'Wf': jax.random.normal(ks[4], (D, H * M), jnp.float32) * sc(D), 'g_norm_w': jnp.ones((V,), jnp.float32), 'Wo': jax.random.normal(ks[5], (H * V, D), jnp.float32) * sc(H * V)}
    _L0_attn_all = _L0_attn_setup()
    _L0_attn_in = {k: v for k, v in _L0_attn_all.items() if k in ('Wq', 'Wk', 'Wv', 'Wf', 'g_norm_w', 'Wo')}
    del _L0_attn_all

    def _L0_xattn_setup():
        import jax, jax.numpy as jnp
        import numpy as np
        SCALE_BASE = 512.0
        GN_EPS = 1e-05

        def _xpos(x, downscale):
            L, D = (x.shape[-2], x.shape[-1])
            half = D // 2
            base = (jnp.arange(0, D, 2, dtype=jnp.float32) + 0.4 * D) / (1.4 * D)
            min_pos = -(L // 2)
            power = (jnp.arange(min_pos, min_pos + L, dtype=jnp.float32) / SCALE_BASE)[:, None]
            scale = base[None, :] ** power
            inv_freq = 1.0 / 10000.0 ** (jnp.arange(half, dtype=jnp.float32) / half)
            ang = jnp.arange(L, dtype=jnp.float32)[:, None] * inv_freq[None, :]
            sin, cos = (jnp.sin(ang), jnp.cos(ang))
            if downscale:
                scale = 1.0 / scale
            sin_s = jnp.repeat(sin * scale, 2, axis=-1)
            cos_s = jnp.repeat(cos * scale, 2, axis=-1)
            x1, x2 = (x[..., ::2], x[..., 1::2])
            rot = jnp.stack((-x2, x1), axis=-1).reshape(x.shape)
            return x * cos_s + rot * sin_s

        def _decay_mask(L, H):
            gammas = 1.0 - jnp.exp(jnp.linspace(np.log(1.0 / 32.0), np.log(1.0 / 512.0), H)).astype(jnp.float32)
            idx = jnp.arange(L)
            dist = idx[:, None] - idx[None, :]
            causal = dist >= 0
            d = jnp.maximum(dist, 0).astype(jnp.float32)
            return jnp.where(causal[None], gammas[:, None, None] ** d[None], 0.0)
        key = jax.random.key(seed)
        ks = jax.random.split(key, 9)
        B, L, D, H = (2, 512, 256, 16)
        hd = D // H
        return {'query': jax.random.normal(ks[0], (B, L, D), jnp.float32), 'key': jax.random.normal(ks[1], (B, L, D), jnp.float32), 'value': jax.random.normal(ks[2], (B, L, D), jnp.float32), 'W_Q': jax.random.normal(ks[3], (H, D, hd), jnp.float32) / D, 'W_K': jax.random.normal(ks[4], (H, D, hd), jnp.float32) / D, 'W_V': jax.random.normal(ks[5], (H, D, hd), jnp.float32) / D, 'g_w': jax.random.normal(ks[6], (D, D), jnp.float32) * (2.0 / (D + D)) ** 0.5, 'g_b': jnp.zeros((D,), jnp.float32), 'out_w': jax.random.normal(ks[7], (D, D), jnp.float32) * (2.0 / (D + D)) ** 0.5, 'out_b': jnp.zeros((D,), jnp.float32)}
    _L0_xattn_all = _L0_xattn_setup()
    _L0_xattn_in = {k: v for k, v in _L0_xattn_all.items() if k in ('W_Q', 'W_K', 'W_V', 'g_w', 'g_b', 'out_w', 'out_b')}
    del _L0_xattn_all

    def _L0_ffn_setup():
        import jax, jax.numpy as jnp
        import numpy as np
        N_EMBD = 256
        N_STATE = 1024
        key = jax.random.key(seed)
        k_x, k_w1, k_b1, k_w2, k_b2 = jax.random.split(key, 5)
        x = jax.random.normal(k_x, (4, 512, N_EMBD), dtype=jnp.float32)
        w1 = jax.random.normal(k_w1, (N_EMBD, N_STATE), dtype=jnp.float32) * (1.0 / np.sqrt(N_EMBD))
        b1 = jax.random.normal(k_b1, (N_STATE,), dtype=jnp.float32) * 0.02
        w2 = jax.random.normal(k_w2, (N_STATE, N_EMBD), dtype=jnp.float32) * (1.0 / np.sqrt(N_STATE))
        b2 = jax.random.normal(k_b2, (N_EMBD,), dtype=jnp.float32) * 0.02
        return {'x': x, 'w1': w1, 'b1': b1, 'w2': w2, 'b2': b2}
    _L0_ffn_all = _L0_ffn_setup()
    _L0_ffn_in = {k: v for k, v in _L0_ffn_all.items() if k in ('w1', 'b1', 'w2', 'b2')}
    del _L0_ffn_all
    return {'x': x, 'ctx_1024': ctx_1024, 'L0_attn_Wq': _L0_attn_in['Wq'], 'L0_attn_Wk': _L0_attn_in['Wk'], 'L0_attn_Wv': _L0_attn_in['Wv'], 'L0_attn_Wf': _L0_attn_in['Wf'], 'L0_attn_g_norm_w': _L0_attn_in['g_norm_w'], 'L0_attn_Wo': _L0_attn_in['Wo'], 'L0_xattn_W_Q': _L0_xattn_in['W_Q'], 'L0_xattn_W_K': _L0_xattn_in['W_K'], 'L0_xattn_W_V': _L0_xattn_in['W_V'], 'L0_xattn_g_w': _L0_xattn_in['g_w'], 'L0_xattn_g_b': _L0_xattn_in['g_b'], 'L0_xattn_out_w': _L0_xattn_in['out_w'], 'L0_xattn_out_b': _L0_xattn_in['out_b'], 'L0_ffn_w1': _L0_ffn_in['w1'], 'L0_ffn_b1': _L0_ffn_in['b1'], 'L0_ffn_w2': _L0_ffn_in['w2'], 'L0_ffn_b2': _L0_ffn_in['b2']}

def reference(x, ctx_1024, L0_attn_Wq, L0_attn_Wk, L0_attn_Wv, L0_attn_Wf, L0_attn_g_norm_w, L0_attn_Wo, L0_xattn_W_Q, L0_xattn_W_K, L0_xattn_W_V, L0_xattn_g_w, L0_xattn_g_b, L0_xattn_out_w, L0_xattn_out_b, L0_ffn_w1, L0_ffn_b1, L0_ffn_w2, L0_ffn_b2):
    import jax
    import jax.numpy as jnp

    def _L0_attn_ref(x, Wq, Wk, Wv, Wf, g_norm_w, Wo):
        import jax, jax.numpy as jnp
        import numpy as np
        B, T, D = (4, 512, 256)
        H = 4
        K = D // H
        V = D // H
        M = 64
        GATE_LOGIT_NORMALIZER = 8.0
        NORM_EPS = 1e-05

        def _swish(x):
            return x * jax.nn.sigmoid(x)

        def _gsa_recurrence(q, k, v, s, g, scale):
            b, t, h, dk = q.shape
            dv = v.shape[-1]
            m = s.shape[-1]

            def step(carry, inp):
                hk, hv = carry
                q_t, k_t, v_t, s_t, g_t = inp
                ge = jnp.exp(g_t)
                hk = hk * ge[:, :, None, :] + k_t[..., :, None] * s_t[..., None, :]
                logits = jnp.einsum('bhk,bhkm->bhm', q_t * scale, hk)
                p = jax.nn.softmax(logits, axis=-1)
                hv = hv * ge[..., :, None] + s_t[..., :, None] * v_t[..., None, :]
                o_t = jnp.einsum('bhm,bhmv->bhv', p, hv)
                return ((hk, hv), o_t)
            init = (jnp.zeros((b, h, dk, m), q.dtype), jnp.zeros((b, h, m, dv), q.dtype))
            xs = tuple((jnp.moveaxis(a, 1, 0) for a in (q, k, v, s, g)))
            _, o = jax.lax.scan(step, init, xs)
            return jnp.moveaxis(o, 0, 1)
        b, t, d = x.shape
        q = _swish((x @ Wq).reshape(b, t, H, K))
        k = _swish((x @ Wk).reshape(b, t, H, K))
        v = (x @ Wv).reshape(b, t, H, V)
        f = jax.nn.log_sigmoid((x @ Wf).reshape(b, t, H, M)) / GATE_LOGIT_NORMALIZER
        s = 1.0 - jnp.exp(f)
        o = _gsa_recurrence(q, k, v, s, f, scale=K ** (-0.5))
        o = o * jax.lax.rsqrt(jnp.mean(o * o, axis=-1, keepdims=True) + NORM_EPS) * g_norm_w
        return o.reshape(b, t, H * V) @ Wo

    def _L0_xattn_ref(query, key, value, W_Q, W_K, W_V, g_w, g_b, out_w, out_b):
        import jax, jax.numpy as jnp
        import numpy as np
        SCALE_BASE = 512.0
        GN_EPS = 1e-05

        def _xpos(x, downscale):
            L, D = (x.shape[-2], x.shape[-1])
            half = D // 2
            base = (jnp.arange(0, D, 2, dtype=jnp.float32) + 0.4 * D) / (1.4 * D)
            min_pos = -(L // 2)
            power = (jnp.arange(min_pos, min_pos + L, dtype=jnp.float32) / SCALE_BASE)[:, None]
            scale = base[None, :] ** power
            inv_freq = 1.0 / 10000.0 ** (jnp.arange(half, dtype=jnp.float32) / half)
            ang = jnp.arange(L, dtype=jnp.float32)[:, None] * inv_freq[None, :]
            sin, cos = (jnp.sin(ang), jnp.cos(ang))
            if downscale:
                scale = 1.0 / scale
            sin_s = jnp.repeat(sin * scale, 2, axis=-1)
            cos_s = jnp.repeat(cos * scale, 2, axis=-1)
            x1, x2 = (x[..., ::2], x[..., 1::2])
            rot = jnp.stack((-x2, x1), axis=-1).reshape(x.shape)
            return x * cos_s + rot * sin_s

        def _decay_mask(L, H):
            gammas = 1.0 - jnp.exp(jnp.linspace(np.log(1.0 / 32.0), np.log(1.0 / 512.0), H)).astype(jnp.float32)
            idx = jnp.arange(L)
            dist = idx[:, None] - idx[None, :]
            causal = dist >= 0
            d = jnp.maximum(dist, 0).astype(jnp.float32)
            return jnp.where(causal[None], gammas[:, None, None] ** d[None], 0.0)
        B, L, D = query.shape
        H = W_Q.shape[0]
        q = jnp.einsum('bld,hde->bhle', query, W_Q)
        k = jnp.einsum('bld,hde->bhle', key, W_K)
        v = jnp.einsum('bld,hde->bhle', value, W_V)
        q = _xpos(q, downscale=False)
        k = _xpos(k, downscale=True)
        sim = jnp.einsum('bhnd,bhsd->bhns', q, k) * _decay_mask(L, H)[None]
        ret = jnp.einsum('bhns,bhsd->bhnd', sim, v)
        mu = ret.mean(axis=-1, keepdims=True)
        var = ret.var(axis=-1, keepdims=True)
        ret = (ret - mu) / jnp.sqrt(var + GN_EPS)
        ret = ret.transpose(0, 2, 1, 3).reshape(B, L, D)
        gate = jax.nn.silu(query @ g_w.T + g_b)
        return ret * gate @ out_w.T + out_b

    def _L0_ffn_ref(x, w1, b1, w2, b2):
        import jax, jax.numpy as jnp
        import numpy as np
        N_EMBD = 256
        N_STATE = 1024
        h = jax.nn.gelu(jnp.einsum('bse,eh->bsh', x, w1) + b1, approximate=False)
        return jnp.einsum('bsh,he->bse', h, w2) + b2
    x = _layernorm(x + _L0_attn_ref(x, L0_attn_Wq, L0_attn_Wk, L0_attn_Wv, L0_attn_Wf, L0_attn_g_norm_w, L0_attn_Wo), axis=-1)
    x = _layernorm(x + _L0_xattn_ref(x, ctx_1024, ctx_1024, L0_xattn_W_Q, L0_xattn_W_K, L0_xattn_W_V, L0_xattn_g_w, L0_xattn_g_b, L0_xattn_out_w, L0_xattn_out_b), axis=-1)
    x = _layernorm(x + _L0_ffn_ref(x, L0_ffn_w1, L0_ffn_b1, L0_ffn_w2, L0_ffn_b2), axis=-1)
    return x

_drawn_inputs = setup_inputs


def setup_inputs(seed=0):
    import zlib

    import numpy as np

    out = dict(_drawn_inputs(seed))
    spreads = {'L0_attn_g_norm_w': (1.0, 0.2), 'L0_xattn_g_b': (0.0, 0.1), 'L0_xattn_out_b': (0.0, 0.1)}
    factors = {'L0_attn_Wq': 6.591, 'L0_attn_Wk': 6.3, 'L0_ffn_b1': 5.053, 'L0_ffn_b2': 3.46}
    for name, (base, spread) in spreads.items():
        noise = np.random.default_rng([zlib.crc32(name.encode()), seed]).standard_normal(out[name].shape)
        drawn = base * np.exp(spread * noise) if base else spread * noise
        out[name] = jnp.asarray(drawn.astype(out[name].dtype))
    for name, factor in factors.items():
        out[name] = (out[name] * factor).astype(out[name].dtype)
    return out
```

```python
import numpy as np
import concourse.bass as bass
from concourse import mybir
from concourse.alu_op_type import AluOpType as ALU

F32 = mybir.dt.float32
ACT = mybir.ActivationFunctionType
AX = mybir.AxisListType

B, T, D = 8, 256, 256
P = 128
NC = T // P
KK = D // P
HA, MA = 4, 64
HB, EB = 16, 16
F = 1024
NF = F // P
TT = 512
NT = B * T // TT
EPS = 1e-5
BIG = 1e30
PACK = T * KK


def decoder_kernel(nc, x_tok, x_feat, c_feat, wq, wk, wv, wf, gcol, wo, rq, rk, rv, gw, gb, ow, ob,
                   w1, b1, w2, b2, ident, mask, decay_w, rope, parity, state_mask, out):
    def sb(name, shape):
        return nc.alloc_sbuf_tensor(name, shape, F32)

    def sem(name):
        return nc.alloc_semaphore(name)

    def halves(ap):
        return ap.rearrange("p (c d) -> p c d", c=NC)

    W2 = sb("W2", [P, NF, D])
    Wq, Wk, Wv, Wf = (W2[:, 2 * n:2 * n + 2, :] for n in range(4))
    Wo, Gcol = sb("Wo", [P, KK, D]), sb("Gcol", [P, 1])
    RQ, RK, RV, GW, OW = (sb(n, [P, KK, D]) for n in ("RQ", "RK", "RV", "GW", "OW"))
    GB, OB, B2 = sb("GB", [P, D]), sb("OB", [P, D]), sb("B2", [P, D])
    W1, B1 = sb("W1", [P, KK, F]), sb("B1", [P, NF])
    Ident = sb("Ident", [P, P])
    Mask = sb("Mask", [P, 2, P])
    DecayW = sb("DecayW", [P, 3, P])
    Rope = sb("Rope", [P, 4, NC, D])
    Parity = sb("Parity", [P, 2])
    StateMask = sb("StateMask", [P, KK, P])
    Half = sb("Half", [P, NC * HB])
    One, Eps, EpsA, EpsB = (sb(n, [P, 1]) for n in ("One", "Eps", "EpsA", "EpsB"))
    RVmean = sb("RVmean", [P, KK * HB])

    qT_all, kT_all = sb("qT_all", [P, B, PACK]), sb("kT_all", [P, B, PACK])
    v_all, e_all, f_all = sb("v_all", [P, B, PACK]), sb("e_all", [P, B, PACK]), sb("f_all", [P, B, PACK])
    x2_all, x2T_all = e_all, f_all

    kTs, qTs = sb("kTs", [P, PACK]), sb("qTs", [P, PACK])
    eq, ek, ex = sb("eq", [P, PACK]), sb("ek", [P, PACK]), sb("ex", [P, PACK])
    ex01, kb01 = sb("ex01", [P, D]), sb("kb01", [P, D])
    kb, kbT = sb("kb", [P, PACK]), sb("kbT", [P, KK, NC, P])
    Sm = sb("Sm", [P, 3, PACK])
    lg, pe_x, paT = sb("lg", [P, PACK]), sb("pe_x", [P, PACK]), sb("paT", [P, KK, NC, P])
    pa = pe_x
    mx, Zs, ms, zz, rn = (sb(n, [P, NC * HA]) for n in ("mx", "Zs", "ms", "zz", "rn"))
    PT = Sm
    Hv = sb("Hv", [P, D])
    osq = lg
    on, onT = sb("on", [P, PACK]), sb("onT", [P, KK, NC, P])
    xres, yA, x1 = sb("xres", [P, NC, D]), sb("yA", [P, NC, D]), sb("x1", [P, NC, D])
    bnA, mvA, rsA = sb("bnA", [P, NC, 6]), sb("mvA", [P, NC, 2]), sb("rsA", [P, NC])

    cT = sb("cT", [P, KK, T])
    x1b, x1T = sb("x1b", [P, NC, D]), sb("x1T", [P, KK, NC, P])
    qc, qs, kc, ks = (sb(n, [P, PACK]) for n in ("qc", "qs", "kc", "ks"))
    qx, kx, vb = qc, kc, sb("vb", [P, NC, D])
    gz, gt = sb("gz", [P, PACK]), sb("gt", [P, PACK])
    gate = gt
    qxT = sb("qxT", [P, KK, P])
    qxP = sb("qxP", [P, KK, NC, 2, P])
    kxT = sb("kxT", [P, KK, NC, P])
    St = sb("St", [P, KK, P])
    NR = 8
    RS = 3
    Sb = sb("Sb", [P, RS, PACK])
    rsq = gz
    rvar, rr = sb("rvar", [P, NC * HB]), sb("rr", [P, NC * HB])
    rnm, rgT = sb("rnm", [P, PACK]), sb("rgT", [P, KK, NC, P])
    rg = rnm
    yB, x2 = x1b, sb("x2", [P, NC, D])
    xT = [halves(qc[:]), halves(qs[:])]
    thq, thk, az = (Sb[:, 0, :], Sb[:, 1, :]), (Sb[:, 2, :], rnm[:]), (kc[:], ks[:])

    bnB, mvB, rsB = sb("bnB", [P, NC, 6]), sb("mvB", [P, NC, 2]), sb("rsB", [P, NC])

    hT = qT_all
    x2b, yF, xo = (kT_all[:, 2 * n:2 * n + 2, :].rearrange("p a (b d) -> p (a b) d", d=D) for n in range(3))
    bnF, mvF, rsF = sb("bnF", [P, 4, 6]), sb("mvF", [P, 4, 2]), sb("rsF", [P, 4])

    bank = [nc.alloc_psum_tensor(f"bank{n}", [P, 512], F32) for n in range(8)]

    s_w_loop0, s_w_a, s_w_b, s_w_f = sem("w_loop0"), sem("w_a"), sem("w_b"), sem("w_f")
    s_xT = [sem("xT_even"), sem("xT_odd")]
    s_xres, s_cT, s_out = sem("xres_in"), sem("cT_in"), sem("out_stored")
    s_half, s_wo, s_ow, s_rvm, s_rv = sem("half"), sem("wo_scaled"), sem("ow_halved"), sem("rv_mean"), sem("rv_centred")
    s_qp, s_kp, s_vp, s_zp = sem("q_psum"), sem("k_psum"), sem("v_psum"), sem("z_psum")
    s_thq, s_thk, s_v, s_az, s_e = sem("q_tanh"), sem("k_tanh"), sem("v_kept"), sem("z_abs"), sem("z_exp")
    s_q, s_k, s_mz, s_ln, s_f = sem("q_kept"), sem("k_kept"), sem("z_min"), sem("z_ln"), sem("f_kept")
    s_kTs, s_qTs, s_ex, s_sg = sem("kT_copied"), sem("qT_copied"), sem("gate_exp"), sem("slot_gain")
    s_Ep, s_E01p, s_eq, s_ek, s_ex01 = sem("E_psum"), sem("E01_psum"), sem("e_query"), sem("e_key"), sem("e_next")
    s_kb, s_kb01 = sem("key_gain"), sem("key_gain_next")
    s_Sp, s_Sm = sem("S_psum"), sem("S_masked")
    s_kbTp, s_kbT = sem("kbT_psum"), sem("kbT")
    s_Lp, s_lg, s_mx, s_lc, s_pe = sem("L_psum"), sem("logits"), sem("logit_max"), sem("logits_shifted"), sem("p_exp")
    s_Z, s_zz, s_pa, s_paTp, s_paT = sem("p_sum"), sem("p_sum_sq"), sem("p_decayed"), sem("paT_psum"), sem("paT")
    s_PTp, s_PT, s_Hvp, s_Hv = sem("PT_psum"), sem("PT_masked"), sem("Hv_psum"), sem("Hv")
    s_Op, s_osq, s_ms, s_rn0, s_rn, s_on = sem("O_psum"), sem("O_sq"), sem("O_ms"), sem("rn_var"), sem("rn"), sem("O_normed")
    s_onTp, s_onT, s_Yp, s_yA = sem("onT_psum"), sem("onT"), sem("Y_psum"), sem("yA")
    s_bnA, s_mvA, s_rsA, s_x1 = sem("bnA"), sem("mvA"), sem("rsA"), sem("x1")
    s_va, s_zz2 = sem("varA_eps"), sem("Z2_eps")
    s_x1b, s_x1Tp, s_x1T = sem("x1_plus_bias"), sem("x1T_psum"), sem("x1T")
    s_bqp, s_bkp, s_bvp, s_bgp = sem("bq_psum"), sem("bk_psum"), sem("bv_psum"), sem("bg_psum")
    s_qcs, s_kcs, s_qx, s_kx, s_vb = sem("q_rope_parts"), sem("k_rope_parts"), sem("q_roped"), sem("k_roped"), sem("bv")
    s_gz, s_gt, s_gate = sem("gate_z"), sem("gate_tanh"), sem("gate")
    s_qxTp, s_kxTp, s_qxT, s_qxP, s_kxT = sem("qxT_psum"), sem("kxT_psum"), sem("qxT"), sem("qxP"), sem("kxT")
    s_Stp, s_St = sem("state_psum"), sem("state")
    s_Sbp, s_Sb, s_ret = sem("ret_scores_psum"), sem("ret_scores"), sem("ret_group_summed")
    s_rsq, s_rvar, s_rr0, s_rr, s_rnm, s_rg = sem("ret_sq"), sem("ret_var"), sem("ret_var_eps"), sem("ret_rstd"), sem("ret_normed"), sem("ret_gated")
    s_rgTp, s_rgT, s_Y2p, s_yB = sem("rgT_psum"), sem("rgT"), sem("Y2_psum"), sem("yB")
    s_bnB, s_mvB, s_rsB, s_x2, s_x2k = sem("bnB"), sem("mvB"), sem("rsB"), sem("x2"), sem("x2_kept")
    s_vb2 = sem("varB_eps")
    s_x2Tp, s_x2T = sem("x2T_psum"), sem("x2T_kept")
    s_hp, s_h, s_hused = sem("h_psum"), sem("h_gelu"), sem("h_used")
    s_x2b, s_yFp, s_yF = sem("x2_plus_b2"), sem("yF_psum"), sem("yF")
    s_bnF, s_mvF, s_rsF, s_xo = sem("bnF"), sem("mvF"), sem("rsF"), sem("xo")
    s_vf = sem("varF_eps")

    def heads(ap, h):
        return ap.rearrange("p (g e) -> p g e", g=NC * h)

    def per_head(stat, h, e):
        return stat.unsqueeze(2).to_broadcast([P, NC * h, e])

    def after(eng, semaphore, count):
        if not isinstance(count, int) or count > 0:
            eng.wait_ge(semaphore, count)

    def quarters(ap, n):
        return ap.rearrange("p (h t) -> p h t", h=n)

    mask_two = Mask.ap().rearrange("p a t -> p (a t)").unsqueeze(1).to_broadcast([P, 2, 2 * P])
    causal_two = Mask[:, 0, :].unsqueeze(1).to_broadcast([P, 2, P])
    causal_four = Mask[:, 0, :].unsqueeze(1).to_broadcast([P, 4, P])

    def both_chunks(row_bias):
        return row_bias.unsqueeze(1).to_broadcast([P, NC, D])

    def swapped(ap):
        return ap.rearrange("p (n two) -> p n two", two=2)[:, :, ::-1]

    block = nc.Block()
    with block:
        @block.sync
        def _(sp):
            for w, src in ((Wf, wf), (Wv, wv), (Wq, wq), (Wk, wk)):
                sp.dma_start(w, src).then_inc(s_w_loop0, 16)

            def load_xT(j, r):
                if not isinstance(j, int):
                    sp.wait_ge(s_kp, 2 * j + r - 1)
                sp.dma_start(xT[r], x_feat[2 * j + r]).then_inc(s_xT[r], 16)

            load_xT(0, 0)
            load_xT(0, 1)
            for w, src in ((DecayW, decay_w), (Ident, ident), (Mask, mask), (Wo, wo), (Gcol, gcol)):
                sp.dma_start(w[:], src).then_inc(s_w_a, 16)
            with sp.Fori(1, B // 2) as j:
                load_xT(j, 0)
                load_xT(j, 1)
            for w, src in ((RQ, rq), (RK, rk), (RV, rv), (GW, gw), (OW, ow), (GB, gb), (OB, ob),
                           (Rope, rope), (Parity, parity), (StateMask, state_mask)):
                sp.dma_start(w[:], src).then_inc(s_w_b, 16)
            sp.dma_start(xres[:], x_tok[0]).then_inc(s_xres, 16)
            sp.dma_start(cT[:], c_feat[0]).then_inc(s_cT, 16)
            sp.wait_ge(s_kp, B)
            for w, src in ((W1, w1), (B1, b1), (W2, w2), (B2, b2)):
                sp.dma_start(w[:], src).then_inc(s_w_f, 16)
            with sp.Fori(1, B) as i:
                sp.wait_ge(s_yA, i)
                sp.dma_start(xres[:], x_tok[i]).then_inc(s_xres, 16)
                sp.wait_ge(s_bvp, i)
                sp.dma_start(cT[:], c_feat[i]).then_inc(s_cT, 16)
            with sp.Fori(0, NT) as n:
                sp.wait_ge(s_xo, 4 * n + 4)
                sp.dma_start(out[n], xo).then_inc(s_out, 16)
            sp.wait_ge(s_out, 16 * NT)

        @block.tensor
        def _(pe):
            mm, tr = nc.tensor.matmul, nc.tensor.transpose

            def project0(j, r):
                n = 2 * j + r
                pe.wait_ge(s_xT[r], 16 * (j + 1))
                if not isinstance(j, int):
                    pe.wait_ge(s_mz, n - 1)
                    pe.wait_ge(s_e, n - 1)
                for w, o, consumer, s in ((Wf, 3, None, s_zp), (Wv, 2, s_v, s_vp)):
                    if consumer is not None and not isinstance(j, int):
                        pe.wait_ge(consumer, n - 1)
                    for c in range(NC):
                        for kk in range(KK):
                            last = mm(bank[4 * r + o][:, c * D:(c + 1) * D], xT[r][:, kk, c * P:(c + 1) * P], w[:, kk, :],
                                      start=kk == 0, stop=kk == KK - 1)
                    last.then_inc(s, 1)
                for w, o, consumer, s in ((Wq, 0, s_q, s_qp), (Wk, 1, s_k, s_kp)):
                    if not isinstance(j, int):
                        pe.wait_ge(consumer, n - 1)
                    for g in range(KK):
                        for kk in range(KK):
                            last = mm(bank[4 * r + o][:, g * T:(g + 1) * T], w[:, kk, g * P:(g + 1) * P], xT[r][:, kk, :],
                                      start=kk == 0, stop=kk == KK - 1)
                    last.then_inc(s, 1)

            pe.wait_ge(s_w_loop0, 64)
            project0(0, 0)
            project0(0, 1)
            with pe.Fori(1, B // 2) as j:
                project0(j, 0)
                project0(j, 1)

            def a_decay(i):
                pe.wait_ge(s_f, i + 1)
                after(pe, s_onT, i)
                mm(bank[0][:, 0:D], DecayW[:, 0, :], f_all[:, i, 0:D], start=True, stop=True)
                mm(bank[0][:, D:2 * D], DecayW[:, 0, :], f_all[:, i, D:2 * D], start=True, stop=True).then_inc(s_Ep, 1)
                after(pe, s_yA, i)
                mm(bank[1][:, 0:D], DecayW[:, 1, :], f_all[:, i, 0:D], start=True, stop=False)
                mm(bank[1][:, 0:D], DecayW[:, 2, :], f_all[:, i, D:2 * D], start=False, stop=True).then_inc(s_E01p, 1)

            def a_scores(i):
                pe.wait_ge(s_kTs, i + 1)
                pe.wait_ge(s_qTs, i + 1)
                after(pe, s_Hv, i)
                after(pe, s_on, i)
                for g in range(KK):
                    for hh in range(2):
                        r = slice(64 * hh, 64 * hh + 64)
                        last = mm(bank[2 + hh][:, g * T:(g + 1) * T], kTs[r, g * T:g * T + P], qTs[r, g * T:(g + 1) * T],
                                  start=True, stop=True)
                last.then_inc(s_Sp, 1)
                pe.wait_ge(s_ek, i + 1)
                pe.wait_ge(s_ex01, i + 1)
                for g in range(KK):
                    for hh in range(2):
                        r = slice(64 * hh, 64 * hh + 64)
                        last = mm(bank[hh][:, g * P:(g + 1) * P], kTs[r, g * T + P:(g + 1) * T],
                                  qTs[r, g * T + P:(g + 1) * T], start=True, stop=True)
                last.then_inc(s_Sp, 1)

            def transposes(dst, src, ready, count, done):
                pe.wait_ge(ready, count)
                for g in range(KK):
                    for c in range(NC):
                        o = (g * NC + c) * P
                        last = tr(dst[:, o:o + P], src[:, c * D + g * P:c * D + (g + 1) * P], Ident[:])
                last.then_inc(done, 1)

            def a_kbT(i):
                pe.wait_ge(s_Sm, 4 * i + 4)
                transposes(bank[1], kb, s_kb, i + 1, s_kbTp)

            def a_logits(i):
                pe.wait_ge(s_kb, i + 1)
                pe.wait_ge(s_kb01, i + 1)
                for h in range(HA):
                    g, hh = h // 2, h % 2
                    m = slice(h * MA, (h + 1) * MA)
                    m1 = slice(D + h * MA, D + (h + 1) * MA)
                    mm(bank[2][:, m], Sm[:, hh, g * T:g * T + P], kb[:, m], start=True, stop=True)
                    mm(bank[2][:, m1], Sm[:, hh, g * T + P:(g + 1) * T], kb01[:, m], start=True, stop=False)
                    last = mm(bank[2][:, m1], Sm[:, 2, (2 * hh + g) * P:(2 * hh + g + 1) * P], kb[:, m1], start=False, stop=True)
                last.then_inc(s_Lp, 1)

            def a_paT(i):
                transposes(bank[3], pa, s_pa, i + 1, s_paTp)

            def a_weights(i):
                pe.wait_ge(s_kbT, i + 1)
                pe.wait_ge(s_paT, i + 1)
                for g in range(KK):
                    for c in range(NC):
                        for hh in range(2):
                            r, o = slice(64 * hh, 64 * hh + 64), (2 * g + c) * P
                            last = mm(bank[hh][:, o:o + P], kbT[r, g, c, :], paT[r, g, c, :], start=True, stop=True)
                last.then_inc(s_PTp, 1)

            def a_state(i):
                pe.wait_ge(s_lg, i + 1)
                for g in range(KK):
                    last = mm(bank[2][:, g * P:(g + 1) * P], kb01[:, g * P:(g + 1) * P], v_all[:, i, g * P:(g + 1) * P],
                              start=True, stop=True)
                last.then_inc(s_Hvp, 1)

            def a_out(i):
                pe.wait_ge(s_PT, 2 * i + 2)
                pe.wait_ge(s_Hv, i + 1)
                for g in range(KK):
                    mm(bank[3][:, D + g * P:D + (g + 1) * P], paT[:, g, 1, :], Hv[:, g * P:(g + 1) * P], start=True, stop=False,
                       skip_group_check=True)
                    for c in (1, 0):
                        for hh in range(2):
                            m = slice(c * D + (2 * g + hh) * MA, c * D + (2 * g + hh + 1) * MA)
                            last = mm(bank[3][:, m], PT[:, hh, (2 * g + c) * P:(2 * g + c + 1) * P], v_all[:, i, m],
                                      start=c == 0, stop=True, skip_group_check=True)
                last.then_inc(s_Op, 1)

            def project(dst, srcT, w, done):
                for c in range(NC):
                    for kk in range(KK):
                        last = mm(dst[:, c * D:(c + 1) * D], srcT[:, kk, c * P:(c + 1) * P] if len(srcT.shape) == 3
                                  else srcT[:, kk, c, :], w[:, kk, :], start=kk == 0, stop=kk == KK - 1)
                last.then_inc(done, 1)

            def a_onT(i):
                transposes(bank[0], on, s_on, i + 1, s_onTp)

            def a_project(i):
                pe.wait_ge(s_onT, i + 1)
                project(bank[1], onT, Wo, s_Yp)

            def b_x1T(i):
                after(pe, s_yB, i)
                transposes(bank[4], x1.ap().rearrange("p c d -> p (c d)"), s_x1, NC * (i + 1), s_x1Tp)

            def b_kv(i):
                pe.wait_ge(s_cT, 16 * (i + 1))
                after(pe, s_x2T, i)
                project(bank[6], cT, RK, s_bkp)
                project(bank[7], cT, RV, s_bvp)

            def b_qg(i):
                pe.wait_ge(s_x1T, i + 1)
                project(bank[5], x1T, RQ, s_bqp)
                project(bank[4], x1T, GW, s_bgp)

            def b_ropedT(i):
                transposes(bank[6], kx, s_kx, i + 1, s_kxTp)
                transposes(bank[5], qx, s_qx, i + 1, s_qxTp)

            def b_state(i):
                pe.wait_ge(s_vb, i + 1)
                for g in range(KK):
                    last = mm(bank[7][:, g * P:(g + 1) * P], kx[:, g * P:(g + 1) * P], vb[:, 0, g * P:(g + 1) * P],
                              start=True, stop=True)
                last.then_inc(s_Stp, 1)

            def b_scores(i, n):
                c, j = n // 4, n % 4
                r = slice(32 * j, 32 * j + 32)
                if n == 0:
                    pe.wait_ge(s_kxT, i + 1)
                    pe.wait_ge(s_qxP, i + 1)
                    pe.wait_ge(s_gz, i + 1)
                if n >= RS:
                    pe.wait_ge(s_Sb, NR * i + n - RS + 1)
                for g in range(KK):
                    last = mm(bank[4 + n % RS][:, g * T:(g + 1) * T], kxT[r, g, c, :], qxP[r, g, c, :, :], start=True, stop=True)
                last.then_inc(s_Sbp, 1)

            def b_sum(i, n):
                c, j = n // 4, n % 4
                pe.wait_ge(s_Sb, NR * i + n + 1)
                if n == 0:
                    pe.wait_ge(s_St, i + 1)
                    for g in range(KK):
                        mm(bank[7][:, D + g * P:D + (g + 1) * P], qxT[:, g, :], St[:, g, :], start=g == 0, stop=False,
                           skip_group_check=True)
                for g in range(KK):
                    for par in range(2):
                        h = 8 * g + 2 * j + par
                        last = mm(bank[7][:, c * D + h * EB:c * D + (h + 1) * EB],
                                  Sb[:, n % RS, (2 * g + par) * P:(2 * g + par + 1) * P],
                                  vb[:, c, h * EB:(h + 1) * EB], start=False, stop=True, skip_group_check=True)
                last.then_inc(s_ret, 1)

            def b_rgT(i):
                pe.wait_ge(s_Sb, NR * (i + 1))
                transposes(bank[4], rg, s_rg, i + 1, s_rgTp)

            def b_project(i):
                pe.wait_ge(s_rgT, i + 1)
                project(bank[5], rgT, OW, s_Y2p)

            def b_x2T(i):
                transposes(bank[6], x2.ap().rearrange("p c d -> p (c d)"), s_x2, NC * (i + 1), s_x2Tp)

            def step(a, b):
                if a is not None:
                    a_decay(a)
                    a_scores(a)
                if b is not None:
                    b_kv(b)
                    b_x1T(b)
                if a is not None:
                    a_kbT(a)
                if b is not None:
                    b_qg(b)
                if a is not None:
                    a_logits(a)
                if b is not None:
                    b_ropedT(b)
                    b_state(b)
                    b_scores(b, 0)
                    b_scores(b, 1)
                    b_scores(b, 2)
                if a is not None:
                    a_state(a)
                    a_paT(a)
                if b is not None:
                    for n in range(0, 3):
                        b_sum(b, n)
                        b_scores(b, n + RS)
                if a is not None:
                    a_weights(a)
                if b is not None:
                    for n in range(3, 5):
                        b_sum(b, n)
                        b_scores(b, n + RS)
                if a is not None:
                    a_out(a)
                if b is not None:
                    for n in range(5, NR):
                        b_sum(b, n)
                if a is not None:
                    a_onT(a)
                    a_project(a)
                if b is not None:
                    b_rgT(b)
                    b_project(b)
                    b_x2T(b)

            pe.wait_ge(s_w_a, 5 * 16)
            pe.wait_ge(s_v, B)
            pe.wait_ge(s_mz, B)
            pe.wait_ge(s_e, B)
            pe.wait_ge(s_q, B)
            pe.wait_ge(s_k, B)
            pe.wait_ge(s_wo, 1)
            step(0, None)
            pe.wait_ge(s_w_b, 10 * 16)
            pe.wait_ge(s_rv, 1)
            pe.wait_ge(s_ow, 1)
            step(1, 0)
            with pe.Fori(2, B) as i:
                step(i, i - 1)
            step(None, B - 1)

            def ffn_up(n, f):
                for kk in range(KK):
                    for rr2 in range(2):
                        last = mm(bank[f % 4][:, rr2 * T:(rr2 + 1) * T], W1[:, kk, f * P:(f + 1) * P],
                                  x2T_all[:, 2 * n + rr2, kk * T:(kk + 1) * T], start=kk == 0 and rr2 == 0, stop=kk == KK - 1,
                                  skip_group_check=True)
                last.then_inc(s_hp, 1)

            def ffn_down(n, f):
                pe.wait_ge(s_h, NF * n + f + 1)
                if f == 0:
                    after(pe, s_yF, 4 * n)
                for t in range(4):
                    last = mm(bank[4 + t // 2][:, (t % 2) * D:(t % 2 + 1) * D], hT[:, f, t * P:(t + 1) * P], W2[:, f, :],
                              start=f == 0 and t % 2 == 0, stop=f == NF - 1, skip_group_check=True)
                last.then_inc(s_hused, 1)

            pe.wait_ge(s_w_f, 4 * 16)
            pe.wait_ge(s_x2T, B)
            def ffn(n):
                for f in range(3):
                    ffn_up(n, f)
                for f in range(NF):
                    if f + 3 < NF:
                        if f + 3 >= 4:
                            pe.wait_ge(s_h, NF * n + f)
                        ffn_up(n, f + 3)
                    ffn_down(n, f)

            ffn(0)
            with pe.Fori(1, NT) as n:
                ffn(n)

        @block.scalar
        def _(act):
            activation = nc.scalar.activation

            def evacuate0(j, r):
                n = 2 * j + r
                act.wait_ge(s_zp, n + 1)
                if not isinstance(j, int):
                    act.wait_ge(s_e, n - 1)
                activation(az[r], bank[4 * r + 3][:], ACT.Abs).then_inc(s_az, 1)
                act.wait_ge(s_vp, n + 1)
                activation(v_all[:, n, :], bank[4 * r + 2][:], ACT.Copy).then_inc(s_v, 1)
                act.wait_ge(s_az, n + 1)
                activation(e_all[:, n, :], az[r], ACT.Exp, scale=-1.0).then_inc(s_e, 1)
                if not isinstance(j, int):
                    act.wait_ge(s_q, n - 1)
                    act.wait_ge(s_k, n - 1)
                act.wait_ge(s_qp, n + 1)
                activation(thq[r], bank[4 * r + 0][:], ACT.Tanh, scale=0.5).then_inc(s_thq, 1)
                act.wait_ge(s_kp, n + 1)
                activation(thk[r], bank[4 * r + 1][:], ACT.Tanh, scale=0.5).then_inc(s_thk, 1)

            evacuate0(0, 0)
            evacuate0(0, 1)
            with act.Fori(1, B // 2) as j:
                evacuate0(j, 0)
                evacuate0(j, 1)
            act.wait_ge(s_e, B)
            with act.Fori(0, B) as i:
                activation(e_all[:, i, :], e_all[:, i, :], ACT.Ln, bias=1.0).then_inc(s_ln, 1)

            def a_gains(i):
                act.wait_ge(s_f, i + 1)
                after(act, s_kb, i)
                after(act, s_kb01, i)
                activation(ex[:], f_all[:, i, :], ACT.Exp, scale=0.125).then_inc(s_ex, 1)
                act.wait_ge(s_Ep, i + 1)
                after(act, s_pa, i)
                activation(eq[:], bank[0][:], ACT.Exp).then_inc(s_eq, 1)
                activation(ek[:], bank[0][:], ACT.Exp, scale=-1.0).then_inc(s_ek, 1)
                act.wait_ge(s_E01p, i + 1)
                activation(ex01[:], bank[1][:, 0:D], ACT.Exp).then_inc(s_ex01, 1)

            def a_kbT(i):
                act.wait_ge(s_kbTp, i + 1)
                after(act, s_PTp, i)
                activation(kbT.ap().rearrange("p g c t -> p (g c t)"), bank[1][:], ACT.Copy).then_inc(s_kbT, 1)

            def a_exp(i):
                act.wait_ge(s_lc, i + 1)
                after(act, s_paTp, i)
                activation(pe_x[:], lg[:], ACT.Exp, scale=1.0 / 32.0).then_inc(s_pe, 1)

            def a_state(i):
                act.wait_ge(s_Hvp, i + 1)
                after(act, s_Op, i)
                for hh in range(2):
                    r = slice(64 * hh, 64 * hh + 64)
                    last = activation(Hv[r, :].rearrange("p (g m) -> p g m", g=KK)[:, :, 64 * hh:64 * hh + 64],
                                      bank[2][r, 0:D].rearrange("p (g m) -> p g m", g=KK)[:, :, 64 * hh:64 * hh + 64], ACT.Copy)
                last.then_inc(s_Hv, 1)

            def a_paT(i):
                act.wait_ge(s_paTp, i + 1)
                activation(paT.ap().rearrange("p g c t -> p (g c t)"), bank[3][:], ACT.Copy).then_inc(s_paT, 1)

            def a_square(i):
                act.wait_ge(s_Op, i + 1)
                after(act, s_ms, i)
                activation(osq[:], bank[3][:], ACT.Square).then_inc(s_osq, 1)

            def a_onT(i):
                act.wait_ge(s_onTp, i + 1)
                after(act, s_Yp, i)
                activation(onT.ap().rearrange("p g c t -> p (g c t)"), bank[0][:], ACT.Copy).then_inc(s_onT, 1)

            def b_x1T(i):
                act.wait_ge(s_x1Tp, i + 1)
                after(act, s_bgp, i)
                activation(x1T.ap().rearrange("p g c t -> p (g c t)"), bank[4][:], ACT.Copy).then_inc(s_x1T, 1)

            def b_v(i):
                act.wait_ge(s_bvp, i + 1)
                after(act, s_ret, NR * i)
                activation(vb.ap().rearrange("p c d -> p (c d)"), bank[7][:], ACT.Copy).then_inc(s_vb, 1)

            def b_gate(i):
                act.wait_ge(s_gz, i + 1)
                after(act, s_rg, i)
                activation(gt[:], gz[:], ACT.Tanh, scale=0.5).then_inc(s_gt, 1)

            def b_kxT(i):
                act.wait_ge(s_kxTp, i + 1)
                activation(kxT.ap().rearrange("p g c t -> p (g c t)"), bank[6][:], ACT.Copy).then_inc(s_kxT, 1)

            def b_qxT(i):
                act.wait_ge(s_qxTp, i + 1)
                qp = bank[5].ap().rearrange("p (g c t) -> p (g c) t", g=KK, c=NC)
                for par in range(2):
                    activation(qxP[:, :, :, par, :].rearrange("p g c t -> p (g c) t"), qp, ACT.Copy,
                               scale=Parity[:, par:par + 1])
                activation(qxT[:], bank[5].ap().rearrange("p (g c t) -> p g c t", g=KK, c=NC)[:, :, 1, :],
                           ACT.Copy).then_inc(s_qxP, 1)

            def b_square(i):
                act.wait_ge(s_ret, NR * (i + 1))
                act.wait_ge(s_gate, i + 1)
                activation(rsq[:], bank[7][:], ACT.Square).then_inc(s_rsq, 1)

            def b_rgT(i):
                act.wait_ge(s_rgTp, i + 1)
                after(act, s_Y2p, i)
                activation(rgT.ap().rearrange("p g c t -> p (g c t)"), bank[4][:], ACT.Copy).then_inc(s_rgT, 1)

            def b_x2T(i):
                act.wait_ge(s_x2Tp, i + 1)
                activation(x2T_all[:, i, :], bank[6][:], ACT.Copy).then_inc(s_x2T, 1)

            def step(a, b):
                if a is not None:
                    a_gains(a)
                if b is not None:
                    b_x1T(b)
                    b_v(b)
                if a is not None:
                    a_kbT(a)
                if b is not None:
                    b_kxT(b)
                    b_qxT(b)
                    b_gate(b)
                if a is not None:
                    a_exp(a)
                    a_state(a)
                    a_paT(a)
                    a_square(a)
                if b is not None:
                    b_square(b)
                if a is not None:
                    a_onT(a)
                if b is not None:
                    b_rgT(b)
                    b_x2T(b)

            act.wait_ge(s_half, 1)
            step(0, None)
            act.wait_ge(s_w_b, 10 * 16)
            step(1, 0)
            with act.Fori(2, B) as i:
                step(i, i - 1)
            step(None, B - 1)

            act.wait_ge(s_w_f, 4 * 16)
            def ffn(n):
                for f in range(NF):
                    act.wait_ge(s_hp, NF * n + f + 1)
                    after(act, s_hused, NF * n)
                    activation(hT[:, f, :], bank[f % 4][:], ACT.Gelu, bias=B1[:, f:f + 1]).then_inc(s_h, 1)

            ffn(0)
            with act.Fori(1, NT) as n:
                ffn(n)

        @block.vector
        def _(dve):
            v = nc.vector

            def evacuate0(j, r):
                n = 2 * j + r
                dve.wait_ge(s_az, n + 1)
                v.tensor_scalar(f_all[:, n, :], bank[4 * r + 3][:], 0.0, None, ALU.min).then_inc(s_mz, 1)
                dve.wait_ge(s_thq, n + 1)
                v.scalar_tensor_tensor(qT_all[:, n, :], thq[r], 1.0, bank[4 * r][:], ALU.add, ALU.mult).then_inc(s_q, 1)
                dve.wait_ge(s_thk, n + 1)
                v.scalar_tensor_tensor(kT_all[:, n, :], thk[r], 1.0, bank[4 * r + 1][:], ALU.add, ALU.mult).then_inc(s_k, 1)

            for tile, value in ((Hv, 0.0), (Half, -0.5), (One, 1.0), (Eps, EPS), (EpsA, MA * EPS), (EpsB, EB * EPS)):
                dve.memset(tile[:], value).then_inc(s_half, 1)
            evacuate0(0, 0)
            evacuate0(0, 1)
            with dve.Fori(1, B // 2) as j:
                evacuate0(j, 0)
                evacuate0(j, 1)
            dve.wait_ge(s_w_a, 5 * 16)
            v.tensor_scalar(Wo[:], Wo[:], Gcol[:, 0:1], MA ** 0.5, ALU.mult, ALU.mult).then_inc(s_wo, 1)

            def layer_norm(i, y, bn, mv, rs, s_y, s_bn, s_mv, s_rs, tiles, dst, s_dst, counts=1):
                dve.wait_ge(s_y, counts * (i + 1))
                for c in range(tiles):
                    v.bn_stats(bn[:, c, :], y[:, c, :]).then_inc(s_bn, 1)
                for c in range(tiles):
                    dve.wait_ge(s_bn, tiles * i + c + 1)
                    dve.nop(nofuse=True)
                    v.bn_aggr(mv[:, c, :], bn[:, c, :]).then_inc(s_mv, 1)
                dve.wait_ge(s_rs, i + 1)
                for c in range(tiles):
                    v.tensor_scalar(dst[:, c, :], y[:, c, :], mv[:, c, 0:1], rs[:, c:c + 1], ALU.subtract, ALU.mult)\
                        .then_inc(s_dst, 1)

            def a_keys(i):
                dve.wait_ge(s_ek, i + 1)
                dve.wait_ge(s_sg, i + 1)
                after(dve, s_Lp, i)
                v.scalar_tensor_tensor(kb[:], ek[:], BIG, ex[:], ALU.min, ALU.mult).then_inc(s_kb, 1)

            def a_mask(i):
                after(dve, s_Op, i)
                for n, b in enumerate((2, 3)):
                    dve.wait_ge(s_Sp, 2 * i + 1)
                    v.tensor_tensor(quarters(Sm[:, n, :], 2), quarters(bank[b][:], 2), mask_two, ALU.mult).then_inc(s_Sm, 1)
                for hh in range(2):
                    dve.wait_ge(s_Sp, 2 * i + 2)
                    v.tensor_tensor(quarters(Sm[:, 2, hh * T:(hh + 1) * T], 2), quarters(bank[hh][:, 0:T], 2), causal_two,
                                    ALU.mult).then_inc(s_Sm, 1)

            def a_softmax(i):
                dve.wait_ge(s_Lp, i + 1)
                dve.wait_ge(s_eq, i + 1)
                v.scalar_tensor_tensor(lg[:], eq[:], BIG, bank[2][:], ALU.min, ALU.mult).then_inc(s_lg, 1)
                dve.wait_ge(s_lg, i + 1)
                v.tensor_reduce(mx[:], heads(lg[:], HA), AX.X, ALU.max).then_inc(s_mx, 1)
                dve.wait_ge(s_mx, i + 1)
                v.tensor_tensor(heads(lg[:], HA), heads(lg[:], HA), per_head(mx[:], HA, MA), ALU.subtract).then_inc(s_lc, 1)

            def a_sum(i):
                dve.wait_ge(s_pe, i + 1)
                after(dve, s_zz, i)
                v.tensor_reduce(Zs[:], heads(pe_x[:], HA), AX.X, ALU.add).then_inc(s_Z, 1)
                dve.wait_ge(s_Z, i + 1)
                v.scalar_tensor_tensor(pa[:], eq[:], BIG, pe_x[:], ALU.min, ALU.mult).then_inc(s_pa, 1)

            def a_weights(i):
                for hh in range(2):
                    dve.wait_ge(s_PTp, i + 1)
                    v.tensor_tensor(quarters(PT[:, hh, :], 4), quarters(bank[hh][:], 4), causal_four, ALU.mult).then_inc(s_PT, 1)

            def a_norm(i):
                dve.wait_ge(s_osq, i + 1)
                after(dve, s_rn0, i)
                v.tensor_reduce(ms[:], heads(osq[:], HA), AX.X, ALU.add).then_inc(s_ms, 1)
                dve.wait_ge(s_rn, i + 1)
                v.tensor_tensor(heads(on[:], HA), heads(bank[3][:], HA), per_head(rn[:], HA, MA), ALU.mult).then_inc(s_on, 1)

            def a_residual(i):
                dve.wait_ge(s_Yp, i + 1)
                dve.wait_ge(s_xres, 16 * (i + 1))
                v.tensor_tensor(yA.ap().rearrange("p c d -> p (c d)"), xres.ap().rearrange("p c d -> p (c d)"), bank[1][:],
                                ALU.add).then_inc(s_yA, 1)
                after(dve, s_x1b, i)
                layer_norm(i, yA, bnA, mvA, rsA, s_yA, s_bnA, s_mvA, s_rsA, NC, x1, s_x1)

            def b_rope(i, src, s_ready, c_out, s_out, kind, s_done, *s_used):
                dve.wait_ge(s_ready, i + 1)
                for s in s_used:
                    after(dve, s, i)
                v.tensor_tensor(c_out[:], bank[src][:], Rope[:, 2 * kind].rearrange("p c d -> p (c d)"), ALU.mult)
                v.tensor_tensor(s_out.ap().rearrange("p (n two) -> p n two", two=2), swapped(bank[src][:]),
                                Rope[:, 2 * kind + 1].rearrange("p c (n two) -> p (c n) two", two=2), ALU.mult)\
                    .then_inc(s_done, 1)

            def b_gate(i):
                dve.wait_ge(s_bgp, i + 1)
                v.tensor_tensor(halves(gz[:]), halves(bank[4][:]), both_chunks(GB[:]), ALU.add).then_inc(s_gz, 1)

            def b_gate2(i):
                dve.wait_ge(s_gt, i + 1)
                v.scalar_tensor_tensor(gate[:], gt[:], 1.0, gz[:], ALU.add, ALU.mult).then_inc(s_gate, 1)

            def b_state(i):
                dve.wait_ge(s_Stp, i + 1)
                v.tensor_tensor(St.ap().rearrange("p g d -> p (g d)"), bank[7][:, 0:D],
                                StateMask.ap().rearrange("p g d -> p (g d)"), ALU.mult).then_inc(s_St, 1)

            def b_mask(i, n):
                dve.wait_ge(s_Sbp, NR * i + n + 1)
                if n >= RS:
                    dve.wait_ge(s_ret, NR * i + n - RS + 1)
                v.tensor_tensor(quarters(Sb[:, n % RS, :], 4), quarters(bank[4 + n % RS][:], 4), causal_four, ALU.mult).then_inc(s_Sb, 1)

            def b_norm(i):
                dve.wait_ge(s_rsq, i + 1)
                after(dve, s_rr0, i)
                v.tensor_reduce(rvar[:], heads(rsq[:], HB), AX.X, ALU.add).then_inc(s_rvar, 1)
                dve.wait_ge(s_rr, i + 1)
                after(dve, s_rgTp, i)
                v.tensor_tensor(heads(rnm[:], HB), heads(bank[7][:], HB), per_head(rr[:], HB, EB), ALU.mult).then_inc(s_rnm, 1)

            def b_residual(i):
                dve.wait_ge(s_Y2p, i + 1)
                dve.wait_ge(s_x1b, i + 1)
                v.tensor_tensor(yB.ap().rearrange("p c d -> p (c d)"), x1b.ap().rearrange("p c d -> p (c d)"), bank[5][:],
                                ALU.add).then_inc(s_yB, 1)
                after(dve, s_x2k, i)
                after(dve, s_x2Tp, i)
                layer_norm(i, yB, bnB, mvB, rsB, s_yB, s_bnB, s_mvB, s_rsB, NC, x2, s_x2)

            def step(a, b):
                if a is not None:
                    a_keys(a)
                    a_mask(a)
                if b is not None:
                    b_rope(b, 6, s_bkp, kc, ks, 1, s_kcs, s_kxTp, s_Stp)
                    b_rope(b, 5, s_bqp, qc, qs, 0, s_qcs, s_qxTp)
                    b_gate(b)
                if a is not None:
                    a_softmax(a)
                if b is not None:
                    b_state(b)
                    for n in range(3):
                        b_mask(b, n)
                if a is not None:
                    a_sum(a)
                if b is not None:
                    b_gate2(b)
                    for n in range(3, 6):
                        b_mask(b, n)
                if a is not None:
                    a_weights(a)
                if b is not None:
                    for n in range(6, 8):
                        b_mask(b, n)
                if a is not None:
                    a_norm(a)
                if b is not None:
                    b_norm(b)
                if a is not None:
                    a_residual(a)
                if b is not None:
                    b_residual(b)

            step(0, None)
            dve.wait_ge(s_w_b, 10 * 16)
            v.tensor_scalar(OW[:], OW[:], 0.5 * EB ** 0.5, None, ALU.mult).then_inc(s_ow, 1)
            rv_heads = RV.ap().rearrange("p k (h e) -> p (k h) e", e=EB)
            v.tensor_reduce(RVmean[:], rv_heads, AX.X, ALU.add).then_inc(s_rvm, 1)
            dve.wait_ge(s_rvm, 1)
            v.tensor_scalar(RVmean[:], RVmean[:], 1.0 / EB, None, ALU.mult).then_inc(s_rvm, 1)
            dve.wait_ge(s_rvm, 2)
            v.tensor_tensor(rv_heads, rv_heads, RVmean.ap().unsqueeze(2).to_broadcast([P, KK * HB, EB]), ALU.subtract)\
                .then_inc(s_rv, 1)
            step(1, 0)
            with dve.Fori(2, B) as i:
                step(i, i - 1)
            step(None, B - 1)

            def ffn(n):
                dve.wait_ge(s_x2b, n + 1)
                after(dve, s_xo, 4 * n)
                dve.wait_ge(s_hused, NF * (n + 1))
                for t in range(4):
                    v.tensor_tensor(yF[:, t, :], x2b[:, t, :], bank[4 + t // 2][:, (t % 2) * D:(t % 2 + 1) * D], ALU.add)\
                        .then_inc(s_yF, 1)
                after(dve, s_out, 16 * n)
                layer_norm(n, yF, bnF, mvF, rsF, s_yF, s_bnF, s_mvF, s_rsF, 4, xo, s_xo, counts=4)

            ffn(0)
            with dve.Fori(1, NT) as n:
                ffn(n)

        @block.gpsimd
        def _(pool):
            g = nc.gpsimd

            def rstd(dst, var, eps, n, s_mid, s_done, i):
                g.tensor_tensor(dst, var, eps[:].to_broadcast([P, n]), ALU.add).then_inc(s_mid, 1)
                pool.wait_ge(s_mid, i + 1)
                g.tensor_tensor(dst, dst, Half[:, 0:n], ALU.pow).then_inc(s_done, 1)

            with pool.Fori(0, B) as i:
                pool.wait_ge(s_ln, i + 1)
                pool.wait_ge(s_mz, i + 1)
                g.tensor_tensor(f_all[:, i, :], f_all[:, i, :], e_all[:, i, :], ALU.subtract).then_inc(s_f, 1)

            def a_inputs(i):
                pool.wait_ge(s_k, i + 1)
                after(pool, s_Sp, 2 * i)
                g.tensor_copy(kTs[:], kT_all[:, i, :]).then_inc(s_kTs, 1)
                pool.wait_ge(s_q, i + 1)
                g.tensor_copy(qTs[:], qT_all[:, i, :]).then_inc(s_qTs, 1)
                pool.wait_ge(s_ex, i + 1)
                g.tensor_tensor(ex[:], One[:].to_broadcast([P, PACK]), ex[:], ALU.subtract).then_inc(s_sg, 1)
                pool.wait_ge(s_ex01, i + 1)
                pool.wait_ge(s_sg, i + 1)
                after(pool, s_Hvp, i)
                g.tensor_tensor(kb01[:], ex01[:], ex[:, 0:D], ALU.mult).then_inc(s_kb01, 1)

            def a_decayed(i):
                pool.wait_ge(s_Z, i + 1)
                g.tensor_tensor(zz[:], Zs[:], Zs[:], ALU.mult).then_inc(s_zz, 1)

            def a_norm(i):
                pool.wait_ge(s_zz, i + 1)
                g.tensor_tensor(zz[:], zz[:], EpsA[:].to_broadcast([P, NC * HA]), ALU.mult).then_inc(s_zz2, 1)
                pool.wait_ge(s_ms, i + 1)
                pool.wait_ge(s_zz2, i + 1)
                g.tensor_tensor(zz[:], ms[:], zz[:], ALU.add).then_inc(s_rn0, 1)
                pool.wait_ge(s_rn0, i + 1)
                after(pool, s_on, i)
                g.tensor_tensor(rn[:], zz[:], Half[:, 0:NC * HA], ALU.pow).then_inc(s_rn, 1)

            def a_rstd(i):
                pool.wait_ge(s_mvA, NC * (i + 1))
                after(pool, s_x1, NC * i)
                rstd(rsA[:], mvA[:, :, 1], Eps, NC, s_va, s_rsA, i)

            def b_bias(i):
                pool.wait_ge(s_x1, NC * (i + 1))
                after(pool, s_x2, NC * i)
                g.tensor_tensor(x1b[:], x1[:], both_chunks(OB[:]), ALU.add).then_inc(s_x1b, 1)

            def b_rope(i):
                pool.wait_ge(s_kcs, i + 1)
                g.tensor_tensor(kx[:], kc[:], ks[:], ALU.add).then_inc(s_kx, 1)
                pool.wait_ge(s_qcs, i + 1)
                g.tensor_tensor(qx[:], qc[:], qs[:], ALU.add).then_inc(s_qx, 1)

            def b_norm(i):
                pool.wait_ge(s_rvar, i + 1)
                after(pool, s_rnm, i)
                rstd(rr[:], rvar[:], EpsB, NC * HB, s_rr0, s_rr, i)
                pool.wait_ge(s_rnm, i + 1)
                pool.wait_ge(s_gate, i + 1)
                g.tensor_tensor(rg[:], rnm[:], gate[:], ALU.mult).then_inc(s_rg, 1)

            def b_rstd(i):
                pool.wait_ge(s_mvB, NC * (i + 1))
                after(pool, s_x2, NC * i)
                rstd(rsB[:], mvB[:, :, 1], Eps, NC, s_vb2, s_rsB, i)
                pool.wait_ge(s_x2, NC * (i + 1))
                g.tensor_copy(x2_all[:, i, :], x2.ap().rearrange("p c d -> p (c d)")).then_inc(s_x2k, 1)

            def step(a, b):
                if a is not None:
                    a_inputs(a)
                if b is not None:
                    b_bias(b)
                    b_rope(b)
                if a is not None:
                    a_decayed(a)
                    a_norm(a)
                if b is not None:
                    b_norm(b)
                if a is not None:
                    a_rstd(a)
                if b is not None:
                    b_rstd(b)

            pool.wait_ge(s_half, 6)
            step(0, None)
            pool.wait_ge(s_w_b, 10 * 16)
            step(1, 0)
            with pool.Fori(2, B) as i:
                step(i, i - 1)
            step(None, B - 1)

            pool.wait_ge(s_w_f, 4 * 16)
            pool.wait_ge(s_x2k, B)
            def ffn(n):
                after(pool, s_yF, 4 * n)
                for r in range(2):
                    last = g.tensor_tensor(x2b[:, 2 * r:2 * r + 2, :], halves(x2_all[:, 2 * n + r, :]), both_chunks(B2[:]), ALU.add)
                last.then_inc(s_x2b, 1)
                pool.wait_ge(s_mvF, 4 * (n + 1))
                after(pool, s_xo, 4 * n)
                rstd(rsF[:], mvF[:, :, 1], Eps, 4, s_vf, s_rsF, n)

            ffn(0)
            with pool.Fori(1, NT) as n:
                ffn(n)


def shape_constants():
    s = np.arange(P)
    causal = (s[:, None] <= s[None, :]).astype(np.float32)
    mask = np.stack([causal, np.ones((P, P), np.float32)], axis=1)
    mid = P // 2 - 1
    src, tok = s[:, None], s[None, :]
    own = ((src > mid) & (src <= tok)).astype(np.float32) - ((src <= mid) & (src > tok)).astype(np.float32)
    later = (src > tok).astype(np.float32)
    nxt = (src <= mid).astype(np.float32) * np.ones((P, P), np.float32)
    decay_w = np.stack([own, later, nxt], axis=1) / np.float32(8.0)
    f32 = np.float32
    base = (np.arange(0, EB, 2, dtype=f32) + f32(0.4 * EB)) / f32(1.4 * EB)
    power = (np.arange(-(T // 2), T - T // 2, dtype=f32) / f32(512.0))[:, None]
    scale = np.power(base[None, :], power, dtype=f32)
    inv_freq = (f32(1.0) / np.power(f32(10000.0), np.arange(EB // 2, dtype=f32) / f32(EB // 2), dtype=f32)).astype(f32)
    ang = np.arange(T, dtype=f32)[:, None] * inv_freq[None, :]
    gam = f32(1.0) - np.exp(np.linspace(np.log(1 / 32.0), np.log(1 / 512.0), HB)).astype(f32)
    rel = np.arange(T) % P - P // 2
    tables = []
    for sc, sign in ((scale.astype(np.float64), 1.0), (1.0 / scale.astype(np.float64), -1.0)):
        dec = gam.astype(np.float64)[None, :] ** (sign * rel[:, None])
        for fn, signs in ((np.cos, (1.0, 1.0)), (np.sin, (-1.0, 1.0))):
            pair = fn(ang.astype(np.float64)) * sc
            pair = np.stack([pair * signs[0], pair * signs[1]], axis=-1).reshape(T, EB)
            full = (dec[:, :, None] * pair[:, None, :]).reshape(T, D)
            tables.append(full.reshape(NC, P, D).transpose(1, 0, 2))
    rope = np.stack(tables, axis=1).astype(f32)
    parity = np.stack([(s // EB) % 2 == 0, (s // EB) % 2 == 1], axis=1).astype(f32)
    head = s // EB
    state_mask = np.zeros((P, KK, P), f32)
    for g in range(KK):
        state_mask[:, g, :] = (head[:, None] == head[None, :]) * (gam.astype(np.float64)[g * 8 + head] ** P)[:, None]
    return dict(ident=np.eye(P, dtype=f32), mask=mask, decay_w=decay_w.astype(f32), rope=rope,
                parity=parity, state_mask=state_mask)


def kernel(x, ctx_1024, L0_attn_Wq, L0_attn_Wk, L0_attn_Wv, L0_attn_Wf, L0_attn_g_norm_w, L0_attn_Wo,
           L0_xattn_W_Q, L0_xattn_W_K, L0_xattn_W_V, L0_xattn_g_w, L0_xattn_g_b, L0_xattn_out_w, L0_xattn_out_b,
           L0_ffn_w1, L0_ffn_b1, L0_ffn_w2, L0_ffn_b2):
    import concourse.bacc as bacc
    from concourse.bass_utils import run_bass_kernel_spmd

    def tokens(a):
        return a.reshape(B, NC, P, D).transpose(0, 2, 1, 3)

    def features(a):
        return a.transpose(0, 2, 1).reshape(B, KK, P, T).transpose(0, 2, 1, 3)

    def weight(w):
        return w.reshape(w.shape[0] // P, P, w.shape[1]).transpose(1, 0, 2)

    def head_weight(w):
        return weight(w.transpose(1, 0, 2).reshape(D, D))

    def row(b):
        return np.broadcast_to(b[None, :], (P, D))

    arrays = dict(
        x_tok=tokens(x), x_feat=features(x), c_feat=features(ctx_1024),
        wq=weight(L0_attn_Wq), wk=weight(L0_attn_Wk), wv=weight(L0_attn_Wv), wf=weight(L0_attn_Wf),
        gcol=np.concatenate([L0_attn_g_norm_w] * 2)[:, None], wo=weight(L0_attn_Wo),
        rq=head_weight(L0_xattn_W_Q), rk=head_weight(L0_xattn_W_K), rv=head_weight(L0_xattn_W_V),
        gw=weight(L0_xattn_g_w.transpose(1, 0)), gb=row(L0_xattn_g_b),
        ow=weight(L0_xattn_out_w.transpose(1, 0)), ob=row(L0_xattn_out_b),
        w1=weight(L0_ffn_w1), b1=L0_ffn_b1.reshape(NF, P).transpose(1, 0), w2=weight(L0_ffn_w2), b2=row(L0_ffn_b2),
        **shape_constants())
    nc = bacc.Bacc("TRN2", target_bir_lowering=False, num_devices=1)
    ins, feed = {}, {}
    for name, a in arrays.items():
        a = np.ascontiguousarray(a)
        feed[f"in_{name}"] = a
        ins[name] = nc.dram_tensor(f"in_{name}", a.shape, mybir.dt.from_np(a.dtype), kind="ExternalInput").ap()
    out = nc.dram_tensor("out_rows", (NT, P, 4, D), F32, kind="ExternalOutput").ap()
    decoder_kernel(nc, out=out, **ins)
    r = run_bass_kernel_spmd(nc, [feed], core_ids=[0])
    got = r.results[0]["out_rows"]
    return got.transpose(0, 2, 1, 3).reshape(B, T, D)
```

```python
import numpy as np
import concourse.bass as bass
from concourse import mybir
from concourse.alu_op_type import AluOpType as ALU

F32, F32R = mybir.dt.float32, mybir.dt.float32r
ACT = mybir.ActivationFunctionType
AX = mybir.AxisListType

B, T, D = 8, 256, 256
P = 128
NC = T // P
KK = D // P
HA, MA = 4, 64
HB, EB = 16, 16
F = 1024
NF = F // P
TT = 512
NT = B * T // TT
EPS = 1e-5
BIG = 1e30
PACK = T * KK


def decoder_kernel(nc, x_tok, x_feat, c_feat, wq, wk, wv, wf, gcol, wo, rq, rk, rv, gw, gb, ow, ob,
                   w1, b1, w2, b2, ident, mask, decay_w, rope, parity, state_mask, out):
    place = {}

    def sb(name, shape):
        place[name] = (nc.sbuf_base + 31) // 32 * 32
        return nc.alloc_sbuf_tensor(name, shape, F32)

    def over(name, shape, dtype, at, start=0):
        return nc.alloc_sbuf_tensor_at(name, shape, dtype, offset=place[at] + 4 * start)

    def sem(name):
        return nc.alloc_semaphore(name)

    def halves(ap):
        return ap.rearrange("p (c d) -> p c d", c=NC)

    W2 = sb("W2", [P, NF, D])
    Wq, Wk, Wv, Wf = (W2[:, 2 * n:2 * n + 2, :] for n in range(4))
    def split_weight(name, at, start=0):
        return (nc.alloc_sbuf_tensor(name + "h", [P, KK, D], F32R), over(name + "l", [P, KK, D], F32R, at, start))

    Wo, Gcol = sb("Wo", [P, KK, D]), sb("Gcol", [P, 1])
    RQ, RK, RV, GW, OW = (sb(n, [P, KK, D]) for n in ("RQ", "RK", "RV", "GW", "OW"))
    Wq2, Wk2, Wv2 = (split_weight(w, "W2", n * PACK) for n, w in enumerate(("Wq", "Wk", "Wv")))
    Wo2, RQ2, RK2, RV2, GW2, OW2 = (split_weight(w, w) for w in ("Wo", "RQ", "RK", "RV", "GW", "OW"))
    GB, OB, B2 = sb("GB", [P, D]), sb("OB", [P, D]), sb("B2", [P, D])
    B1 = sb("B1", [P, NF])
    Ident = sb("Ident", [P, P])
    Mask = sb("Mask", [P, 2, P])
    DecayW = sb("DecayW", [P, 3, P])
    work_b = sb("work_b", [P, 4 * PACK + NC * KK * HB // KK * (P + EB)])
    Rope = work_b[:, 0:4 * PACK].rearrange("p (n c d) -> p n c d", n=4, c=NC)
    Parity = sb("Parity", [P, 2])
    StateMask = sb("StateMask", [P, KK, P])
    Half = sb("Half", [P, NC * HB])
    One, Eps, EpsA, EpsB = (sb(n, [P, 1]) for n in ("One", "Eps", "EpsA", "EpsB"))
    RVmean = sb("RVmean", [P, KK * HB])

    e_all, f_all = sb("e_all", [P, B, PACK]), sb("f_all", [P, B, PACK])
    x2_all, x2T_all = e_all, f_all

    def split_tile(name, at=None):
        lower = over(name + "l", [P, KK, T], F32R, at) if at else nc.alloc_sbuf_tensor(name + "l", [P, KK, T], F32R)
        return nc.alloc_sbuf_tensor(name + "h", [P, KK, T], F32R), lower

    xTp, thq, thk = sb("xTp", [P, KK, T]), sb("thq", [P, PACK]), sb("thk", [P, PACK])
    xTp2 = split_tile("xTp", "xTp")
    kTs, qTs, vs = sb("kTs", [P, PACK]), sb("qTs", [P, PACK]), sb("vs", [P, PACK])

    work_a = sb("work_a", [P, 12 * PACK])
    Sm = work_a[:, 0:3 * PACK].rearrange("p (n x) -> p n x", n=3)
    eq, ek, ex, kb, kbT, lg, pe_x, paT = (work_a[:, n * PACK:(n + 1) * PACK] for n in range(3, 11))
    kbT, paT = (x.rearrange("p (g c t) -> p g c t", g=KK, c=NC) for x in (kbT, paT))
    ex01, kb01 = (work_a[:, 11 * PACK + n * D:11 * PACK + (n + 1) * D] for n in range(2))
    pa = pe_x
    mx, Zs, ms, zz, rn = (sb(n, [P, NC * HA]) for n in ("mx", "Zs", "ms", "zz", "rn"))
    PT = Sm
    Hv = sb("Hv", [P, D])
    osq = lg
    on, onT = pa, split_tile("onT")
    xres, yA, x1 = sb("xres", [P, NC, D]), sb("yA", [P, NC, D]), sb("x1", [P, NC, D])
    bnA, mvA, rsA = sb("bnA", [P, NC, 6]), sb("mvA", [P, NC, 2]), sb("rsA", [P, NC])

    cT = sb("cT", [P, KK, T])
    cT2 = split_tile("cT", "cT")
    x1b, x1T = sb("x1b", [P, NC, D]), split_tile("x1T")
    work_c = sb("work_c", [P, 10 * PACK])
    qc, qs, kc, ks = (work_c[:, n * PACK:(n + 1) * PACK] for n in range(4))
    qx, kx, vb = qc, kc, sb("vb", [P, D])
    Vp = work_b[:, 4 * PACK:].rearrange("p (a w) -> p a w", a=NC * KK)
    gz, gt = sb("gz", [P, PACK]), sb("gt", [P, PACK])
    gate = gt
    qxT = sb("qxT", [P, KK, P])
    qxP = work_c[:, 4 * PACK:6 * PACK].rearrange("p (g c a t) -> p g c a t", g=KK, c=NC, a=2)
    kxT = work_c[:, 6 * PACK:7 * PACK].rearrange("p (g c t) -> p g c t", g=KK, c=NC)
    St = sb("St", [P, KK, P])
    NR = 8
    RS = 3
    Sb = work_c[:, 7 * PACK:10 * PACK].rearrange("p (n x) -> p n x", n=RS)
    rsq = gz
    rvar, rr = sb("rvar", [P, NC * HB]), sb("rr", [P, NC * HB])
    rnm, rgT = sb("rnm", [P, PACK]), split_tile("rgT")
    rg = rnm
    yB, x2 = x1b, sb("x2", [P, NC, D])
    xT = [halves(qc), halves(qs)]
    az = kc, ks

    bnB, mvB, rsB = sb("bnB", [P, NC, 6]), sb("mvB", [P, NC, 2]), sb("rsB", [P, NC])

    W1 = sb("W1", [P, KK, F])
    W1h, W2h = over("W1h", [P, KK, F], F32R, "work_a"), over("W2h", [P, NF, D], F32R, "work_a", 4 * PACK)
    W1l, W2l = over("W1l", [P, KK, F], F32R, "W1"), over("W2l", [P, NF, D], F32R, "W2")
    x2Th, x2Tl = over("x2Th", [P, B, PACK], F32R, "work_b"), over("x2Tl", [P, B, PACK], F32R, "f_all")
    HR = 4
    hid = over("hid", [P, HR, TT], F32, "work_a", 8 * PACK)
    hidh, hidl = (over(name, [P, HR, TT], F32R, "work_c", n * HR * TT) for n, name in enumerate(("hidh", "hidl")))
    x2b = over("x2b", [P, 4, D], F32, "work_c", 8 * PACK)
    yF, xo = (over(name, [P, 4, D], F32, "work_b", (B + 2 * n) * PACK) for n, name in enumerate(("yF", "xo")))
    bnF, mvF, rsF = sb("bnF", [P, 4, 6]), sb("mvF", [P, 4, 2]), sb("rsF", [P, 4])

    bank = [nc.alloc_psum_tensor(f"bank{n}", [P, 512], F32) for n in range(8)]

    s_w_loop0, s_w_qkv, s_w_a, s_w_b, s_w_f = sem("w_loop0"), sem("w_qkv"), sem("w_a"), sem("w_b"), sem("w_f")
    s_xT = [sem("xT_even"), sem("xT_odd")]
    s_xTp = sem("xTp_in")
    s_xres, s_cT, s_out = sem("xres_in"), sem("cT_in"), sem("out_stored")
    s_half, s_wo, s_rvm, s_rv = sem("half"), sem("wo_scaled"), sem("rv_mean"), sem("rv_centred")
    s_pwh, s_pwl = sem("weights_upper"), sem("weights_lower")
    s_xph, s_xpl, s_cTh, s_cTl = sem("xTp_upper"), sem("xTp_lower"), sem("cT_upper"), sem("cT_lower")
    s_onTh, s_x1Th, s_rgTh = sem("onT_upper"), sem("x1T_upper"), sem("rgT_upper")
    s_Vp0 = sem("value_windows_cleared")
    s_qp, s_kp, s_vp, s_zp = sem("q_psum"), sem("k_psum"), sem("v_psum"), sem("z_psum")
    s_thq, s_thk, s_v, s_az, s_e = sem("q_tanh"), sem("k_tanh"), sem("v_kept"), sem("z_abs"), sem("z_exp")
    s_q, s_k, s_mz, s_ln, s_f = sem("q_kept"), sem("k_kept"), sem("z_min"), sem("z_ln"), sem("f_kept")
    s_ex, s_sg = sem("gate_exp"), sem("slot_gain")
    s_Ep, s_E01p, s_eq, s_ek, s_ex01 = sem("E_psum"), sem("E01_psum"), sem("e_query"), sem("e_key"), sem("e_next")
    s_kb, s_kb01 = sem("key_gain"), sem("key_gain_next")
    s_Sp, s_Sm = sem("S_psum"), sem("S_masked")
    s_kbTp, s_kbT = sem("kbT_psum"), sem("kbT")
    s_Lp, s_lg, s_mx, s_lc, s_pe = sem("L_psum"), sem("logits"), sem("logit_max"), sem("logits_shifted"), sem("p_exp")
    s_Z, s_zz, s_pa, s_paTp, s_paT = sem("p_sum"), sem("p_sum_sq"), sem("p_decayed"), sem("paT_psum"), sem("paT")
    s_PTp, s_PT, s_Hvp, s_Hv = sem("PT_psum"), sem("PT_masked"), sem("Hv_psum"), sem("Hv")
    s_Op, s_osq, s_ms, s_rn0, s_rn, s_on = sem("O_psum"), sem("O_sq"), sem("O_ms"), sem("rn_var"), sem("rn"), sem("O_normed")
    s_onTp, s_onT, s_Yp, s_yA = sem("onT_psum"), sem("onT"), sem("Y_psum"), sem("yA")
    s_bnA, s_mvA, s_rsA, s_x1 = sem("bnA"), sem("mvA"), sem("rsA"), sem("x1")
    s_va, s_zz2 = sem("varA_eps"), sem("Z2_eps")
    s_x1b, s_x1Tp, s_x1T = sem("x1_plus_bias"), sem("x1T_psum"), sem("x1T")
    s_bqp, s_bkp, s_bvp, s_bgp = sem("bq_psum"), sem("bk_psum"), sem("bv_psum"), sem("bg_psum")
    s_qcs, s_kcs, s_qx, s_kx, s_vb = sem("q_rope_parts"), sem("k_rope_parts"), sem("q_roped"), sem("k_roped"), sem("bv")
    s_gz, s_gt, s_gate = sem("gate_z"), sem("gate_tanh"), sem("gate")
    s_qxTp, s_kxTp, s_qxT, s_qxP, s_kxT = sem("qxT_psum"), sem("kxT_psum"), sem("qxT"), sem("qxP"), sem("kxT")
    s_Stp, s_St = sem("state_psum"), sem("state")
    s_Sbp, s_Sb, s_ret = sem("ret_scores_psum"), sem("ret_scores"), sem("ret_group_summed")
    s_rsq, s_rvar, s_rr0, s_rr, s_rnm, s_rg = sem("ret_sq"), sem("ret_var"), sem("ret_var_eps"), sem("ret_rstd"), sem("ret_normed"), sem("ret_gated")
    s_rgTp, s_rgT, s_Y2p, s_yB = sem("rgT_psum"), sem("rgT"), sem("Y2_psum"), sem("yB")
    s_bnB, s_mvB, s_rsB, s_x2, s_x2k = sem("bnB"), sem("mvB"), sem("rsB"), sem("x2"), sem("x2_kept")
    s_vb2 = sem("varB_eps")
    s_x2Tp, s_x2T = sem("x2T_psum"), sem("x2T_kept")
    s_hp, s_h, s_hused = sem("h_psum"), sem("h_gelu"), sem("h_used")
    s_hh, s_hl = sem("h_upper"), sem("h_lower")
    s_wh, s_wl, s_xh, s_xl = sem("ffn_weight_upper"), sem("ffn_weight_lower"), sem("x2T_upper"), sem("x2T_lower")
    s_x2b, s_yFp, s_yF = sem("x2_plus_b2"), sem("yF_psum"), sem("yF")
    s_bnF, s_mvF, s_rsF, s_xo = sem("bnF"), sem("mvF"), sem("rsF"), sem("xo")
    s_vf = sem("varF_eps")

    def heads(ap, h):
        return ap.rearrange("p (g e) -> p g e", g=NC * h)

    def per_head(stat, h, e):
        return stat.unsqueeze(2).to_broadcast([P, NC * h, e])

    def after(eng, semaphore, count):
        if not isinstance(count, int) or count > 0:
            eng.wait_ge(semaphore, count)

    def rows(count):
        return min(count, B) if isinstance(count, int) else count

    def quarters(ap, n):
        return ap.rearrange("p (h t) -> p h t", h=n)

    mask_two = Mask.ap().rearrange("p a t -> p (a t)").unsqueeze(1).to_broadcast([P, 2, 2 * P])
    causal_two = Mask[:, 0, :].unsqueeze(1).to_broadcast([P, 2, P])
    causal_four = Mask[:, 0, :].unsqueeze(1).to_broadcast([P, 4, P])

    def wide(b, c, hh):
        o = c * D + hh * MA
        return bank[b][:, o:o + P]

    def used(b):
        return bank[b].ap().rearrange("p (q m) -> p q m", q=4)[:, :, 0:MA]

    def packed(ap):
        return ap.rearrange("p (q m) -> p q m", q=4)

    def both_chunks(row_bias):
        return row_bias.unsqueeze(1).to_broadcast([P, NC, D])

    def swapped(ap):
        return ap.rearrange("p (n two) -> p n two", two=2)[:, :, ::-1]

    block = nc.Block()
    with block:
        @block.sync
        def _(sp):
            sp.dma_start(Wf, wf).then_inc(s_w_loop0, 16)

            def load_xT(j, r):
                if not isinstance(j, int):
                    sp.wait_ge(s_zp, 2 * j + r - 1)
                sp.dma_start(xT[r][:], x_feat[2 * j + r]).then_inc(s_xT[r], 16)

            load_xT(0, 0)
            load_xT(0, 1)
            sp.dma_start(xTp[:], x_feat[0]).then_inc(s_xTp, 16)
            for w, src in ((Wv, wv), (Wq, wq), (Wk, wk)):
                sp.dma_start(w, src).then_inc(s_w_qkv, 16)
            with sp.Fori(1, B // 2) as j:
                load_xT(j, 0)
                load_xT(j, 1)
            for w, src in ((DecayW, decay_w), (Mask, mask), (Ident, ident), (Wo, wo), (Gcol, gcol)):
                sp.dma_start(w[:], src).then_inc(s_w_a, 16)
            sp.dma_start(xres[:], x_tok[0]).then_inc(s_xres, 16)
            sp.dma_start(cT[:], c_feat[0]).then_inc(s_cT, 16)
            sp.wait_ge(s_kp, 1)
            sp.dma_start(xTp[:], x_feat[1]).then_inc(s_xTp, 16)
            for w, src in ((RV, rv), (OW, ow), (RQ, rq), (RK, rk), (GW, gw), (GB, gb), (OB, ob),
                           (Rope, rope), (Parity, parity), (StateMask, state_mask)):
                sp.dma_start(w[:], src).then_inc(s_w_b, 16)
            for w, src in ((W1, w1), (B1, b1), (B2, b2)):
                sp.dma_start(w[:], src).then_inc(s_w_f, 16)

            def load_rows(i):
                sp.wait_ge(s_kp, i)
                sp.dma_start(xTp[:], x_feat[i]).then_inc(s_xTp, 16)
                sp.wait_ge(s_yA, i - 1)
                sp.dma_start(xres[:], x_tok[i - 1]).then_inc(s_xres, 16)
                sp.wait_ge(s_bvp, i - 1)
                sp.dma_start(cT[:], c_feat[i - 1]).then_inc(s_cT, 16)

            with sp.Fori(2, B) as i:
                load_rows(i)
            sp.wait_ge(s_yA, B - 1)
            sp.dma_start(xres[:], x_tok[B - 1]).then_inc(s_xres, 16)
            sp.wait_ge(s_bvp, B - 1)
            sp.dma_start(cT[:], c_feat[B - 1]).then_inc(s_cT, 16)
            sp.wait_ge(s_kp, B)
            sp.dma_start(W2[:], w2).then_inc(s_w_f, 16)
            with sp.Fori(0, NT) as n:
                sp.wait_ge(s_xo, 4 * n + 4)
                sp.dma_start(out[n], xo[:]).then_inc(s_out, 16)
            sp.wait_ge(s_out, 16 * NT)

        @block.tensor
        def _(pe):
            mm, tr = nc.tensor.matmul, nc.tensor.transpose

            def forget0(j, r):
                n = 2 * j + r
                pe.wait_ge(s_xT[r], 16 * (j + 1))
                if not isinstance(j, int):
                    pe.wait_ge(s_mz, n - 1)
                    pe.wait_ge(s_az, n - 1)
                for c in range(NC):
                    for kk in range(KK):
                        last = mm(bank[4 * r + 3][:, c * D:(c + 1) * D], xT[r][:, kk, c * P:(c + 1) * P], Wf[:, kk, :],
                                  start=kk == 0, stop=kk == KK - 1)
                last.then_inc(s_zp, 1)

            pe.wait_ge(s_w_loop0, 16)
            forget0(0, 0)
            forget0(0, 1)
            with pe.Fori(1, B // 2) as j:
                forget0(j, 0)
                forget0(j, 1)

            def three_passes(a, b):
                return [(u, w, kk) for kk in range(KK) for u, w in ((a[0], b[0]), (a[0], b[1]), (a[1], b[0]))]

            def p_v(i):
                pe.wait_ge(s_xpl, i + 1)
                after(pe, s_Sb, NR * (i - 2) + 6)
                project(bank[6], xTp2, Wv2, s_vp)

            def p_qk(i, b, w, done, n):
                after(pe, s_Sb, NR * (i - 2) + n)
                for g in range(KK):
                    for m, (w_part, x_part, kk) in enumerate(three_passes(w, xTp2)):
                        last = mm(bank[b][:, g * T:(g + 1) * T], w_part[:, kk, g * P:(g + 1) * P], x_part[:, kk, :],
                                  start=m == 0, stop=m == 3 * KK - 1)
                last.then_inc(done, 1)

            def a_decay(i):
                pe.wait_ge(s_f, i + 1)
                after(pe, s_on, 2 * i)
                mm(bank[0][:, 0:D], DecayW[:, 0, :], f_all[:, i, 0:D], start=True, stop=True)
                mm(bank[0][:, D:2 * D], DecayW[:, 0, :], f_all[:, i, D:2 * D], start=True, stop=True).then_inc(s_Ep, 1)
                mm(bank[1][:, 0:D], DecayW[:, 1, :], f_all[:, i, 0:D], start=True, stop=False)
                mm(bank[1][:, 0:D], DecayW[:, 2, :], f_all[:, i, D:2 * D], start=False, stop=True).then_inc(s_E01p, 1)

            def a_scores(i):
                pe.wait_ge(s_k, i + 1)
                pe.wait_ge(s_q, i + 1)
                after(pe, s_onT, i)
                after(pe, s_yA, i)
                for g in range(KK):
                    for hh in range(2):
                        r = slice(64 * hh, 64 * hh + 64)
                        last = mm(bank[2 + hh][:, g * T:(g + 1) * T], kTs[r, g * T:g * T + P], qTs[r, g * T:(g + 1) * T],
                                  start=True, stop=True)
                last.then_inc(s_Sp, 1)
                pe.wait_ge(s_ek, i + 1)
                pe.wait_ge(s_ex01, i + 1)
                for g in range(KK):
                    for hh in range(2):
                        r = slice(64 * hh, 64 * hh + 64)
                        last = mm(bank[hh][:, g * P:(g + 1) * P], kTs[r, g * T + P:(g + 1) * T],
                                  qTs[r, g * T + P:(g + 1) * T], start=True, stop=True)
                last.then_inc(s_Sp, 1)

            def transposes(dst, src, ready, count, done, chunk_major=True):
                pe.wait_ge(ready, count)
                for g in range(KK):
                    for c in range(NC):
                        o = (g * NC + c) * P
                        i = c * D + g * P if chunk_major else o
                        last = tr(dst[:, o:o + P], src[:, i:i + P], Ident[:])
                last.then_inc(done, 1)

            def a_kbT(i):
                pe.wait_ge(s_Sm, 4 * i + 4)
                transposes(bank[0], kb, s_kb, i + 1, s_kbTp)

            def a_logits(i):
                pe.wait_ge(s_kb, i + 1)
                pe.wait_ge(s_kb01, i + 1)
                for g in range(KK):
                    for hh in range(2):
                        m, m1 = slice(g * P, (g + 1) * P), slice(D + g * P, D + (g + 1) * P)
                        mm(wide(2 + g, 0, hh), Sm[:, hh, g * T:g * T + P], kb[:, m], start=True, stop=True, skip_group_check=True)
                        mm(wide(2 + g, 1, hh), Sm[:, hh, g * T + P:(g + 1) * T], kb01[:, m], start=True, stop=False, skip_group_check=True)
                        last = mm(wide(2 + g, 1, hh), Sm[:, 2, (2 * hh + g) * P:(2 * hh + g + 1) * P], kb[:, m1],
                                  start=False, stop=True, skip_group_check=True)
                last.then_inc(s_Lp, 1)

            def a_paT(i):
                after(pe, s_kxT, i)
                transposes(bank[1], pa, s_pa, i + 1, s_paTp, chunk_major=False)

            def a_weights(i):
                pe.wait_ge(s_kbT, i + 1)
                pe.wait_ge(s_paT, i + 1)
                for g in range(KK):
                    for c in range(NC):
                        for hh in range(2):
                            r, o = slice(64 * hh, 64 * hh + 64), (2 * g + c) * P
                            last = mm(bank[2 + hh][:, o:o + P], kbT[r, g, c, :], paT[r, g, c, :], start=True, stop=True)
                last.then_inc(s_PTp, 1)

            def a_state(i):
                pe.wait_ge(s_kbT, i + 1)
                pe.wait_ge(s_v, i + 1)
                for g in range(KK):
                    last = mm(bank[0][:, g * P:(g + 1) * P], kb01[:, g * P:(g + 1) * P], vs[:, g * P:(g + 1) * P],
                              start=True, stop=True)
                last.then_inc(s_Hvp, 1)

            def a_out(i):
                after(pe, s_x2T, i - 1)
                pe.wait_ge(s_PT, 2 * i + 2)
                pe.wait_ge(s_Hv, i + 1)
                for g in range(KK):
                    for hh in range(2):
                        m, m1 = slice(g * P, (g + 1) * P), slice(D + g * P, D + (g + 1) * P)
                        mm(wide(g, 0, hh), PT[:, hh, 2 * g * P:(2 * g + 1) * P], vs[:, m], start=True, stop=True, skip_group_check=True)
                        mm(wide(g, 1, hh), PT[:, hh, (2 * g + 1) * P:(2 * g + 2) * P], vs[:, m1],
                           start=True, stop=False, skip_group_check=True)
                        last = mm(wide(g, 1, hh), paT[:, g, 1, :], Hv[:, m], start=False, stop=True, skip_group_check=True)
                last.then_inc(s_Op, 1)

            def project(dst, srcT, w, done):
                for c in range(NC):
                    for m, (x_part, w_part, kk) in enumerate(three_passes(srcT, w)):
                        last = mm(dst[:, c * D:(c + 1) * D], x_part[:, kk, c * P:(c + 1) * P], w_part[:, kk, :],
                                  start=m == 0, stop=m == 3 * KK - 1)
                last.then_inc(done, 1)

            def a_onT(i):
                transposes(bank[2], on, s_on, 2 * i + 2, s_onTp, chunk_major=False)

            def a_project(i):
                pe.wait_ge(s_onT, i + 1)
                pe.wait_ge(s_pwl, 4)
                project(bank[3], onT, Wo2, s_Yp)

            def b_k(i):
                pe.wait_ge(s_cTl, i + 1)
                pe.wait_ge(s_v, rows(i + 2))
                project(bank[6], cT2, RK2, s_bkp)

            def b_x1T(i):
                pe.wait_ge(s_k, rows(i + 2))
                transposes(bank[5], x1.ap().rearrange("p c d -> p (c d)"), s_x1, NC * (i + 1), s_x1Tp)

            def b_qg(i):
                pe.wait_ge(s_x1T, i + 1)
                project(bank[5], x1T, RQ2, s_bqp)
                pe.wait_ge(s_kcs, i + 1)
                project(bank[6], x1T, GW2, s_bgp)

            def b_v(i):
                after(pe, s_rnm, i)
                project(bank[7], cT2, RV2, s_bvp)

            def b_kxT(i):
                transposes(bank[1], kx, s_kx, i + 1, s_kxTp)

            def b_qxT(i):
                transposes(bank[5], qx, s_qx, i + 1, s_qxTp)

            def b_state(i):
                pe.wait_ge(s_vb, i + 1)
                for g in range(KK):
                    last = mm(bank[7][:, g * P:(g + 1) * P], kx[:, g * P:(g + 1) * P], vb[:, g * P:(g + 1) * P],
                              start=True, stop=True)
                last.then_inc(s_Stp, 1)

            def b_scores(i, n):
                c, j = n // 4, n % 4
                r = slice(32 * j, 32 * j + 32)
                if n == 0:
                    pe.wait_ge(s_kxT, i + 1)
                    pe.wait_ge(s_qxP, i + 1)
                    after(pe, s_yB, i)
                    pe.wait_ge(s_gz, i + 1)
                if n >= RS:
                    pe.wait_ge(s_Sb, NR * i + n - RS + 1)
                for g in range(KK):
                    last = mm(bank[4 + n % RS][:, g * T:(g + 1) * T], kxT[r, g, c, :], qxP[r, g, c, :, :], start=True, stop=True)
                last.then_inc(s_Sbp, 1)

            def b_sum(i, n):
                c, j = n // 4, n % 4
                pe.wait_ge(s_Sb, NR * i + n + 1)
                if n == 0:
                    pe.wait_ge(s_St, i + 1)
                    for g in range(KK):
                        mm(bank[7][:, D + g * P:D + (g + 1) * P], qxT[:, g, :], St[:, g, :], start=g == 0, stop=False,
                           skip_group_check=True)
                for g in range(KK):
                    for par in range(2):
                        h = 2 * j + par
                        last = mm(bank[7][:, c * D + g * P:c * D + (g + 1) * P],
                                  Sb[:, n % RS, (2 * g + par) * P:(2 * g + par + 1) * P],
                                  Vp[:, c * KK + g, h * P:(h + 1) * P], start=False, stop=True, skip_group_check=True)
                last.then_inc(s_ret, 1)

            def b_rgT(i, b=4):
                pe.wait_ge(s_q, rows(i + 3))
                transposes(bank[b], rg, s_rg, i + 1, s_rgTp)

            def b_project(i, b=4):
                pe.wait_ge(s_rgT, i + 1)
                project(bank[b], rgT, OW2, s_Y2p)

            def b_x2T(i, b=0):
                pe.wait_ge(s_Hv, rows(i + 3))
                transposes(bank[b], x2.ap().rearrange("p c d -> p (c d)"), s_x2, NC * (i + 1), s_x2Tp)

            def step(p, a, b, c):
                if a is not None:
                    a_decay(a)
                    a_scores(a)
                if b is not None:
                    b_x1T(b)
                    b_k(b)
                if a is not None:
                    a_kbT(a)
                    a_logits(a)
                if c is not None:
                    b_rgT(c)
                if b is not None:
                    b_kxT(b)
                    b_qg(b)
                    b_v(b)
                if c is not None:
                    b_project(c)
                if b is not None:
                    b_qxT(b)
                if a is not None:
                    a_state(a)
                if b is not None:
                    b_state(b)
                if a is not None:
                    a_paT(a)
                if b is not None:
                    for n in range(RS):
                        b_scores(b, n)
                    b_sum(b, 0)
                    b_scores(b, 3)
                if c is not None:
                    b_x2T(c)
                if a is not None:
                    a_weights(a)
                if b is not None:
                    b_sum(b, 1)
                    b_scores(b, 4)
                    b_sum(b, 2)
                if a is not None:
                    a_out(a)
                if b is not None:
                    b_scores(b, 5)
                    b_sum(b, 3)
                    b_scores(b, 6)
                    b_sum(b, 4)
                    b_scores(b, 7)
                    b_sum(b, 5)
                if p is not None:
                    p_v(p)
                if a is not None:
                    a_onT(a)
                if b is not None:
                    b_sum(b, 6)
                if p is not None:
                    p_qk(p, 4, Wq2, s_qp, 7)
                if a is not None:
                    a_project(a)
                if b is not None:
                    b_sum(b, 7)
                if p is not None:
                    p_qk(p, 5, Wk2, s_kp, 8)

            pe.wait_ge(s_az, B)
            pe.wait_ge(s_mz, B)
            pe.wait_ge(s_pwl, 3)
            step(0, None, None, None)
            pe.wait_ge(s_w_a, 5 * 16)
            step(1, 0, None, None)
            pe.wait_ge(s_pwl, 9)
            step(2, 1, 0, None)
            with pe.Fori(3, B) as i:
                step(i, i - 1, i - 2, i - 3)
            step(None, B - 1, B - 2, B - 3)
            step(None, None, B - 1, B - 2)

            xh, xl = (x.rearrange("p (n r) x -> p n r x", r=2) for x in (x2Th, x2Tl))

            def ffn_up(n, f):
                passes = [(w, x, kk) for kk in range(KK) for w, x in ((W1h, xh), (W1h, xl), (W1l, xh))]
                for m, (w, x, kk) in enumerate(passes):
                    last = mm(bank[f % HR].ap().rearrange("p (r t) -> p r t", r=2), w[:, kk, f * P:(f + 1) * P],
                              x[:, n, :, kk * T:(kk + 1) * T],
                              start=m == 0, stop=m == len(passes) - 1)
                last.then_inc(s_hp, 1)

            def ffn_down(n, f):
                pe.wait_ge(s_hl, NF * n + f + 1)
                if f == 0:
                    after(pe, s_yF, 4 * n)
                for t in range(4):
                    for m, (h, w) in enumerate(((hidh, W2h), (hidh, W2l), (hidl, W2h))):
                        last = mm(bank[4 + t // 2][:, (t % 2) * D:(t % 2 + 1) * D], h[:, f % HR, t * P:(t + 1) * P], w[:, f, :],
                                  start=f == 0 and t % 2 == 0 and m == 0, stop=f == NF - 1 and m == 2, skip_group_check=True)
                last.then_inc(s_hused, 1)

            def ffn(n, last_row=None):
                pe.wait_ge(s_xl, 2 * n + 2)
                for f in range(3):
                    ffn_up(n, f)
                for f in range(NF):
                    if f + 3 < NF:
                        if f + 3 >= 4:
                            pe.wait_ge(s_h, NF * n + f)
                        ffn_up(n, f + 3)
                    ffn_down(n, f)
                    if last_row is not None and f == 2:
                        b_rgT(last_row, 6)
                    if last_row is not None and f == 4:
                        b_project(last_row, 6)
                    if last_row is not None and f == 7:
                        b_x2T(last_row, 7)

            pe.wait_ge(s_wl, 2)
            pe.wait_ge(s_x2T, B - 1)
            ffn(0, last_row=B - 1)
            with pe.Fori(1, NT) as n:
                ffn(n)

        @block.scalar
        def _(act):
            activation = nc.scalar.activation

            def split_upper(dst, src, done):
                activation(dst, src, ACT.Copy).then_inc(done, 1)

            def evacuate0(j, r):
                n = 2 * j + r
                act.wait_ge(s_zp, n + 1)
                if not isinstance(j, int):
                    act.wait_ge(s_e, n - 1)
                activation(az[r], bank[4 * r + 3][:], ACT.Abs).then_inc(s_az, 1)
                act.wait_ge(s_az, n + 1)
                activation(e_all[:, n, :], az[r], ACT.Exp, scale=-1.0).then_inc(s_e, 1)

            evacuate0(0, 0)
            evacuate0(0, 1)
            with act.Fori(1, B // 2) as j:
                evacuate0(j, 0)
                evacuate0(j, 1)
            act.wait_ge(s_w_qkv, 3 * 16)
            for w2, w in ((Wv2, Wv), (Wq2, Wq), (Wk2, Wk)):
                split_upper(w2[0][:], w, s_pwh)
            act.wait_ge(s_xTp, 16)
            split_upper(xTp2[0][:], xTp[:], s_xph)
            act.wait_ge(s_e, B)
            for r in (slice(0, 2), slice(2, B)):
                activation(e_all[:, r, :], e_all[:, r, :], ACT.Ln, bias=1.0).then_inc(s_ln, r.stop - r.start)

            def split_c(i):
                act.wait_ge(s_cT, 16 * (i + 1))
                split_upper(cT2[0][:], cT[:], s_cTh)

            def p_split(i):
                if isinstance(i, int) and i == 0:
                    return
                act.wait_ge(s_xTp, 16 * (i + 1))
                split_upper(xTp2[0][:], xTp[:], s_xph)

            def p_v(i):
                act.wait_ge(s_vp, i + 1)
                after(act, s_Op, i)
                activation(vs[:], bank[6][:], ACT.Copy).then_inc(s_v, 1)

            def p_tanh(i, b, ready, th, done, used_by):
                act.wait_ge(ready, i + 1)
                after(act, used_by, i)
                activation(th[:], bank[b][:], ACT.Tanh, scale=0.5).then_inc(done, 1)

            def a_gains(i):
                act.wait_ge(s_f, i + 1)
                after(act, s_kb, i)
                after(act, s_kb01, i)
                activation(ex[:], f_all[:, i, :], ACT.Exp, scale=0.125).then_inc(s_ex, 1)
                act.wait_ge(s_Ep, i + 1)
                after(act, s_pa, i)
                activation(eq.rearrange("p (g c x) -> p c g x", g=KK, c=NC),
                           bank[0].ap().rearrange("p (c g x) -> p c g x", g=KK, c=NC), ACT.Exp).then_inc(s_eq, 1)
                activation(ek[:], bank[0][:], ACT.Exp, scale=-1.0).then_inc(s_ek, 1)
                act.wait_ge(s_E01p, i + 1)
                activation(ex01[:], bank[1][:, 0:D], ACT.Exp).then_inc(s_ex01, 1)

            def a_kbT(i):
                act.wait_ge(s_kbTp, i + 1)
                after(act, s_PTp, i)
                activation(kbT.rearrange("p g c t -> p (g c t)"), bank[0][:], ACT.Copy).then_inc(s_kbT, 1)

            def a_exp(i):
                act.wait_ge(s_lc, i + 1)
                after(act, s_onTp, i)
                activation(pe_x[:], lg[:], ACT.Exp, scale=1.0 / 32.0).then_inc(s_pe, 1)

            def a_state(i):
                act.wait_ge(s_Hvp, i + 1)
                after(act, s_Op, i)
                for hh in range(2):
                    r = slice(64 * hh, 64 * hh + 64)
                    last = activation(Hv[r, :].rearrange("p (g m) -> p g m", g=KK)[:, :, 64 * hh:64 * hh + 64],
                                      bank[0][r, 0:D].rearrange("p (g m) -> p g m", g=KK)[:, :, 64 * hh:64 * hh + 64], ACT.Copy)
                last.then_inc(s_Hv, 1)

            def a_paT(i):
                act.wait_ge(s_paTp, i + 1)
                activation(paT.rearrange("p g c t -> p (g c t)"), bank[1][:], ACT.Copy).then_inc(s_paT, 1)

            def a_square(i):
                act.wait_ge(s_Op, i + 1)
                after(act, s_ms, i)
                for g in range(KK):
                    activation(packed(osq[:, g * D:(g + 1) * D]), used(g), ACT.Square).then_inc(s_osq, 1)

            def a_onT(i):
                act.wait_ge(s_onTp, i + 1)
                after(act, s_Yp, i)
                split_upper(onT[0].ap().rearrange("p k t -> p (k t)"), bank[2][:], s_onTh)

            def b_x1T(i):
                act.wait_ge(s_x1Tp, i + 1)
                after(act, s_bgp, i)
                split_upper(x1T[0].ap().rearrange("p k t -> p (k t)"), bank[5][:], s_x1Th)

            def b_v(i):
                act.wait_ge(s_bvp, i + 1)
                after(act, s_ret, NR * i)
                activation(vb[:], bank[7][:, 0:D], ACT.Copy)
                activation(Vp.rearrange("p a (h w) -> p a h w", w=P + EB)[:, :, :, 0:EB],
                           bank[7].ap().rearrange("p (a h e) -> p a h e", a=NC * KK, e=EB), ACT.Copy).then_inc(s_vb, 1)

            def b_gate(i):
                act.wait_ge(s_gz, i + 1)
                after(act, s_rg, i)
                activation(gt[:], gz[:], ACT.Tanh, scale=0.5).then_inc(s_gt, 1)

            def b_kxT(i):
                act.wait_ge(s_kxTp, i + 1)
                activation(kxT.rearrange("p g c t -> p (g c t)"), bank[1][:], ACT.Copy).then_inc(s_kxT, 1)

            def b_qxT(i):
                act.wait_ge(s_qxTp, i + 1)
                qp = bank[5].ap().rearrange("p (g c t) -> p (g c) t", g=KK, c=NC)
                for par in range(2):
                    activation(qxP[:, :, :, par, :].rearrange("p g c t -> p (g c) t"), qp, ACT.Copy,
                               scale=Parity[:, par:par + 1])
                activation(qxT[:], bank[5].ap().rearrange("p (g c t) -> p g c t", g=KK, c=NC)[:, :, 1, :],
                           ACT.Copy).then_inc(s_qxP, 1)

            def b_square(i):
                act.wait_ge(s_ret, NR * (i + 1))
                act.wait_ge(s_gate, i + 1)
                activation(rsq[:], bank[7][:], ACT.Square).then_inc(s_rsq, 1)

            def b_rgT(i, b=4):
                act.wait_ge(s_rgTp, i + 1)
                after(act, s_Y2p, i)
                split_upper(rgT[0].ap().rearrange("p k t -> p (k t)"), bank[b][:], s_rgTh)

            def b_x2T(i, b=0):
                act.wait_ge(s_x2Tp, i + 1)
                activation(x2T_all[:, i, :], bank[b][:], ACT.Copy).then_inc(s_x2T, 1)

            def split_weights():
                act.wait_ge(s_wo, 1)
                act.wait_ge(s_w_b, 10 * 16)
                act.wait_ge(s_rv, 1)
                for w2, w in ((Wo2, Wo), (RK2, RK), (RQ2, RQ), (GW2, GW), (RV2, RV), (OW2, OW)):
                    split_upper(w2[0][:], w[:], s_pwh)

            def split_ffn_weights():
                act.wait_ge(s_w_f, 4 * 16)
                act.wait_ge(s_Yp, B)
                split_upper(W1h[:], W1[:], s_wh)
                split_upper(W2h[:], W2[:], s_wh)

            def step(p, a, b, c, setup=False, ffn_weights=False):
                if a is not None:
                    a_gains(a)
                if b is not None:
                    b_x1T(b)
                if a is not None:
                    a_kbT(a)
                if b is not None:
                    b_kxT(b)
                if c is not None:
                    b_rgT(c)
                if a is not None:
                    a_exp(a)
                if b is not None:
                    b_v(b)
                    b_gate(b)
                    b_qxT(b)
                if a is not None:
                    a_state(a)
                    a_paT(a)
                if setup:
                    split_weights()
                if ffn_weights:
                    split_ffn_weights()
                if c is not None:
                    b_x2T(c)
                if p is not None:
                    p_split(p)
                if a is not None:
                    split_c(a)
                    a_square(a)
                if p is not None:
                    p_v(p)
                if a is not None:
                    a_onT(a)
                if p is not None:
                    p_tanh(p, 4, s_qp, thq, s_thq, s_q)
                if b is not None:
                    b_square(b)
                if p is not None:
                    p_tanh(p, 5, s_kp, thk, s_thk, s_k)

            act.wait_ge(s_half, 1)
            act.wait_ge(s_Vp0, 1)
            step(0, None, None, None)
            step(1, 0, None, None, setup=True)
            step(2, 1, 0, None)
            with act.Fori(3, B) as i:
                step(i, i - 1, i - 2, i - 3)
            step(None, B - 1, B - 2, B - 3)
            step(None, None, B - 1, B - 2, ffn_weights=True)

            def split_x2(n):
                for r in range(2):
                    act.wait_ge(s_x2T, 2 * n + r + 1)
                    split_upper(x2Th[:, 2 * n + r, :], x2T_all[:, 2 * n + r, :], s_xh)

            def ffn(n, last_row=None):
                for f in range(NF):
                    if last_row is not None and f == 6:
                        b_rgT(last_row, 6)
                    if f == 5 and not (isinstance(n, int) and n == NT - 1):
                        split_x2(n + 1)
                    act.wait_ge(s_hp, NF * n + f + 1)
                    after(act, s_hl, NF * n + f + 1 - HR)
                    activation(hid[:, f % HR, :], bank[f % HR][:], ACT.Gelu, bias=B1[:, f:f + 1]).then_inc(s_h, 1)
                    act.wait_ge(s_h, NF * n + f + 1)
                    after(act, s_hused, NF * n + f + 1 - HR)
                    activation(hidh[:, f % HR, :], hid[:, f % HR, :], ACT.Copy).then_inc(s_hh, 1)

                if last_row is not None:
                    b_x2T(last_row, 7)

            act.wait_ge(s_ret, NR * B)
            act.wait_ge(s_qcs, B)
            split_x2(0)
            ffn(0, last_row=B - 1)
            with act.Fori(1, NT - 1) as n:
                ffn(n)
            ffn(NT - 1)

        @block.vector
        def _(dve):
            v = nc.vector

            def split_lower(dst, src, upper, ready, count, done):
                dve.wait_ge(ready, count)
                v.tensor_tensor(dst, src, upper.bitcast(F32), ALU.subtract).then_inc(done, 1)

            def split_bank(parts, b, ready, i, done):
                split_lower(parts[1].ap().rearrange("p k t -> p (k t)"), bank[b][:],
                            parts[0].ap().rearrange("p k t -> p (k t)"), ready, i + 1, done)

            def evacuate0(j, r):
                n = 2 * j + r
                dve.wait_ge(s_az, n + 1)
                v.tensor_scalar(f_all[:, n, :], bank[4 * r + 3][:], 0.0, None, ALU.min).then_inc(s_mz, 1)

            def p_swish(i, b, th, ready, dst, done):
                dve.wait_ge(ready, i + 1)
                after(dve, s_Sp, 2 * i)
                v.scalar_tensor_tensor(dst[:], th[:], 1.0, bank[b][:], ALU.add, ALU.mult).then_inc(done, 1)

            for tile, value in ((Hv, 0.0), (Half, -0.5), (One, 1.0), (Eps, EPS), (EpsA, MA * EPS), (EpsB, EB * EPS)):
                dve.memset(tile[:], value).then_inc(s_half, 1)
            evacuate0(0, 0)
            evacuate0(0, 1)
            with dve.Fori(1, B // 2) as j:
                evacuate0(j, 0)
                evacuate0(j, 1)
            for n, (w2, w) in enumerate(((Wv2, Wv), (Wq2, Wq), (Wk2, Wk))):
                split_lower(w2[1][:], w, w2[0][:], s_pwh, n + 1, s_pwl)
            dve.wait_ge(s_mz, B)
            with dve.Fori(0, B) as i:
                dve.wait_ge(s_ln, i + 1)
                v.tensor_tensor(f_all[:, i, :], f_all[:, i, :], e_all[:, i, :], ALU.subtract).then_inc(s_f, 1)

            def layer_norm_stats(i, y, bn, mv, s_y, s_bn, s_mv, tiles, counts=1):
                dve.wait_ge(s_y, counts * (i + 1))
                for c in range(tiles):
                    v.bn_stats(bn[:, c, :], y[:, c, :]).then_inc(s_bn, 1)
                for c in range(tiles):
                    dve.wait_ge(s_bn, tiles * i + c + 1)
                    dve.nop(nofuse=True)
                    v.bn_aggr(mv[:, c, :], bn[:, c, :]).then_inc(s_mv, 1)

            def layer_norm_apply(i, y, mv, rs, s_rs, tiles, dst, s_dst):
                dve.wait_ge(s_rs, i + 1)
                for c in range(tiles):
                    v.tensor_scalar(dst[:, c, :], y[:, c, :], mv[:, c, 0:1], rs[:, c:c + 1], ALU.subtract, ALU.mult)\
                        .then_inc(s_dst, 1)

            def a_keys(i):
                dve.wait_ge(s_ex, i + 1)
                v.tensor_scalar(ex[:], ex[:], -1.0, 1.0, ALU.mult, ALU.add).then_inc(s_sg, 1)
                dve.wait_ge(s_ek, i + 1)
                dve.wait_ge(s_sg, i + 1)
                after(dve, s_Lp, i)
                v.scalar_tensor_tensor(kb[:], ek[:], BIG, ex[:], ALU.min, ALU.mult).then_inc(s_kb, 1)
                dve.wait_ge(s_ex01, i + 1)
                after(dve, s_Hvp, i)
                v.tensor_tensor(kb01[:], ex01[:], ex[:, 0:D], ALU.mult).then_inc(s_kb01, 1)

            def a_mask(i):
                after(dve, s_Op, i)
                for n, b in enumerate((2, 3)):
                    dve.wait_ge(s_Sp, 2 * i + 1)
                    v.tensor_tensor(quarters(Sm[:, n, :], 2), quarters(bank[b][:], 2), mask_two, ALU.mult).then_inc(s_Sm, 1)
                for hh in range(2):
                    dve.wait_ge(s_Sp, 2 * i + 2)
                    v.tensor_tensor(quarters(Sm[:, 2, hh * T:(hh + 1) * T], 2), quarters(bank[hh][:, 0:T], 2), causal_two,
                                    ALU.mult).then_inc(s_Sm, 1)

            def a_softmax(i):
                dve.wait_ge(s_Lp, i + 1)
                dve.wait_ge(s_eq, i + 1)
                for g in range(KK):
                    v.scalar_tensor_tensor(packed(lg[:, g * D:(g + 1) * D]), packed(eq[:, g * D:(g + 1) * D]), BIG, used(2 + g),
                                           ALU.min, ALU.mult).then_inc(s_lg, 1)
                dve.wait_ge(s_lg, 2 * i + 2)
                v.tensor_reduce(mx[:], heads(lg[:], HA), AX.X, ALU.max).then_inc(s_mx, 1)
                dve.wait_ge(s_mx, i + 1)
                v.tensor_tensor(heads(lg[:], HA), heads(lg[:], HA), per_head(mx[:], HA, MA), ALU.subtract).then_inc(s_lc, 1)

            def a_sum(i):
                dve.wait_ge(s_pe, i + 1)
                after(dve, s_zz, i)
                v.tensor_reduce(Zs[:], heads(pe_x[:], HA), AX.X, ALU.add).then_inc(s_Z, 1)
                dve.wait_ge(s_Z, i + 1)
                v.scalar_tensor_tensor(pa[:], eq[:], BIG, pe_x[:], ALU.min, ALU.mult).then_inc(s_pa, 1)

            def a_weights(i):
                for hh in range(2):
                    dve.wait_ge(s_PTp, i + 1)
                    v.tensor_tensor(quarters(PT[:, hh, :], 4), quarters(bank[2 + hh][:], 4), causal_four, ALU.mult).then_inc(s_PT, 1)

            def a_norm(i):
                dve.wait_ge(s_osq, 2 * i + 2)
                after(dve, s_rn0, i)
                v.tensor_reduce(ms[:], heads(osq[:], HA), AX.X, ALU.add).then_inc(s_ms, 1)

            def a_normed(i):
                dve.wait_ge(s_rn, i + 1)
                dve.wait_ge(s_paTp, i + 1)
                for g in range(KK):
                    v.tensor_tensor(packed(on[:, g * D:(g + 1) * D]), used(g),
                                    rn[:, 4 * g:4 * g + 4].unsqueeze(2).to_broadcast([P, 4, MA]), ALU.mult).then_inc(s_on, 1)

            def a_residual(i):
                dve.wait_ge(s_Yp, i + 1)
                dve.wait_ge(s_xres, 16 * (i + 1))
                v.tensor_tensor(yA.ap().rearrange("p c d -> p (c d)"), xres.ap().rearrange("p c d -> p (c d)"), bank[3][:],
                                ALU.add).then_inc(s_yA, 1)
                layer_norm_stats(i, yA, bnA, mvA, s_yA, s_bnA, s_mvA, NC)

            def a_x1(i):
                after(dve, s_x1b, i)
                layer_norm_apply(i, yA, mvA, rsA, s_rsA, NC, x1, s_x1)

            def b_rope(i, src, s_ready, c_out, s_out, kind, s_done, *s_used):
                dve.wait_ge(s_ready, i + 1)
                for s in s_used:
                    after(dve, s, i)
                v.tensor_tensor(c_out, bank[src][:], Rope[:, 2 * kind].rearrange("p c d -> p (c d)"), ALU.mult)
                v.tensor_tensor(s_out.rearrange("p (n two) -> p n two", two=2), swapped(bank[src][:]),
                                Rope[:, 2 * kind + 1].rearrange("p c (n two) -> p (c n) two", two=2), ALU.mult)\
                    .then_inc(s_done, 1)

            def b_gate(i):
                dve.wait_ge(s_bgp, i + 1)
                v.tensor_tensor(halves(gz[:]), halves(bank[6][:]), both_chunks(GB[:]), ALU.add).then_inc(s_gz, 1)

            def b_gate2(i):
                dve.wait_ge(s_gt, i + 1)
                v.scalar_tensor_tensor(gate[:], gt[:], 1.0, gz[:], ALU.add, ALU.mult).then_inc(s_gate, 1)

            def b_state(i):
                dve.wait_ge(s_Stp, i + 1)
                v.tensor_tensor(St.ap().rearrange("p g d -> p (g d)"), bank[7][:, 0:D],
                                StateMask.ap().rearrange("p g d -> p (g d)"), ALU.mult).then_inc(s_St, 1)

            def b_mask(i, n):
                dve.wait_ge(s_Sbp, NR * i + n + 1)
                if n >= RS:
                    dve.wait_ge(s_ret, NR * i + n - RS + 1)
                v.tensor_tensor(quarters(Sb[:, n % RS, :], 4), quarters(bank[4 + n % RS][:], 4), causal_four, ALU.mult).then_inc(s_Sb, 1)

            def b_norm(i):
                dve.wait_ge(s_rsq, i + 1)
                after(dve, s_rr0, i)
                v.tensor_reduce(rvar[:], heads(rsq[:], HB), AX.X, ALU.add).then_inc(s_rvar, 1)

            def b_gated(i):
                dve.wait_ge(s_rr, i + 1)
                after(dve, s_rgTp, i)
                v.tensor_tensor(heads(rnm[:], HB), heads(bank[7][:], HB), per_head(rr[:], HB, EB), ALU.mult).then_inc(s_rnm, 1)
                dve.wait_ge(s_rnm, i + 1)
                v.tensor_tensor(rg[:], rnm[:], gate[:], ALU.mult).then_inc(s_rg, 1)

            def b_residual(i, b=4):
                dve.wait_ge(s_Y2p, i + 1)
                dve.wait_ge(s_x1b, i + 1)
                v.tensor_tensor(yB.ap().rearrange("p c d -> p (c d)"), x1b.ap().rearrange("p c d -> p (c d)"), bank[b][:],
                                ALU.add).then_inc(s_yB, 1)
                layer_norm_stats(i, yB, bnB, mvB, s_yB, s_bnB, s_mvB, NC)

            def b_x2(i):
                after(dve, s_x2k, i)
                after(dve, s_x2Tp, i)
                layer_norm_apply(i, yB, mvB, rsB, s_rsB, NC, x2, s_x2)

            def scale_weights():
                dve.wait_ge(s_w_a, 5 * 16)
                v.tensor_scalar(Wo[:], Wo[:], Gcol[:, 0:1], MA ** 0.5, ALU.mult, ALU.mult).then_inc(s_wo, 1)
                dve.wait_ge(s_w_b, 10 * 16)
                v.tensor_scalar(OW[:], OW[:], 0.5 * EB ** 0.5, None, ALU.mult)
                rv_heads = RV.ap().rearrange("p k (h e) -> p (k h) e", e=EB)
                v.tensor_reduce(RVmean[:], rv_heads, AX.X, ALU.add).then_inc(s_rvm, 1)
                dve.wait_ge(s_rvm, 1)
                v.tensor_scalar(RVmean[:], RVmean[:], 1.0 / EB, None, ALU.mult).then_inc(s_rvm, 1)
                dve.wait_ge(s_rvm, 2)
                v.tensor_tensor(rv_heads, rv_heads, RVmean.ap().unsqueeze(2).to_broadcast([P, KK * HB, EB]), ALU.subtract)\
                    .then_inc(s_rv, 1)

            def split_weights():
                for n, (w2, w) in enumerate(((Wo2, Wo), (RK2, RK), (RQ2, RQ), (GW2, GW), (RV2, RV), (OW2, OW))):
                    split_lower(w2[1][:], w[:], w2[0][:], s_pwh, n + 4, s_pwl)

            def step(p, a, b, c, setup=False):
                if a is not None:
                    a_keys(a)
                    a_mask(a)
                if b is not None:
                    b_rope(b, 6, s_bkp, kc, ks, 1, s_kcs, s_kxTp, s_Stp)
                    split_bank(x1T, 5, s_x1Th, b, s_x1T)
                if c is not None:
                    b_gated(c)
                if a is not None:
                    a_softmax(a)
                if c is not None:
                    split_bank(rgT, 4, s_rgTh, c, s_rgT)
                if b is not None:
                    b_rope(b, 5, s_bqp, qc, qs, 0, s_qcs, s_qxTp)
                    b_gate(b)
                if a is not None:
                    a_sum(a)
                if c is not None:
                    b_residual(c)
                if setup:
                    scale_weights()
                if b is not None:
                    b_gate2(b)
                    b_state(b)
                if c is not None:
                    b_x2(c)
                if b is not None:
                    for n in range(4):
                        b_mask(b, n)
                if a is not None:
                    a_weights(a)
                if setup:
                    split_weights()
                if b is not None:
                    b_mask(b, 4)
                    b_mask(b, 5)
                if a is not None:
                    a_norm(a)
                if b is not None:
                    b_mask(b, 6)
                if a is not None:
                    a_normed(a)
                if b is not None:
                    b_mask(b, 7)
                if a is not None:
                    split_bank(onT, 2, s_onTh, a, s_onT)
                if p is not None:
                    p_swish(p, 4, thq, s_thq, qTs, s_q)
                if a is not None:
                    a_residual(a)
                if b is not None:
                    b_norm(b)
                if p is not None:
                    p_swish(p, 5, thk, s_thk, kTs, s_k)
                if a is not None:
                    a_x1(a)

            step(0, None, None, None)
            step(1, 0, None, None, setup=True)
            step(2, 1, 0, None)
            with dve.Fori(3, B) as i:
                step(i, i - 1, i - 2, i - 3)
            step(None, B - 1, B - 2, B - 3)
            step(None, None, B - 1, B - 2)

            def split_x2(n):
                for r in range(2):
                    split_lower(x2Tl[:, 2 * n + r, :], x2T_all[:, 2 * n + r, :], x2Th[:, 2 * n + r, :],
                                s_xh, 2 * n + r + 1, s_xl)

            def ffn(n, last_row=None):
                first, last = (isinstance(n, int) and n == m for m in (0, NT - 1))
                for f in range(NF):
                    if f == 2 and not first:
                        layer_norm_stats(n - 1, yF, bnF, mvF, s_yF, s_bnF, s_mvF, 4, counts=4)
                    if f == 4 and not first:
                        layer_norm_apply(n - 1, yF, mvF, rsF, s_rsF, 4, xo, s_xo)
                    if f == 2 and last_row is not None:
                        b_gated(last_row)
                    if f == 6 and last_row is not None:
                        split_bank(rgT, 6, s_rgTh, last_row, s_rgT)
                    if f == 6 and not last:
                        split_x2(n + 1)
                    after(dve, s_hused, NF * n + f + 1 - HR)
                    split_lower(hidl[:, f % HR, :], hid[:, f % HR, :], hidh[:, f % HR, :], s_hh, NF * n + f + 1, s_hl)
                if last_row is not None:
                    b_residual(last_row, 6)
                    b_x2(last_row)
                dve.wait_ge(s_x2b, n + 1)
                after(dve, s_out, 16 * n)
                after(dve, s_xo, 4 * n)
                dve.wait_ge(s_hused, NF * (n + 1))
                for t in range(4):
                    v.tensor_tensor(yF[:, t, :], x2b[:, t, :], bank[4 + t // 2][:, (t % 2) * D:(t % 2 + 1) * D], ALU.add)\
                        .then_inc(s_yF, 1)

            split_x2(0)
            ffn(0, last_row=B - 1)
            with dve.Fori(1, NT - 1) as n:
                ffn(n)
            ffn(NT - 1)
            layer_norm_stats(NT - 1, yF, bnF, mvF, s_yF, s_bnF, s_mvF, 4, counts=4)
            layer_norm_apply(NT - 1, yF, mvF, rsF, s_rsF, 4, xo, s_xo)

        @block.gpsimd
        def _(pool):
            g = nc.gpsimd

            def rstd(dst, var, eps, n, s_mid, s_done, i):
                g.tensor_tensor(dst, var, eps[:].to_broadcast([P, n]), ALU.add).then_inc(s_mid, 1)
                pool.wait_ge(s_mid, i + 1)
                g.tensor_tensor(dst, dst, Half[:, 0:n], ALU.pow).then_inc(s_done, 1)

            def split_lower(dst, src, upper, ready, count, done):
                pool.wait_ge(ready, count)
                g.tensor_tensor(dst[:], src[:], upper[:].bitcast(F32), ALU.subtract).then_inc(done, 1)

            def a_decayed(i):
                pool.wait_ge(s_Z, i + 1)
                g.tensor_tensor(zz[:], Zs[:], Zs[:], ALU.mult).then_inc(s_zz, 1)

            def a_norm(i):
                pool.wait_ge(s_zz, i + 1)
                g.tensor_tensor(zz[:], zz[:], EpsA[:].to_broadcast([P, NC * HA]), ALU.mult).then_inc(s_zz2, 1)
                pool.wait_ge(s_ms, i + 1)
                pool.wait_ge(s_zz2, i + 1)
                g.tensor_tensor(zz[:], ms[:], zz[:], ALU.add).then_inc(s_rn0, 1)
                pool.wait_ge(s_rn0, i + 1)
                after(pool, s_on, i)
                g.tensor_tensor(rn[:], zz[:], Half[:, 0:NC * HA], ALU.pow).then_inc(s_rn, 1)

            def a_rstd(i):
                pool.wait_ge(s_mvA, NC * (i + 1))
                after(pool, s_x1, NC * i)
                rstd(rsA[:], mvA[:, :, 1], Eps, NC, s_va, s_rsA, i)

            def b_bias(i):
                pool.wait_ge(s_x1, NC * (i + 1))
                after(pool, s_x2, NC * i)
                g.tensor_tensor(x1b[:], x1[:], both_chunks(OB[:]), ALU.add).then_inc(s_x1b, 1)

            def b_rope_k(i):
                pool.wait_ge(s_kcs, i + 1)
                g.tensor_tensor(kx[:], kc[:], ks[:], ALU.add).then_inc(s_kx, 1)

            def b_rope_q(i):
                pool.wait_ge(s_qcs, i + 1)
                g.tensor_tensor(qx[:], qc[:], qs[:], ALU.add).then_inc(s_qx, 1)

            def b_norm(i):
                pool.wait_ge(s_rvar, i + 1)
                after(pool, s_rnm, i)
                rstd(rr[:], rvar[:], EpsB, NC * HB, s_rr0, s_rr, i)

            def b_rstd(i):
                pool.wait_ge(s_mvB, NC * (i + 1))
                after(pool, s_x2, NC * i)
                rstd(rsB[:], mvB[:, :, 1], Eps, NC, s_vb2, s_rsB, i)
                pool.wait_ge(s_x2, NC * (i + 1))
                g.tensor_copy(x2_all[:, i, :], x2.ap().rearrange("p c d -> p (c d)")).then_inc(s_x2k, 1)

            def step(p, a, b, c, ffn_weights=False):
                if b is not None:
                    b_rope_k(b)
                    b_rope_q(b)
                if c is not None:
                    b_rstd(c)
                if b is not None:
                    b_bias(b)
                if p is not None:
                    split_lower(xTp2[1], xTp, xTp2[0], s_xph, p + 1, s_xpl)
                if a is not None:
                    split_lower(cT2[1], cT, cT2[0], s_cTh, a + 1, s_cTl)
                    a_decayed(a)
                    a_norm(a)
                    a_rstd(a)
                if ffn_weights:
                    split_lower(W1l, W1, W1h, s_wh, 1, s_wl)
                    split_lower(W2l, W2, W2h, s_wh, 2, s_wl)
                if b is not None:
                    b_norm(b)

            g.memset(Vp[:], 0.0).then_inc(s_Vp0, 1)
            pool.wait_ge(s_half, 6)
            step(0, None, None, None)
            step(1, 0, None, None)
            pool.wait_ge(s_w_b, 10 * 16)
            step(2, 1, 0, None)
            with pool.Fori(3, B) as i:
                step(i, i - 1, i - 2, i - 3)
            step(None, B - 1, B - 2, B - 3)
            step(None, None, B - 1, B - 2, ffn_weights=True)

            def ffn(n):
                pool.wait_ge(s_x2k, 2 * n + 2)
                after(pool, s_yF, 4 * n)
                for r in range(2):
                    last = g.tensor_tensor(x2b[:, 2 * r:2 * r + 2, :], halves(x2_all[:, 2 * n + r, :]), both_chunks(B2[:]), ALU.add)
                last.then_inc(s_x2b, 1)

            def ffn_rstd(n):
                pool.wait_ge(s_mvF, 4 * (n + 1))
                rstd(rsF[:], mvF[:, :, 1], Eps, 4, s_vf, s_rsF, n)

            pool.wait_ge(s_ret, NR * B)
            ffn(0)
            b_rstd(B - 1)
            with pool.Fori(1, NT) as n:
                ffn(n)
                ffn_rstd(n - 1)
            ffn_rstd(NT - 1)


def shape_constants():
    s = np.arange(P)
    causal = (s[:, None] <= s[None, :]).astype(np.float32)
    mask = np.stack([causal, np.ones((P, P), np.float32)], axis=1)
    mid = P // 2 - 1
    src, tok = s[:, None], s[None, :]
    own = ((src > mid) & (src <= tok)).astype(np.float32) - ((src <= mid) & (src > tok)).astype(np.float32)
    later = (src > tok).astype(np.float32)
    nxt = (src <= mid).astype(np.float32) * np.ones((P, P), np.float32)
    decay_w = np.stack([own, later, nxt], axis=1) / np.float32(8.0)
    f32 = np.float32
    base = (np.arange(0, EB, 2, dtype=f32) + f32(0.4 * EB)) / f32(1.4 * EB)
    power = (np.arange(-(T // 2), T - T // 2, dtype=f32) / f32(512.0))[:, None]
    scale = np.power(base[None, :], power, dtype=f32)
    inv_freq = (f32(1.0) / np.power(f32(10000.0), np.arange(EB // 2, dtype=f32) / f32(EB // 2), dtype=f32)).astype(f32)
    ang = np.arange(T, dtype=f32)[:, None] * inv_freq[None, :]
    gam = f32(1.0) - np.exp(np.linspace(np.log(1 / 32.0), np.log(1 / 512.0), HB)).astype(f32)
    rel = np.arange(T) % P - P // 2
    tables = []
    for sc, sign in ((scale.astype(np.float64), 1.0), (1.0 / scale.astype(np.float64), -1.0)):
        dec = gam.astype(np.float64)[None, :] ** (sign * rel[:, None])
        for fn, signs in ((np.cos, (1.0, 1.0)), (np.sin, (-1.0, 1.0))):
            pair = fn(ang.astype(np.float64)) * sc
            pair = np.stack([pair * signs[0], pair * signs[1]], axis=-1).reshape(T, EB)
            full = (dec[:, :, None] * pair[:, None, :]).reshape(T, D)
            tables.append(full.reshape(NC, P, D).transpose(1, 0, 2))
    rope = np.stack(tables, axis=1).astype(f32)
    parity = np.stack([(s // EB) % 2 == 0, (s // EB) % 2 == 1], axis=1).astype(f32)
    head = s // EB
    state_mask = np.zeros((P, KK, P), f32)
    for g in range(KK):
        state_mask[:, g, :] = (head[:, None] == head[None, :]) * (gam.astype(np.float64)[g * 8 + head] ** P)[:, None]
    return dict(ident=np.eye(P, dtype=f32), mask=mask, decay_w=decay_w.astype(f32), rope=rope,
                parity=parity, state_mask=state_mask)


def kernel(x, ctx_1024, L0_attn_Wq, L0_attn_Wk, L0_attn_Wv, L0_attn_Wf, L0_attn_g_norm_w, L0_attn_Wo,
           L0_xattn_W_Q, L0_xattn_W_K, L0_xattn_W_V, L0_xattn_g_w, L0_xattn_g_b, L0_xattn_out_w, L0_xattn_out_b,
           L0_ffn_w1, L0_ffn_b1, L0_ffn_w2, L0_ffn_b2):
    import concourse.bacc as bacc
    from concourse.bass_utils import run_bass_kernel_spmd

    def tokens(a):
        return a.reshape(B, NC, P, D).transpose(0, 2, 1, 3)

    def features(a):
        return a.transpose(0, 2, 1).reshape(B, KK, P, T).transpose(0, 2, 1, 3)

    def weight(w):
        return w.reshape(w.shape[0] // P, P, w.shape[1]).transpose(1, 0, 2)

    def head_weight(w):
        return weight(w.transpose(1, 0, 2).reshape(D, D))

    def row(b):
        return np.broadcast_to(b[None, :], (P, D))

    arrays = dict(
        x_tok=tokens(x), x_feat=features(x), c_feat=features(ctx_1024),
        wq=weight(L0_attn_Wq), wk=weight(L0_attn_Wk), wv=weight(L0_attn_Wv), wf=weight(L0_attn_Wf),
        gcol=np.concatenate([L0_attn_g_norm_w] * 2)[:, None], wo=weight(L0_attn_Wo),
        rq=head_weight(L0_xattn_W_Q), rk=head_weight(L0_xattn_W_K), rv=head_weight(L0_xattn_W_V),
        gw=weight(L0_xattn_g_w.transpose(1, 0)), gb=row(L0_xattn_g_b),
        ow=weight(L0_xattn_out_w.transpose(1, 0)), ob=row(L0_xattn_out_b),
        w1=weight(L0_ffn_w1), b1=L0_ffn_b1.reshape(NF, P).transpose(1, 0), w2=weight(L0_ffn_w2), b2=row(L0_ffn_b2),
        **shape_constants())
    nc = bacc.Bacc("TRN2", target_bir_lowering=False, num_devices=1)
    ins, feed = {}, {}
    for name, a in arrays.items():
        a = np.ascontiguousarray(a)
        feed[f"in_{name}"] = a
        ins[name] = nc.dram_tensor(f"in_{name}", a.shape, mybir.dt.from_np(a.dtype), kind="ExternalInput").ap()
    out = nc.dram_tensor("out_rows", (NT, P, 4, D), F32, kind="ExternalOutput").ap()
    decoder_kernel(nc, out=out, **ins)
    r = run_bass_kernel_spmd(nc, [feed], core_ids=[0])
    got = r.results[0]["out_rows"]
    return got.transpose(0, 2, 1, 3).reshape(B, T, D)
```

```python
import numpy as np
import concourse.bass as bass
from concourse import mybir
from concourse.alu_op_type import AluOpType as ALU

F32, F32R = mybir.dt.float32, mybir.dt.float32r
ACT = mybir.ActivationFunctionType
AX = mybir.AxisListType

B, T, D = 8, 256, 256
P = 128
NC = T // P
KK = D // P
HA, MA = 4, 64
HB, EB = 16, 16
F = 1024
NF = F // P
TT = 512
NT = B * T // TT
EPS = 1e-5
BIG = 1e30
PACK = T * KK


def decoder_kernel(nc, x_tok, x_feat, c_feat, wq, wk, wv, wf, gcol, wo, rq, rk, rv, gw, gb, ow, ob,
                   w1, b1, w2, b2, ident, mask, decay_w, rope, parity, state_mask, out):
    place = {}

    def sb(name, shape):
        place[name] = (nc.sbuf_base + 31) // 32 * 32
        return nc.alloc_sbuf_tensor(name, shape, F32)

    def over(name, shape, dtype, at, start=0):
        return nc.alloc_sbuf_tensor_at(name, shape, dtype, offset=place[at] + 4 * start)

    def sem(name):
        return nc.alloc_semaphore(name)

    def halves(ap):
        return ap.rearrange("p (c d) -> p c d", c=NC)

    W2 = sb("W2", [P, NF, D])
    Wq, Wk, Wv, Wf = (W2[:, 2 * n:2 * n + 2, :] for n in range(4))
    def split_weight(name, at, start=0):
        return (nc.alloc_sbuf_tensor(name + "h", [P, KK, D], F32R), over(name + "l", [P, KK, D], F32R, at, start))

    Wo, Gcol = sb("Wo", [P, KK, D]), sb("Gcol", [P, 1])
    RQ, RK, RV, GW, OW = (sb(n, [P, KK, D]) for n in ("RQ", "RK", "RV", "GW", "OW"))
    Wq2, Wk2, Wv2 = (split_weight(w, "W2", n * PACK) for n, w in enumerate(("Wq", "Wk", "Wv")))
    Wo2, RQ2, RK2, RV2, GW2, OW2 = (split_weight(w, w) for w in ("Wo", "RQ", "RK", "RV", "GW", "OW"))
    GB, OB, B2 = sb("GB", [P, D]), sb("OB", [P, D]), sb("B2", [P, D])
    B1 = sb("B1", [P, NF])
    Ident = sb("Ident", [P, P])
    Mask = sb("Mask", [P, 2, P])
    DecayW = sb("DecayW", [P, 3, P])
    work_b = sb("work_b", [P, 4 * PACK + NC * KK * HB // KK * (P + EB)])
    DecayWr = over("DecayWr", [P, 3, P], F32R, "DecayW")
    Rope = work_b[:, 0:4 * PACK].rearrange("p (n c d) -> p n c d", n=4, c=NC)
    Parity = sb("Parity", [P, 2])
    StateMask = sb("StateMask", [P, KK, P])
    Half = sb("Half", [P, NC * HB])
    One, Eps, EpsA, EpsB = (sb(n, [P, 1]) for n in ("One", "Eps", "EpsA", "EpsB"))
    RVmean = sb("RVmean", [P, KK * HB])

    e_all, f_all = sb("e_all", [P, B, PACK]), sb("f_all", [P, B, PACK])
    x2_all, x2T_all = e_all, f_all

    def split_tile(name, at=None):
        lower = over(name + "l", [P, KK, T], F32R, at) if at else nc.alloc_sbuf_tensor(name + "l", [P, KK, T], F32R)
        return nc.alloc_sbuf_tensor(name + "h", [P, KK, T], F32R), lower

    xTp, th = sb("xTp", [P, KK, T]), sb("th", [P, PACK])
    xTp2 = split_tile("xTp", "xTp")
    kTs, qTs, vs = sb("kTs", [P, PACK]), sb("qTs", [P, PACK]), sb("vs", [P, PACK])

    fh, fl = (nc.alloc_sbuf_tensor(n, [P, PACK], F32R) for n in ("fh", "fl"))
    work_a = sb("work_a", [P, 12 * PACK])
    Sm = work_a[:, 0:3 * PACK].rearrange("p (n x) -> p n x", n=3)
    eq, ek, ex, kb, kbT, lg, pe_x, paT = (work_a[:, n * PACK:(n + 1) * PACK] for n in range(3, 11))
    kbT, paT = (x.rearrange("p (g c t) -> p g c t", g=KK, c=NC) for x in (kbT, paT))
    ex01, kb01 = (work_a[:, 11 * PACK + n * D:11 * PACK + (n + 1) * D] for n in range(2))
    pa = pe_x
    mx, Zs, ms, zz, rn = (sb(n, [P, NC * HA]) for n in ("mx", "Zs", "ms", "zz", "rn"))
    PT = Sm
    Hv = sb("Hv", [P, D])
    osq = lg
    on, onT = pa, split_tile("onT")
    xres, x1 = sb("xres", [P, NC, D]), sb("x1", [P, NC, D])
    yA = xres
    bnA, mvA, rsA = sb("bnA", [P, NC, 6]), sb("mvA", [P, NC, 2]), sb("rsA", [P, NC])

    cT = sb("cT", [P, KK, T])
    cT2 = split_tile("cT", "cT")
    x1b, x1T = sb("x1b", [P, NC, D]), split_tile("x1T")
    work_c = sb("work_c", [P, 10 * PACK])
    qc, qs, kc, ks = (work_c[:, n * PACK:(n + 1) * PACK] for n in range(4))
    qx, kx, vb = qc, kc, sb("vb", [P, D])
    Vp = work_b[:, 4 * PACK:].rearrange("p (a w) -> p a w", a=NC * KK)
    gz, gt = sb("gz", [P, PACK]), sb("gt", [P, PACK])
    gate = gt
    qxT = sb("qxT", [P, KK, P])
    qxP = work_c[:, 4 * PACK:6 * PACK].rearrange("p (g c a t) -> p g c a t", g=KK, c=NC, a=2)
    kxT = work_c[:, 6 * PACK:7 * PACK].rearrange("p (g c t) -> p g c t", g=KK, c=NC)
    St = sb("St", [P, KK, P])
    NR = 8
    RS = 3
    Sb = work_c[:, 7 * PACK:10 * PACK].rearrange("p (n x) -> p n x", n=RS)
    rsq = gz
    rvar, rr = sb("rvar", [P, NC * HB]), sb("rr", [P, NC * HB])
    rnm, rgT = sb("rnm", [P, PACK]), split_tile("rgT")
    rg = rnm
    yB, x2 = x1b, sb("x2", [P, NC, D])
    xT = [halves(qc), halves(qs)]
    az = kc, ks

    bnB, mvB, rsB = sb("bnB", [P, NC, 6]), sb("mvB", [P, NC, 2]), sb("rsB", [P, NC])

    W1 = sb("W1", [P, KK, F])
    W1h, W2h = over("W1h", [P, KK, F], F32R, "work_a"), over("W2h", [P, NF, D], F32R, "work_a", 4 * PACK)
    W1l, W2l = over("W1l", [P, KK, F], F32R, "W1"), over("W2l", [P, NF, D], F32R, "W2")
    x2Th, x2Tl = over("x2Th", [P, B, PACK], F32R, "work_b"), over("x2Tl", [P, B, PACK], F32R, "f_all")
    HR = 4
    hid = over("hid", [P, HR, TT], F32, "work_a", 8 * PACK)
    hidh, hidl = (over(name, [P, HR, TT], F32R, "work_c", n * HR * TT) for n, name in enumerate(("hidh", "hidl")))
    x2b = over("x2b", [P, 4, D], F32, "work_c", 8 * PACK)
    yF, xo = (over(name, [P, 4, D], F32, "work_b", (B + 2 * n) * PACK) for n, name in enumerate(("yF", "xo")))
    bnF, mvF, rsF = sb("bnF", [P, 4, 6]), sb("mvF", [P, 4, 2]), sb("rsF", [P, 4])

    bank = [nc.alloc_psum_tensor(f"bank{n}", [P, 512], F32) for n in range(8)]

    s_w_forget, s_w_v, s_w_qk, s_w_a, s_w_b, s_w_f = sem("w_forget"), sem("w_v"), sem("w_qk"), sem("w_a"), sem("w_b"), sem("w_f")
    s_xT = [sem("xT_even"), sem("xT_odd")]
    s_xTp = sem("xTp_in")
    s_xres, s_cT, s_out = sem("xres_in"), sem("cT_in"), sem("out_stored")
    s_half, s_wo, s_rvm, s_rv = sem("half"), sem("wo_scaled"), sem("rv_mean"), sem("rv_centred")
    s_pwh, s_pwl = sem("weights_upper"), sem("weights_lower")
    s_xph, s_xpl, s_cTh, s_cTl = sem("xTp_upper"), sem("xTp_lower"), sem("cT_upper"), sem("cT_lower")
    s_onTh, s_x1Th, s_rgTh = sem("onT_upper"), sem("x1T_upper"), sem("rgT_upper")
    s_Vp0 = sem("value_windows_cleared")
    s_qp, s_kp, s_vp, s_zp = sem("q_psum"), sem("k_psum"), sem("v_psum"), sem("z_psum")
    s_thq, s_thk, s_v, s_az, s_e = sem("q_tanh"), sem("k_tanh"), sem("v_kept"), sem("z_abs"), sem("z_exp")
    s_q, s_k, s_mz, s_ln, s_f = sem("q_kept"), sem("k_kept"), sem("z_min"), sem("z_ln"), sem("f_kept")
    s_dw, s_fh, s_fl = sem("decay_weights"), sem("f_upper"), sem("f_lower")
    s_ex, s_sg = sem("gate_exp"), sem("slot_gain")
    s_Ep, s_E01p, s_eq, s_ek, s_ex01 = sem("E_psum"), sem("E01_psum"), sem("e_query"), sem("e_key"), sem("e_next")
    s_kb, s_kb01 = sem("key_gain"), sem("key_gain_next")
    s_Sp, s_Sm = sem("S_psum"), sem("S_masked")
    s_kbTp, s_kbT = sem("kbT_psum"), sem("kbT")
    s_Lp, s_lg, s_mx, s_lc, s_pe = sem("L_psum"), sem("logits"), sem("logit_max"), sem("logits_shifted"), sem("p_exp")
    s_Z, s_zz, s_pa, s_paTp, s_paT = sem("p_sum"), sem("p_sum_sq"), sem("p_decayed"), sem("paT_psum"), sem("paT")
    s_PTp, s_PT, s_Hvp, s_Hv = sem("PT_psum"), sem("PT_masked"), sem("Hv_psum"), sem("Hv")
    s_Op, s_osq, s_ms, s_rn0, s_rn, s_on = sem("O_psum"), sem("O_sq"), sem("O_ms"), sem("rn_var"), sem("rn"), sem("O_normed")
    s_onTp, s_onT, s_Yp, s_yA = sem("onT_psum"), sem("onT"), sem("Y_psum"), sem("yA")
    s_bnA, s_mvA, s_rsA, s_x1 = sem("bnA"), sem("mvA"), sem("rsA"), sem("x1")
    s_va, s_zz2 = sem("varA_eps"), sem("Z2_eps")
    s_x1b, s_x1Tp, s_x1T = sem("x1_plus_bias"), sem("x1T_psum"), sem("x1T")
    s_bqp, s_bkp, s_bvp, s_bgp = sem("bq_psum"), sem("bk_psum"), sem("bv_psum"), sem("bg_psum")
    s_qcs, s_kcs, s_qx, s_kx, s_vb = sem("q_rope_parts"), sem("k_rope_parts"), sem("q_roped"), sem("k_roped"), sem("bv")
    s_gz, s_gt, s_gate = sem("gate_z"), sem("gate_tanh"), sem("gate")
    s_qxTp, s_kxTp, s_qxT, s_qxP, s_kxT = sem("qxT_psum"), sem("kxT_psum"), sem("qxT"), sem("qxP"), sem("kxT")
    s_Stp, s_St = sem("state_psum"), sem("state")
    s_Sbp, s_Sb, s_ret = sem("ret_scores_psum"), sem("ret_scores"), sem("ret_group_summed")
    s_rsq, s_rvar, s_rr0, s_rr, s_rnm, s_rg = sem("ret_sq"), sem("ret_var"), sem("ret_var_eps"), sem("ret_rstd"), sem("ret_normed"), sem("ret_gated")
    s_rgTp, s_rgT, s_Y2p, s_yB = sem("rgT_psum"), sem("rgT"), sem("Y2_psum"), sem("yB")
    s_bnB, s_mvB, s_rsB, s_x2, s_x2k = sem("bnB"), sem("mvB"), sem("rsB"), sem("x2"), sem("x2_kept")
    s_vb2 = sem("varB_eps")
    s_x2Tp, s_x2T = sem("x2T_psum"), sem("x2T_kept")
    s_hp, s_h, s_hused = sem("h_psum"), sem("h_gelu"), sem("h_used")
    s_hh, s_hl = sem("h_upper"), sem("h_lower")
    s_wh, s_wl, s_xh, s_xl = sem("ffn_weight_upper"), sem("ffn_weight_lower"), sem("x2T_upper"), sem("x2T_lower")
    s_x2b, s_yF = sem("x2_plus_b2"), sem("yF")
    s_bnF, s_mvF, s_rsF, s_xo = sem("bnF"), sem("mvF"), sem("rsF"), sem("xo")
    s_vf = sem("varF_eps")

    def logit_bank(n):
        return bank[(7, 4)[n % 2]]

    def heads(ap, h):
        return ap.rearrange("p (g e) -> p g e", g=NC * h)

    def per_head(stat, h, e):
        return stat.unsqueeze(2).to_broadcast([P, NC * h, e])

    def after(eng, semaphore, count):
        if not isinstance(count, int) or count > 0:
            eng.wait_ge(semaphore, count)

    def rows(count):
        return min(count, B) if isinstance(count, int) else count

    def quarters(ap, n):
        return ap.rearrange("p (h t) -> p h t", h=n)

    mask_two = Mask.ap().rearrange("p a t -> p (a t)").unsqueeze(1).to_broadcast([P, 2, 2 * P])
    causal_two = Mask[:, 0, :].unsqueeze(1).to_broadcast([P, 2, P])
    causal_four = Mask[:, 0, :].unsqueeze(1).to_broadcast([P, 4, P])

    def wide(b, c, hh):
        o = c * D + hh * MA
        return bank[b][:, o:o + P]

    def used(b):
        return bank[b].ap().rearrange("p (q m) -> p q m", q=4)[:, :, 0:MA]

    def packed(ap):
        return ap.rearrange("p (q m) -> p q m", q=4)

    def both_chunks(row_bias):
        return row_bias.unsqueeze(1).to_broadcast([P, NC, D])

    def swapped(ap):
        return ap.rearrange("p (n two) -> p n two", two=2)[:, :, ::-1]

    block = nc.Block()
    with block:
        @block.sync
        def _(sp):
            sp.dma_start(Wf, wf).then_inc(s_w_forget, 16)

            def load_xT(n):
                if n >= 2:
                    sp.wait_ge(s_zp, n - 1)
                sp.dma_start(xT[n % 2][:], x_feat[n]).then_inc(s_xT[n % 2], 16)

            load_xT(0)
            load_xT(1)
            sp.dma_start(xTp[:], x_feat[0]).then_inc(s_xTp, 16)
            sp.dma_start(Wv, wv).then_inc(s_w_v, 16)
            for w, src in ((Wq, wq), (Wk, wk)):
                sp.dma_start(w, src).then_inc(s_w_qk, 16)
            load_xT(2)
            load_xT(3)
            for w, src in ((DecayW, decay_w), (Mask, mask), (Ident, ident), (Wo, wo), (Gcol, gcol)):
                sp.dma_start(w[:], src).then_inc(s_w_a, 16)
            sp.dma_start(xres[:], x_tok[0]).then_inc(s_xres, 16)
            sp.dma_start(cT[:], c_feat[0]).then_inc(s_cT, 16)
            sp.wait_ge(s_kp, 1)
            sp.dma_start(xTp[:], x_feat[1]).then_inc(s_xTp, 16)
            for w, src in ((RV, rv), (OW, ow), (RQ, rq), (RK, rk), (GW, gw), (GB, gb), (OB, ob),
                           (Rope, rope), (Parity, parity), (StateMask, state_mask)):
                sp.dma_start(w[:], src).then_inc(s_w_b, 16)
            for n in range(4, B):
                load_xT(n)
            for w, src in ((W1, w1), (B1, b1), (B2, b2)):
                sp.dma_start(w[:], src).then_inc(s_w_f, 16)

            def load_rows(i):
                sp.wait_ge(s_kp, i)
                sp.dma_start(xTp[:], x_feat[i]).then_inc(s_xTp, 16)
                sp.wait_ge(s_x1, NC * (i - 1))
                sp.dma_start(xres[:], x_tok[i - 1]).then_inc(s_xres, 16)
                sp.wait_ge(s_bvp, i - 1)
                sp.dma_start(cT[:], c_feat[i - 1]).then_inc(s_cT, 16)

            with sp.Fori(2, B) as i:
                load_rows(i)
            sp.wait_ge(s_x1, NC * (B - 1))
            sp.dma_start(xres[:], x_tok[B - 1]).then_inc(s_xres, 16)
            sp.wait_ge(s_bvp, B - 1)
            sp.dma_start(cT[:], c_feat[B - 1]).then_inc(s_cT, 16)
            sp.wait_ge(s_kp, B)
            sp.dma_start(W2[:], w2).then_inc(s_w_f, 16)
            with sp.Fori(0, NT) as n:
                sp.wait_ge(s_xo, 4 * n + 4)
                sp.dma_start(out[n], xo[:]).then_inc(s_out, 16)
            sp.wait_ge(s_out, 16 * NT)

        @block.tensor
        def _(pe):
            mm, tr = nc.tensor.matmul, nc.tensor.transpose

            def forget(n):
                pe.wait_ge(s_xT[n % 2], 16 * (n // 2 + 1))
                if n >= 2:
                    pe.wait_ge(s_mz, n - 1)
                    pe.wait_ge(s_az, n - 1)
                for c in range(NC):
                    for kk in range(KK):
                        last = mm(logit_bank(n)[:, c * D:(c + 1) * D], xT[n % 2][:, kk, c * P:(c + 1) * P], Wf[:, kk, :],
                                  start=kk == 0, stop=kk == KK - 1)
                last.then_inc(s_zp, 1)

            pe.wait_ge(s_w_forget, 16)
            forget(0)
            forget(1)

            def three_passes(a, b):
                return [(u, w, kk) for kk in range(KK) for u, w in ((a[0], b[0]), (a[0], b[1]), (a[1], b[0]))]

            def p_v(i):
                pe.wait_ge(s_xpl, i + 1)
                after(pe, s_Sb, NR * (i - 2) + 6)
                project(bank[6], xTp2, Wv2, s_vp)

            def p_qk(i, b, w, done, n):
                if isinstance(i, int) and i == 0:
                    pe.wait_ge(s_az, 2)
                    pe.wait_ge(s_mz, 2)
                    pe.wait_ge(s_pwl, 3)
                after(pe, s_Sb, NR * (i - 2) + n)
                for g in range(KK):
                    for m, (w_part, x_part, kk) in enumerate(three_passes(w, xTp2)):
                        last = mm(bank[b][:, g * T:(g + 1) * T], w_part[:, kk, g * P:(g + 1) * P], x_part[:, kk, :],
                                  start=m == 0, stop=m == 3 * KK - 1)
                last.then_inc(done, 1)

            def a_decay(i):
                pe.wait_ge(s_fl, i + 1)
                after(pe, s_on, 2 * i)
                for m, part in enumerate((fh, fl)):
                    last = mm(bank[0][:], DecayWr[:, 0, :], part[:], start=m == 0, stop=m == 1)
                last.then_inc(s_Ep, 1)
                terms = [(w, part, half) for w, half in ((1, slice(0, D)), (2, slice(D, 2 * D))) for part in (fh, fl)]
                for m, (w, part, half) in enumerate(terms):
                    last = mm(bank[1][:, 0:D], DecayWr[:, w, :], part[:, half], start=m == 0, stop=m == 3)
                last.then_inc(s_E01p, 1)

            def a_scores(i):
                pe.wait_ge(s_k, i + 1)
                pe.wait_ge(s_q, i + 1)
                after(pe, s_onT, i)
                after(pe, s_yA, i)
                for g in range(KK):
                    for hh in range(2):
                        r = slice(64 * hh, 64 * hh + 64)
                        last = mm(bank[2 + hh][:, g * T:(g + 1) * T], kTs[r, g * T:g * T + P], qTs[r, g * T:(g + 1) * T],
                                  start=True, stop=True)
                last.then_inc(s_Sp, 1)
                pe.wait_ge(s_eq, i + 1)
                pe.wait_ge(s_ex01, i + 1)
                for g in range(KK):
                    for hh in range(2):
                        r = slice(64 * hh, 64 * hh + 64)
                        last = mm(bank[hh][:, g * P:(g + 1) * P], kTs[r, g * T + P:(g + 1) * T],
                                  qTs[r, g * T + P:(g + 1) * T], start=True, stop=True)
                last.then_inc(s_Sp, 1)

            def transposes(dst, src, ready, count, done, chunk_major=True):
                pe.wait_ge(ready, count)
                for g in range(KK):
                    for c in range(NC):
                        o = (g * NC + c) * P
                        i = c * D + g * P if chunk_major else o
                        last = tr(dst[:, o:o + P], src[:, i:i + P], Ident[:])
                last.then_inc(done, 1)

            def a_kbT(i):
                pe.wait_ge(s_Sm, 4 * i + 4)
                transposes(bank[0], kb, s_kb, i + 1, s_kbTp)

            def a_logits(i):
                pe.wait_ge(s_kb, i + 1)
                pe.wait_ge(s_kb01, i + 1)
                for g in range(KK):
                    for hh in range(2):
                        m, m1 = slice(g * P, (g + 1) * P), slice(D + g * P, D + (g + 1) * P)
                        mm(wide(2 + g, 0, hh), Sm[:, hh, g * T:g * T + P], kb[:, m], start=True, stop=True, skip_group_check=True)
                        mm(wide(2 + g, 1, hh), Sm[:, hh, g * T + P:(g + 1) * T], kb01[:, m], start=True, stop=False, skip_group_check=True)
                        last = mm(wide(2 + g, 1, hh), Sm[:, 2, (2 * hh + g) * P:(2 * hh + g + 1) * P], kb[:, m1],
                                  start=False, stop=True, skip_group_check=True)
                last.then_inc(s_Lp, 1)

            def a_paT(i):
                after(pe, s_kxT, i)
                transposes(bank[1], pa, s_pa, i + 1, s_paTp, chunk_major=False)

            def a_weights(i):
                pe.wait_ge(s_kbT, i + 1)
                pe.wait_ge(s_paT, i + 1)
                for g in range(KK):
                    for c in range(NC):
                        for hh in range(2):
                            r, o = slice(64 * hh, 64 * hh + 64), (2 * g + c) * P
                            last = mm(bank[2 + hh][:, o:o + P], kbT[r, g, c, :], paT[r, g, c, :], start=True, stop=True)
                last.then_inc(s_PTp, 1)

            def a_state(i):
                pe.wait_ge(s_kbT, i + 1)
                pe.wait_ge(s_v, i + 1)
                for g in range(KK):
                    last = mm(bank[0][:, g * P:(g + 1) * P], kb01[:, g * P:(g + 1) * P], vs[:, g * P:(g + 1) * P],
                              start=True, stop=True)
                last.then_inc(s_Hvp, 1)

            def a_out(i):
                after(pe, s_x2T, i - 1)
                pe.wait_ge(s_PT, 2 * i + 2)
                pe.wait_ge(s_Hv, i + 1)
                for g in range(KK):
                    for hh in range(2):
                        m, m1 = slice(g * P, (g + 1) * P), slice(D + g * P, D + (g + 1) * P)
                        mm(wide(g, 0, hh), PT[:, hh, 2 * g * P:(2 * g + 1) * P], vs[:, m], start=True, stop=True, skip_group_check=True)
                        mm(wide(g, 1, hh), PT[:, hh, (2 * g + 1) * P:(2 * g + 2) * P], vs[:, m1],
                           start=True, stop=False, skip_group_check=True)
                        last = mm(wide(g, 1, hh), paT[:, g, 1, :], Hv[:, m], start=False, stop=True, skip_group_check=True)
                last.then_inc(s_Op, 1)

            def project(dst, srcT, w, done):
                for c in range(NC):
                    for m, (x_part, w_part, kk) in enumerate(three_passes(srcT, w)):
                        last = mm(dst[:, c * D:(c + 1) * D], x_part[:, kk, c * P:(c + 1) * P], w_part[:, kk, :],
                                  start=m == 0, stop=m == 3 * KK - 1)
                last.then_inc(done, 1)

            def a_onT(i):
                transposes(bank[2], on, s_on, 2 * i + 2, s_onTp, chunk_major=False)

            def a_project(i):
                pe.wait_ge(s_onT, i + 1)
                pe.wait_ge(s_pwl, 4)
                project(bank[3], onT, Wo2, s_Yp)

            def b_k(i):
                pe.wait_ge(s_cTl, i + 1)
                pe.wait_ge(s_v, rows(i + 2))
                project(bank[6], cT2, RK2, s_bkp)

            def b_x1T(i):
                pe.wait_ge(s_k, rows(i + 2))
                transposes(bank[5], x1.ap().rearrange("p c d -> p (c d)"), s_x1, NC * (i + 1), s_x1Tp)

            def b_qg(i):
                pe.wait_ge(s_x1T, i + 1)
                project(bank[5], x1T, RQ2, s_bqp)
                pe.wait_ge(s_kcs, i + 1)
                project(bank[6], x1T, GW2, s_bgp)

            def b_v(i, b=7):
                if b == 7:
                    after(pe, s_rnm, i)
                project(bank[b], cT2, RV2, s_bvp)

            def b_kxT(i):
                transposes(bank[1], kx, s_kx, i + 1, s_kxTp)

            def b_qxT(i):
                transposes(bank[5], qx, s_qx, i + 1, s_qxTp)

            def b_state(i):
                pe.wait_ge(s_vb, i + 1)
                after(pe, s_rnm, i)
                for g in range(KK):
                    last = mm(bank[7][:, g * P:(g + 1) * P], kx[:, g * P:(g + 1) * P], vb[:, g * P:(g + 1) * P],
                              start=True, stop=True)
                last.then_inc(s_Stp, 1)

            def b_scores(i, n):
                c, j = n // 4, n % 4
                r = slice(32 * j, 32 * j + 32)
                if n == 0:
                    pe.wait_ge(s_kxT, i + 1)
                    pe.wait_ge(s_qxP, i + 1)
                    after(pe, s_yB, min(i, B - 2) if isinstance(i, int) else i)
                    pe.wait_ge(s_gz, i + 1)
                if n == 1:
                    pe.wait_ge(s_qxT, i + 1)
                if n >= RS:
                    pe.wait_ge(s_Sb, NR * i + n - RS + 1)
                for g in range(KK):
                    last = mm(bank[4 + n % RS][:, g * T:(g + 1) * T], kxT[r, g, c, :], qxP[r, g, c, :, :], start=True, stop=True)
                last.then_inc(s_Sbp, 1)

            def b_sum(i, n):
                c, j = n // 4, n % 4
                pe.wait_ge(s_Sb, NR * i + n + 1)
                if n == 0:
                    pe.wait_ge(s_St, i + 1)
                    for g in range(KK):
                        mm(bank[7][:, D + g * P:D + (g + 1) * P], qxT[:, g, :], St[:, g, :], start=g == 0, stop=False,
                           skip_group_check=True)
                for g in range(KK):
                    for par in range(2):
                        h = 2 * j + par
                        last = mm(bank[7][:, c * D + g * P:c * D + (g + 1) * P],
                                  Sb[:, n % RS, (2 * g + par) * P:(2 * g + par + 1) * P],
                                  Vp[:, c * KK + g, h * P:(h + 1) * P], start=False, stop=True, skip_group_check=True)
                last.then_inc(s_ret, 1)

            def b_rgT(i, b=4):
                pe.wait_ge(s_q, rows(i + 3))
                transposes(bank[b], rg, s_rg, i + 1, s_rgTp)

            def b_project(i, b=4):
                pe.wait_ge(s_rgT, i + 1)
                project(bank[b], rgT, OW2, s_Y2p)

            def b_x2T(i, b=0):
                pe.wait_ge(s_Hv, rows(i + 3))
                transposes(bank[b], x2.ap().rearrange("p c d -> p (c d)"), s_x2, NC * (i + 1), s_x2Tp)

            def step(p, a, b, c, gates=False):
                if a is not None:
                    a_decay(a)
                    a_scores(a)
                if gates:
                    forget(2)
                if b is not None:
                    b_k(b)
                    b_x1T(b)
                if a is not None:
                    a_kbT(a)
                if gates:
                    forget(3)
                if a is not None:
                    a_logits(a)
                if gates:
                    forget(4)
                    forget(5)
                if b is not None:
                    b_kxT(b)
                late = a is None
                if b is not None:
                    b_qg(b)
                if c is not None and not late:
                    b_rgT(c)
                if b is not None:
                    b_v(b, 3 if late else 7)
                    b_qxT(b)
                if c is not None and late:
                    b_rgT(c, 2)
                if c is not None and not late:
                    b_project(c)
                if b is not None:
                    b_state(b)
                if a is not None:
                    a_state(a)
                if b is not None:
                    b_scores(b, 0)
                    b_scores(b, 1)
                if a is not None:
                    a_paT(a)
                if gates:
                    forget(6)
                if b is not None:
                    b_scores(b, 2)
                if c is not None and late:
                    b_project(c, 2)
                if b is not None:
                    b_sum(b, 0)
                    b_scores(b, 3)
                if a is not None:
                    a_weights(a)
                if c is not None and not late:
                    b_x2T(c)
                if gates:
                    forget(7)
                if b is not None:
                    b_sum(b, 1)
                    b_scores(b, 4)
                    b_sum(b, 2)
                if a is not None:
                    a_out(a)
                if b is not None:
                    b_scores(b, 5)
                if c is not None and late:
                    b_x2T(c)
                if b is not None:
                    b_sum(b, 3)
                    b_scores(b, 6)
                    b_sum(b, 4)
                    b_scores(b, 7)
                    b_sum(b, 5)
                if gates:
                    pe.wait_ge(s_mz, B)
                    pe.wait_ge(s_az, B)
                if p is not None:
                    p_v(p)
                if a is not None:
                    a_onT(a)
                if b is not None:
                    b_sum(b, 6)
                if p is not None:
                    p_qk(p, 4, Wq2, s_qp, 7)
                if a is not None:
                    a_project(a)
                if p is not None:
                    p_qk(p, 5, Wk2, s_kp, 8)
                if b is not None:
                    b_sum(b, 7)

            pe.wait_ge(s_pwl, 1)
            step(0, None, None, None)
            pe.wait_ge(s_w_a, 5 * 16)
            pe.wait_ge(s_dw, 1)
            step(1, 0, None, None, gates=True)
            pe.wait_ge(s_pwl, 9)
            step(2, 1, 0, None)
            with pe.Fori(3, B) as i:
                step(i, i - 1, i - 2, i - 3)
            step(None, B - 1, B - 2, B - 3)
            step(None, None, B - 1, B - 2)

            xh, xl = (x.rearrange("p (n r) x -> p n r x", r=2) for x in (x2Th, x2Tl))

            def ffn_up(n, f):
                passes = [(w, x, kk) for kk in range(KK) for w, x in ((W1h, xh), (W1h, xl), (W1l, xh))]
                for m, (w, x, kk) in enumerate(passes):
                    last = mm(bank[f % HR].ap().rearrange("p (r t) -> p r t", r=2), w[:, kk, f * P:(f + 1) * P],
                              x[:, n, :, kk * T:(kk + 1) * T],
                              start=m == 0, stop=m == len(passes) - 1)
                last.then_inc(s_hp, 1)

            def ffn_down(n, f):
                pe.wait_ge(s_hl, NF * n + f + 1)
                if f == 0:
                    after(pe, s_yF, 4 * n)
                for t in range(4):
                    for m, (h, w) in enumerate(((hidh, W2h), (hidh, W2l), (hidl, W2h))):
                        last = mm(bank[4 + t // 2][:, (t % 2) * D:(t % 2 + 1) * D], h[:, f % HR, t * P:(t + 1) * P], w[:, f, :],
                                  start=f == 0 and t % 2 == 0 and m == 0, stop=f == NF - 1 and m == 2, skip_group_check=True)
                last.then_inc(s_hused, 1)

            def ffn(n, last_row=None):
                pe.wait_ge(s_xl, 2 * n + 2)
                for f in range(3):
                    ffn_up(n, f)
                for f in range(NF):
                    if f + 3 < NF:
                        if f + 3 >= 4:
                            pe.wait_ge(s_h, NF * n + f)
                        ffn_up(n, f + 3)
                    ffn_down(n, f)
                    if last_row is not None and f == 2:
                        b_rgT(last_row, 6)
                    if last_row is not None and f == 4:
                        b_project(last_row, 6)
                    if last_row is not None and f == 7:
                        b_x2T(last_row, 7)

            pe.wait_ge(s_wl, 2)
            pe.wait_ge(s_x2T, B - 1)
            ffn(0, last_row=B - 1)
            with pe.Fori(1, NT) as n:
                ffn(n)

        @block.scalar
        def _(act):
            activation = nc.scalar.activation

            def split_upper(dst, src, done):
                activation(dst, src, ACT.Copy).then_inc(done, 1)

            def forget(n):
                act.wait_ge(s_zp, n + 1)
                if n >= 2:
                    act.wait_ge(s_e, n - 1)
                activation(az[n % 2], logit_bank(n)[:], ACT.Abs).then_inc(s_az, 1)
                act.wait_ge(s_az, n + 1)
                activation(e_all[:, n, :], az[n % 2], ACT.Exp, scale=-1.0).then_inc(s_e, 1)

            def forget_ln(n0, n1):
                act.wait_ge(s_e, n1)
                activation(e_all[:, n0:n1, :], e_all[:, n0:n1, :], ACT.Ln, bias=1.0).then_inc(s_ln, n1 - n0)

            forget(0)
            act.wait_ge(s_xTp, 16)
            split_upper(xTp2[0][:], xTp[:], s_xph)
            act.wait_ge(s_w_v, 16)
            split_upper(Wv2[0][:], Wv, s_pwh)
            forget(1)
            act.wait_ge(s_w_qk, 2 * 16)
            for w2, w in ((Wq2, Wq), (Wk2, Wk)):
                split_upper(w2[0][:], w, s_pwh)
            forget_ln(0, 1)
            forget_ln(1, 2)

            def split_c(i):
                act.wait_ge(s_cT, 16 * (i + 1))
                split_upper(cT2[0][:], cT[:], s_cTh)

            def p_split(i):
                act.wait_ge(s_xTp, 16 * (i + 1))
                split_upper(xTp2[0][:], xTp[:], s_xph)

            def p_v(i):
                act.wait_ge(s_vp, i + 1)
                after(act, s_Op, i)
                activation(vs[:], bank[6][:], ACT.Copy).then_inc(s_v, 1)

            def p_tanh(i, b, ready, done, used_by, count):
                act.wait_ge(ready, i + 1)
                after(act, used_by, count)
                activation(th[:], bank[b][:], ACT.Tanh, scale=0.5).then_inc(done, 1)

            def f_split(i):
                act.wait_ge(s_f, i + 1)
                after(act, s_E01p, i)
                split_upper(fh[:], f_all[:, i, :], s_fh)

            def a_gates(i):
                activation(ex[:], f_all[:, i, :], ACT.Exp, scale=0.125).then_inc(s_ex, 1)

            def a_gains(i):
                act.wait_ge(s_Ep, i + 1)
                activation(ek[:], bank[0][:], ACT.Exp, scale=-1.0).then_inc(s_ek, 1)
                after(act, s_pa, i)
                activation(eq.rearrange("p (g c x) -> p c g x", g=KK, c=NC),
                           bank[0].ap().rearrange("p (c g x) -> p c g x", g=KK, c=NC), ACT.Exp).then_inc(s_eq, 1)
                act.wait_ge(s_E01p, i + 1)
                activation(ex01[:], bank[1][:, 0:D], ACT.Exp).then_inc(s_ex01, 1)

            def a_kbT(i):
                act.wait_ge(s_kbTp, i + 1)
                after(act, s_PTp, i)
                activation(kbT.rearrange("p g c t -> p (g c t)"), bank[0][:], ACT.Copy).then_inc(s_kbT, 1)

            def a_exp(i):
                act.wait_ge(s_lc, i + 1)
                after(act, s_onTp, i)
                activation(pe_x[:], lg[:], ACT.Exp, scale=1.0 / 32.0).then_inc(s_pe, 1)

            def a_state(i):
                act.wait_ge(s_Hvp, i + 1)
                after(act, s_Op, i)
                for hh in range(2):
                    r = slice(64 * hh, 64 * hh + 64)
                    last = activation(Hv[r, :].rearrange("p (g m) -> p g m", g=KK)[:, :, 64 * hh:64 * hh + 64],
                                      bank[0][r, 0:D].rearrange("p (g m) -> p g m", g=KK)[:, :, 64 * hh:64 * hh + 64], ACT.Copy)
                last.then_inc(s_Hv, 1)

            def a_paT(i):
                act.wait_ge(s_paTp, i + 1)
                activation(paT.rearrange("p g c t -> p (g c t)"), bank[1][:], ACT.Copy).then_inc(s_paT, 1)

            def a_square(i):
                act.wait_ge(s_Op, i + 1)
                after(act, s_ms, i)
                for g in range(KK):
                    activation(packed(osq[:, g * D:(g + 1) * D]), used(g), ACT.Square).then_inc(s_osq, 1)

            def a_onT(i):
                act.wait_ge(s_onTp, i + 1)
                after(act, s_Yp, i)
                split_upper(onT[0].ap().rearrange("p k t -> p (k t)"), bank[2][:], s_onTh)

            def b_x1T(i):
                act.wait_ge(s_x1Tp, i + 1)
                after(act, s_bgp, i)
                split_upper(x1T[0].ap().rearrange("p k t -> p (k t)"), bank[5][:], s_x1Th)

            def b_v(i, b=7):
                act.wait_ge(s_bvp, i + 1)
                after(act, s_ret, NR * i)
                activation(vb[:], bank[b][:, 0:D], ACT.Copy)
                activation(Vp.rearrange("p a (h w) -> p a h w", w=P + EB)[:, :, :, 0:EB],
                           bank[b].ap().rearrange("p (a h e) -> p a h e", a=NC * KK, e=EB), ACT.Copy).then_inc(s_vb, 1)

            def b_gate(i):
                act.wait_ge(s_gz, i + 1)
                after(act, s_rg, i)
                activation(gt[:], gz[:], ACT.Tanh, scale=0.5).then_inc(s_gt, 1)

            def b_kxT(i):
                act.wait_ge(s_kxTp, i + 1)
                activation(kxT.rearrange("p g c t -> p (g c t)"), bank[1][:], ACT.Copy).then_inc(s_kxT, 1)

            def b_qxT(i):
                act.wait_ge(s_qxTp, i + 1)
                qp = bank[5].ap().rearrange("p (g c t) -> p (g c) t", g=KK, c=NC)
                for par in range(2):
                    last = activation(qxP[:, :, :, par, :].rearrange("p g c t -> p (g c) t"), qp, ACT.Copy,
                                      scale=Parity[:, par:par + 1])
                last.then_inc(s_qxP, 1)
                activation(qxT[:], bank[5].ap().rearrange("p (g c t) -> p g c t", g=KK, c=NC)[:, :, 1, :],
                           ACT.Copy).then_inc(s_qxT, 1)

            def b_square(i):
                act.wait_ge(s_ret, NR * (i + 1))
                act.wait_ge(s_gate, i + 1)
                activation(rsq[:], bank[7][:], ACT.Square).then_inc(s_rsq, 1)

            def b_rgT(i, b=4):
                act.wait_ge(s_rgTp, i + 1)
                after(act, s_Y2p, i)
                split_upper(rgT[0].ap().rearrange("p k t -> p (k t)"), bank[b][:], s_rgTh)

            def b_x2T(i, b=0):
                act.wait_ge(s_x2Tp, i + 1)
                activation(x2T_all[:, i, :], bank[b][:], ACT.Copy).then_inc(s_x2T, 1)

            def split_weights():
                act.wait_ge(s_wo, 1)
                act.wait_ge(s_w_b, 10 * 16)
                act.wait_ge(s_rv, 1)
                for w2, w in ((Wo2, Wo), (RK2, RK), (RQ2, RQ), (GW2, GW), (RV2, RV), (OW2, OW)):
                    split_upper(w2[0][:], w[:], s_pwh)

            def split_x2(n):
                for r in range(2):
                    act.wait_ge(s_x2T, 2 * n + r + 1)
                    split_upper(x2Th[:, 2 * n + r, :], x2T_all[:, 2 * n + r, :], s_xh)

            def split_ffn_weights():
                act.wait_ge(s_w_f, 4 * 16)
                act.wait_ge(s_Yp, B)
                split_upper(W1h[:], W1[:], s_wh)
                split_upper(W2h[:], W2[:], s_wh)

            def step(p, a, b, c, setup=False, ffn_weights=False):
                if a is not None:
                    a_gains(a)
                if setup:
                    forget(2)
                if b is not None:
                    b_x1T(b)
                if a is not None:
                    a_kbT(a)
                if setup:
                    forget(3)
                if b is not None:
                    b_kxT(b)
                late = a is None
                if ffn_weights:
                    split_ffn_weights()
                if c is not None and not late:
                    b_rgT(c)
                if a is not None:
                    a_exp(a)
                if setup:
                    forget(4)
                    forget(5)
                if b is not None:
                    b_v(b, 3 if late else 7)
                    b_qxT(b)
                    b_gate(b)
                if c is not None and late:
                    b_rgT(c, 2)
                if a is not None:
                    a_state(a)
                    a_paT(a)
                if setup:
                    forget(6)
                    forget(7)
                if ffn_weights:
                    act.wait_ge(s_qcs, B)
                    split_x2(0)
                if c is not None:
                    b_x2T(c)
                if p is not None:
                    p_split(p)
                if setup:
                    a_square(a)
                if a is not None:
                    split_c(a)
                if p is not None and a is not None:
                    f_split(p)
                if p is not None and a is not None and not setup:
                    a_gates(p)
                if a is not None and not setup:
                    a_square(a)
                if p is not None:
                    p_v(p)
                if setup:
                    split_weights()
                if a is not None:
                    a_onT(a)
                if setup:
                    forget_ln(2, B)
                    a_gates(p)
                if p is not None:
                    p_tanh(p, 4, s_qp, s_thq, s_k, p)
                    p_tanh(p, 5, s_kp, s_thk, s_q, p + 1)
                if b is not None:
                    b_square(b)

            act.wait_ge(s_half, 1)
            act.wait_ge(s_Vp0, 1)
            p_v(0)
            act.wait_ge(s_w_a, 5 * 16)
            activation(DecayWr[:], DecayW[:], ACT.Copy).then_inc(s_dw, 1)
            f_split(0)
            p_tanh(0, 4, s_qp, s_thq, s_k, 0)
            a_gates(0)
            p_tanh(0, 5, s_kp, s_thk, s_q, 1)
            step(1, 0, None, None, setup=True)
            step(2, 1, 0, None)
            with act.Fori(3, B) as i:
                step(i, i - 1, i - 2, i - 3)
            step(None, B - 1, B - 2, B - 3)
            step(None, None, B - 1, B - 2, ffn_weights=True)

            def ffn(n, last_row=None):
                for f in range(NF):
                    if last_row is not None and f == 6:
                        b_rgT(last_row, 6)
                    if f == 5 and not (isinstance(n, int) and n == NT - 1):
                        split_x2(n + 1)
                    act.wait_ge(s_hp, NF * n + f + 1)
                    after(act, s_hl, NF * n + f + 1 - HR)
                    activation(hid[:, f % HR, :], bank[f % HR][:], ACT.Gelu, bias=B1[:, f:f + 1]).then_inc(s_h, 1)
                    act.wait_ge(s_h, NF * n + f + 1)
                    after(act, s_hused, NF * n + f + 1 - HR)
                    activation(hidh[:, f % HR, :], hid[:, f % HR, :], ACT.Copy).then_inc(s_hh, 1)

                if last_row is not None:
                    b_x2T(last_row, 7)

            act.wait_ge(s_ret, NR * B)
            ffn(0, last_row=B - 1)
            with act.Fori(1, NT - 1) as n:
                ffn(n)
            ffn(NT - 1)

        @block.vector
        def _(dve):
            v = nc.vector

            def split_lower(dst, src, upper, ready, count, done):
                dve.wait_ge(ready, count)
                v.tensor_tensor(dst, src, upper.bitcast(F32), ALU.subtract).then_inc(done, 1)

            def split_bank(parts, b, ready, i, done):
                split_lower(parts[1].ap().rearrange("p k t -> p (k t)"), bank[b][:],
                            parts[0].ap().rearrange("p k t -> p (k t)"), ready, i + 1, done)

            def forget(n):
                dve.wait_ge(s_az, n + 1)
                v.tensor_scalar(f_all[:, n, :], logit_bank(n)[:], 0.0, None, ALU.min).then_inc(s_mz, 1)

            def p_swish(i, b, ready, dst, done):
                dve.wait_ge(ready, i + 1)
                after(dve, s_Sp, 2 * i)
                v.scalar_tensor_tensor(dst[:], th[:], 1.0, bank[b][:], ALU.add, ALU.mult).then_inc(done, 1)

            for tile, value in ((Hv, 0.0), (Half, -0.5), (One, 1.0), (Eps, EPS), (EpsA, MA * EPS), (EpsB, EB * EPS)):
                dve.memset(tile[:], value).then_inc(s_half, 1)
            forget(0)
            split_lower(Wv2[1][:], Wv, Wv2[0][:], s_pwh, 1, s_pwl)
            forget(1)
            for n, (w2, w) in enumerate(((Wq2, Wq), (Wk2, Wk))):
                split_lower(w2[1][:], w, w2[0][:], s_pwh, n + 2, s_pwl)
            dve.wait_ge(s_mz, 2)
            for n in range(2):
                dve.wait_ge(s_ln, n + 1)
                v.tensor_tensor(f_all[:, n, :], f_all[:, n, :], e_all[:, n, :], ALU.subtract).then_inc(s_f, 1)

            def layer_norm_stats(i, y, bn, mv, s_y, s_bn, s_mv, tiles, counts=1):
                dve.wait_ge(s_y, counts * (i + 1))
                for c in range(tiles):
                    v.bn_stats(bn[:, c, :], y[:, c, :]).then_inc(s_bn, 1)
                for c in range(tiles):
                    dve.wait_ge(s_bn, tiles * i + c + 1)
                    dve.nop(nofuse=True)
                    v.bn_aggr(mv[:, c, :], bn[:, c, :]).then_inc(s_mv, 1)

            def layer_norm_apply(i, y, mv, rs, s_rs, tiles, dst, s_dst):
                dve.wait_ge(s_rs, i + 1)
                for c in range(tiles):
                    v.tensor_scalar(dst[:, c, :], y[:, c, :], mv[:, c, 0:1], rs[:, c:c + 1], ALU.subtract, ALU.mult)\
                        .then_inc(s_dst, 1)

            def a_keys(i):
                dve.wait_ge(s_ex, i + 1)
                v.tensor_scalar(ex[:], ex[:], -1.0, 1.0, ALU.mult, ALU.add).then_inc(s_sg, 1)
                dve.wait_ge(s_ek, i + 1)
                dve.wait_ge(s_sg, i + 1)
                after(dve, s_Lp, i)
                v.scalar_tensor_tensor(kb[:], ek[:], BIG, ex[:], ALU.min, ALU.mult).then_inc(s_kb, 1)

            def a_keys_next(i):
                dve.wait_ge(s_ex01, i + 1)
                after(dve, s_Hvp, i)
                v.tensor_tensor(kb01[:], ex01[:], ex[:, 0:D], ALU.mult).then_inc(s_kb01, 1)

            def a_mask(i):
                after(dve, s_Op, i)
                for n, b in enumerate((2, 3)):
                    dve.wait_ge(s_Sp, 2 * i + 1)
                    v.tensor_tensor(quarters(Sm[:, n, :], 2), quarters(bank[b][:], 2), mask_two, ALU.mult).then_inc(s_Sm, 1)
                for hh in range(2):
                    dve.wait_ge(s_Sp, 2 * i + 2)
                    v.tensor_tensor(quarters(Sm[:, 2, hh * T:(hh + 1) * T], 2), quarters(bank[hh][:, 0:T], 2), causal_two,
                                    ALU.mult).then_inc(s_Sm, 1)

            def a_softmax(i):
                dve.wait_ge(s_Lp, i + 1)
                dve.wait_ge(s_eq, i + 1)
                for g in range(KK):
                    v.scalar_tensor_tensor(packed(lg[:, g * D:(g + 1) * D]), packed(eq[:, g * D:(g + 1) * D]), BIG, used(2 + g),
                                           ALU.min, ALU.mult).then_inc(s_lg, 1)
                dve.wait_ge(s_lg, 2 * i + 2)
                v.tensor_reduce(mx[:], heads(lg[:], HA), AX.X, ALU.max).then_inc(s_mx, 1)
                dve.wait_ge(s_mx, i + 1)
                v.tensor_tensor(heads(lg[:], HA), heads(lg[:], HA), per_head(mx[:], HA, MA), ALU.subtract).then_inc(s_lc, 1)

            def a_sum(i):
                dve.wait_ge(s_pe, i + 1)
                after(dve, s_zz, i)
                v.tensor_reduce(Zs[:], heads(pe_x[:], HA), AX.X, ALU.add).then_inc(s_Z, 1)
                dve.wait_ge(s_Z, i + 1)
                v.scalar_tensor_tensor(pa[:], eq[:], BIG, pe_x[:], ALU.min, ALU.mult).then_inc(s_pa, 1)

            def a_weights(i):
                for hh in range(2):
                    dve.wait_ge(s_PTp, i + 1)
                    v.tensor_tensor(quarters(PT[:, hh, :], 4), quarters(bank[2 + hh][:], 4), causal_four, ALU.mult).then_inc(s_PT, 1)

            def a_norm(i):
                dve.wait_ge(s_osq, 2 * i + 2)
                after(dve, s_rn0, i)
                v.tensor_reduce(ms[:], heads(osq[:], HA), AX.X, ALU.add).then_inc(s_ms, 1)

            def a_normed(i):
                dve.wait_ge(s_rn, i + 1)
                dve.wait_ge(s_paTp, i + 1)
                for g in range(KK):
                    v.tensor_tensor(packed(on[:, g * D:(g + 1) * D]), used(g),
                                    rn[:, 4 * g:4 * g + 4].unsqueeze(2).to_broadcast([P, 4, MA]), ALU.mult).then_inc(s_on, 1)

            def a_residual(i):
                dve.wait_ge(s_Yp, i + 1)
                dve.wait_ge(s_xres, 16 * (i + 1))
                v.tensor_tensor(yA.ap().rearrange("p c d -> p (c d)"), xres.ap().rearrange("p c d -> p (c d)"), bank[3][:],
                                ALU.add).then_inc(s_yA, 1)
                layer_norm_stats(i, yA, bnA, mvA, s_yA, s_bnA, s_mvA, NC)

            def a_x1(i):
                after(dve, s_x1b, i)
                layer_norm_apply(i, yA, mvA, rsA, s_rsA, NC, x1, s_x1)

            def b_rope(i, src, s_ready, c_out, s_out, kind, s_done, *s_used):
                dve.wait_ge(s_ready, i + 1)
                for s in s_used:
                    after(dve, s, i)
                v.tensor_tensor(c_out, bank[src][:], Rope[:, 2 * kind].rearrange("p c d -> p (c d)"), ALU.mult)
                v.tensor_tensor(s_out.rearrange("p (n two) -> p n two", two=2), swapped(bank[src][:]),
                                Rope[:, 2 * kind + 1].rearrange("p c (n two) -> p (c n) two", two=2), ALU.mult)\
                    .then_inc(s_done, 1)

            def b_rope_sum(i, ready, dst, c_part, s_part, done):
                dve.wait_ge(ready, i + 1)
                v.tensor_tensor(dst, c_part, s_part, ALU.add).then_inc(done, 1)

            def b_gate(i):
                dve.wait_ge(s_bgp, i + 1)
                v.tensor_tensor(halves(gz[:]), halves(bank[6][:]), both_chunks(GB[:]), ALU.add).then_inc(s_gz, 1)

            def b_gate2(i):
                dve.wait_ge(s_gt, i + 1)
                v.scalar_tensor_tensor(gate[:], gt[:], 1.0, gz[:], ALU.add, ALU.mult).then_inc(s_gate, 1)

            def b_state(i):
                dve.wait_ge(s_Stp, i + 1)
                v.tensor_tensor(St.ap().rearrange("p g d -> p (g d)"), bank[7][:, 0:D],
                                StateMask.ap().rearrange("p g d -> p (g d)"), ALU.mult).then_inc(s_St, 1)

            def b_mask(i, n):
                dve.wait_ge(s_Sbp, NR * i + n + 1)
                if n >= RS:
                    dve.wait_ge(s_ret, NR * i + n - RS + 1)
                v.tensor_tensor(quarters(Sb[:, n % RS, :], 4), quarters(bank[4 + n % RS][:], 4), causal_four, ALU.mult).then_inc(s_Sb, 1)

            def b_norm(i):
                dve.wait_ge(s_rsq, i + 1)
                after(dve, s_rr0, i)
                v.tensor_reduce(rvar[:], heads(rsq[:], HB), AX.X, ALU.add).then_inc(s_rvar, 1)

            def b_normed(i):
                dve.wait_ge(s_rr, i + 1)
                after(dve, s_rgTp, i)
                v.tensor_tensor(heads(rnm[:], HB), heads(bank[7][:], HB), per_head(rr[:], HB, EB), ALU.mult).then_inc(s_rnm, 1)

            def b_residual(i, b=4):
                dve.wait_ge(s_Y2p, i + 1)
                dve.wait_ge(s_x1b, i + 1)
                v.tensor_tensor(yB.ap().rearrange("p c d -> p (c d)"), x1b.ap().rearrange("p c d -> p (c d)"), bank[b][:],
                                ALU.add).then_inc(s_yB, 1)
                layer_norm_stats(i, yB, bnB, mvB, s_yB, s_bnB, s_mvB, NC)

            def b_x2(i):
                after(dve, s_x2k, i)
                after(dve, s_x2Tp, i)
                layer_norm_apply(i, yB, mvB, rsB, s_rsB, NC, x2, s_x2)

            def scale_weights():
                dve.wait_ge(s_w_a, 5 * 16)
                v.tensor_scalar(Wo[:], Wo[:], Gcol[:, 0:1], MA ** 0.5, ALU.mult, ALU.mult).then_inc(s_wo, 1)
                dve.wait_ge(s_w_b, 10 * 16)
                v.tensor_scalar(OW[:], OW[:], 0.5 * EB ** 0.5, None, ALU.mult)
                rv_heads = RV.ap().rearrange("p k (h e) -> p (k h) e", e=EB)
                v.tensor_reduce(RVmean[:], rv_heads, AX.X, ALU.add).then_inc(s_rvm, 1)
                dve.wait_ge(s_rvm, 1)
                v.tensor_scalar(RVmean[:], RVmean[:], 1.0 / EB, None, ALU.mult).then_inc(s_rvm, 1)
                dve.wait_ge(s_rvm, 2)
                v.tensor_tensor(rv_heads, rv_heads, RVmean.ap().unsqueeze(2).to_broadcast([P, KK * HB, EB]), ALU.subtract)\
                    .then_inc(s_rv, 1)

            def split_weights():
                for n, (w2, w) in enumerate(((Wo2, Wo), (RK2, RK), (RQ2, RQ), (GW2, GW), (RV2, RV), (OW2, OW))):
                    split_lower(w2[1][:], w[:], w2[0][:], s_pwh, n + 4, s_pwl)

            def split_x2(n):
                for r in range(2):
                    split_lower(x2Tl[:, 2 * n + r, :], x2T_all[:, 2 * n + r, :], x2Th[:, 2 * n + r, :],
                                s_xh, 2 * n + r + 1, s_xl)

            def step(p, a, b, c, setup=False, ffn_weights=False):
                if a is not None:
                    a_keys(a)
                    a_mask(a)
                    a_keys_next(a)
                if setup:
                    forget(2)
                    forget(3)
                late = a is None
                if b is not None:
                    b_rope(b, 6, s_bkp, kc, ks, 1, s_kcs, s_kxTp, s_Stp)
                    b_rope_sum(b, s_kcs, kx, kc, ks, s_kx)
                    split_bank(x1T, 5, s_x1Th, b, s_x1T)
                if c is not None and not late:
                    b_normed(c)
                if a is not None:
                    a_softmax(a)
                if setup:
                    forget(4)
                if b is not None:
                    b_rope(b, 5, s_bqp, qc, qs, 0, s_qcs, s_qxTp)
                    b_rope_sum(b, s_qcs, qx, qc, qs, s_qx)
                if c is not None and not late:
                    split_bank(rgT, 4, s_rgTh, c, s_rgT)
                if b is not None:
                    b_gate(b)
                if c is not None and late:
                    b_normed(c)
                    split_bank(rgT, 2, s_rgTh, c, s_rgT)
                if a is not None:
                    a_sum(a)
                if c is not None and not late:
                    b_residual(c)
                if setup:
                    forget(5)
                    scale_weights()
                if b is not None:
                    b_state(b)
                    for n in range(3):
                        b_mask(b, n)
                if c is not None and late:
                    b_residual(c, 2)
                if c is not None and not late:
                    b_x2(c)
                if b is not None:
                    b_mask(b, 3)
                if c is not None and late:
                    b_x2(c)
                if a is not None:
                    a_weights(a)
                if setup:
                    forget(6)
                    forget(7)
                if b is not None:
                    b_gate2(b)
                if ffn_weights:
                    split_x2(0)
                if b is not None:
                    b_mask(b, 4)
                    b_mask(b, 5)
                if a is not None:
                    a_norm(a)
                if b is not None:
                    b_mask(b, 6)
                if a is not None:
                    a_normed(a)
                if b is not None:
                    b_mask(b, 7)
                if a is not None:
                    split_bank(onT, 2, s_onTh, a, s_onT)
                if setup:
                    split_weights()
                if p is not None:
                    p_swish(p, 4, s_thq, qTs, s_q)
                if a is not None:
                    a_residual(a)
                if p is not None:
                    p_swish(p, 5, s_thk, kTs, s_k)
                if b is not None:
                    b_norm(b)
                if a is not None:
                    a_x1(a)

            step(0, None, None, None)
            step(1, 0, None, None, setup=True)
            dve.wait_ge(s_e, B)
            step(2, 1, 0, None)
            with dve.Fori(3, B) as i:
                step(i, i - 1, i - 2, i - 3)
            step(None, B - 1, B - 2, B - 3)
            step(None, None, B - 1, B - 2, ffn_weights=True)

            def ffn(n, last_row=None):
                first, last = (isinstance(n, int) and n == m for m in (0, NT - 1))
                for f in range(NF):
                    if f == 2 and not first:
                        layer_norm_stats(n - 1, yF, bnF, mvF, s_yF, s_bnF, s_mvF, 4, counts=4)
                    if f == 4 and not first:
                        layer_norm_apply(n - 1, yF, mvF, rsF, s_rsF, 4, xo, s_xo)
                    if f == 2 and last_row is not None:
                        b_normed(last_row)
                    if f == 6 and last_row is not None:
                        split_bank(rgT, 6, s_rgTh, last_row, s_rgT)
                    if f == 6 and not last:
                        split_x2(n + 1)
                    after(dve, s_hused, NF * n + f + 1 - HR)
                    split_lower(hidl[:, f % HR, :], hid[:, f % HR, :], hidh[:, f % HR, :], s_hh, NF * n + f + 1, s_hl)
                if last_row is not None:
                    b_residual(last_row, 6)
                    b_x2(last_row)
                dve.wait_ge(s_x2b, n + 1)
                after(dve, s_out, 16 * n)
                after(dve, s_xo, 4 * n)
                dve.wait_ge(s_hused, NF * (n + 1))
                for t in range(4):
                    v.tensor_tensor(yF[:, t, :], x2b[:, t, :], bank[4 + t // 2][:, (t % 2) * D:(t % 2 + 1) * D], ALU.add)\
                        .then_inc(s_yF, 1)

            ffn(0, last_row=B - 1)
            with dve.Fori(1, NT - 1) as n:
                ffn(n)
            ffn(NT - 1)
            layer_norm_stats(NT - 1, yF, bnF, mvF, s_yF, s_bnF, s_mvF, 4, counts=4)
            layer_norm_apply(NT - 1, yF, mvF, rsF, s_rsF, 4, xo, s_xo)

        @block.gpsimd
        def _(pool):
            g = nc.gpsimd

            def rstd(dst, var, eps, n, s_mid, s_done, i):
                g.tensor_tensor(dst, var, eps[:].to_broadcast([P, n]), ALU.add).then_inc(s_mid, 1)
                pool.wait_ge(s_mid, i + 1)
                g.tensor_tensor(dst, dst, Half[:, 0:n], ALU.pow).then_inc(s_done, 1)

            def split_lower(dst, src, upper, ready, count, done):
                pool.wait_ge(ready, count)
                g.tensor_tensor(dst[:], src[:], upper[:].bitcast(F32), ALU.subtract).then_inc(done, 1)

            def a_decayed(i):
                pool.wait_ge(s_Z, i + 1)
                g.tensor_tensor(zz[:], Zs[:], Zs[:], ALU.mult).then_inc(s_zz, 1)

            def a_norm(i):
                pool.wait_ge(s_zz, i + 1)
                g.tensor_tensor(zz[:], zz[:], EpsA[:].to_broadcast([P, NC * HA]), ALU.mult).then_inc(s_zz2, 1)
                pool.wait_ge(s_ms, i + 1)
                pool.wait_ge(s_zz2, i + 1)
                g.tensor_tensor(zz[:], ms[:], zz[:], ALU.add).then_inc(s_rn0, 1)
                pool.wait_ge(s_rn0, i + 1)
                after(pool, s_on, i)
                g.tensor_tensor(rn[:], zz[:], Half[:, 0:NC * HA], ALU.pow).then_inc(s_rn, 1)

            def a_rstd(i):
                pool.wait_ge(s_mvA, NC * (i + 1))
                after(pool, s_x1, NC * i)
                rstd(rsA[:], mvA[:, :, 1], Eps, NC, s_va, s_rsA, i)

            def b_bias(i):
                pool.wait_ge(s_x1, NC * (i + 1))
                after(pool, s_x2, NC * i)
                g.tensor_tensor(x1b[:], x1[:], both_chunks(OB[:]), ALU.add).then_inc(s_x1b, 1)

            def b_norm(i):
                pool.wait_ge(s_rvar, i + 1)
                after(pool, s_rnm, i)
                rstd(rr[:], rvar[:], EpsB, NC * HB, s_rr0, s_rr, i)

            def b_gated(i):
                pool.wait_ge(s_rnm, i + 1)
                g.tensor_tensor(rg[:], rnm[:], gate[:], ALU.mult).then_inc(s_rg, 1)

            def b_rstd(i):
                pool.wait_ge(s_mvB, NC * (i + 1))
                after(pool, s_x2, NC * i)
                rstd(rsB[:], mvB[:, :, 1], Eps, NC, s_vb2, s_rsB, i)
                pool.wait_ge(s_x2, NC * (i + 1))
                g.tensor_copy(x2_all[:, i, :], x2.ap().rearrange("p c d -> p (c d)")).then_inc(s_x2k, 1)

            def f_split(i):
                pool.wait_ge(s_fh, i + 1)
                g.tensor_tensor(fl[:], f_all[:, i, :], fh[:].bitcast(F32), ALU.subtract).then_inc(s_fl, 1)

            def step(p, a, b, c, setup=False, ffn_weights=False):
                if c is not None:
                    b_gated(c)
                if ffn_weights:
                    split_lower(W1l, W1, W1h, s_wh, 1, s_wl)
                    split_lower(W2l, W2, W2h, s_wh, 2, s_wl)
                if c is not None:
                    b_rstd(c)
                if b is not None:
                    b_bias(b)
                if p is not None:
                    split_lower(xTp2[1], xTp, xTp2[0], s_xph, p + 1, s_xpl)
                if setup:
                    a_decayed(a)
                    a_norm(a)
                if a is not None:
                    split_lower(cT2[1], cT, cT2[0], s_cTh, a + 1, s_cTl)
                if p is not None:
                    f_split(p)
                if a is not None and not setup:
                    a_decayed(a)
                    a_norm(a)
                if a is not None:
                    a_rstd(a)
                if b is not None:
                    b_norm(b)

            g.memset(Vp[:], 0.0).then_inc(s_Vp0, 1)
            pool.wait_ge(s_half, 6)
            step(0, None, None, None)
            step(1, 0, None, None, setup=True)
            pool.wait_ge(s_mz, B)
            pool.wait_ge(s_ln, B)
            g.tensor_tensor(f_all[:, 2:B, :], f_all[:, 2:B, :], e_all[:, 2:B, :], ALU.subtract).then_inc(s_f, B - 2)
            pool.wait_ge(s_w_b, 10 * 16)
            step(2, 1, 0, None)
            with pool.Fori(3, B) as i:
                step(i, i - 1, i - 2, i - 3)
            step(None, B - 1, B - 2, B - 3)
            step(None, None, B - 1, B - 2, ffn_weights=True)

            def ffn(n):
                pool.wait_ge(s_x2k, 2 * n + 2)
                after(pool, s_yF, 4 * n)
                for r in range(2):
                    last = g.tensor_tensor(x2b[:, 2 * r:2 * r + 2, :], halves(x2_all[:, 2 * n + r, :]), both_chunks(B2[:]), ALU.add)
                last.then_inc(s_x2b, 1)

            def ffn_rstd(n):
                pool.wait_ge(s_mvF, 4 * (n + 1))
                rstd(rsF[:], mvF[:, :, 1], Eps, 4, s_vf, s_rsF, n)

            pool.wait_ge(s_ret, NR * B)
            ffn(0)
            b_gated(B - 1)
            b_rstd(B - 1)
            with pool.Fori(1, NT) as n:
                ffn(n)
                ffn_rstd(n - 1)
            ffn_rstd(NT - 1)


def shape_constants():
    s = np.arange(P)
    causal = (s[:, None] <= s[None, :]).astype(np.float32)
    mask = np.stack([causal, np.ones((P, P), np.float32)], axis=1)
    mid = P // 2 - 1
    src, tok = s[:, None], s[None, :]
    own = ((src > mid) & (src <= tok)).astype(np.float32) - ((src <= mid) & (src > tok)).astype(np.float32)
    later = (src > tok).astype(np.float32)
    nxt = (src <= mid).astype(np.float32) * np.ones((P, P), np.float32)
    decay_w = np.stack([own, later, nxt], axis=1) / np.float32(8.0)
    f32 = np.float32
    base = (np.arange(0, EB, 2, dtype=f32) + f32(0.4 * EB)) / f32(1.4 * EB)
    power = (np.arange(-(T // 2), T - T // 2, dtype=f32) / f32(512.0))[:, None]
    scale = np.power(base[None, :], power, dtype=f32)
    inv_freq = (f32(1.0) / np.power(f32(10000.0), np.arange(EB // 2, dtype=f32) / f32(EB // 2), dtype=f32)).astype(f32)
    ang = np.arange(T, dtype=f32)[:, None] * inv_freq[None, :]
    gam = f32(1.0) - np.exp(np.linspace(np.log(1 / 32.0), np.log(1 / 512.0), HB)).astype(f32)
    rel = np.arange(T) % P - P // 2
    tables = []
    for sc, sign in ((scale.astype(np.float64), 1.0), (1.0 / scale.astype(np.float64), -1.0)):
        dec = gam.astype(np.float64)[None, :] ** (sign * rel[:, None])
        for fn, signs in ((np.cos, (1.0, 1.0)), (np.sin, (-1.0, 1.0))):
            pair = fn(ang.astype(np.float64)) * sc
            pair = np.stack([pair * signs[0], pair * signs[1]], axis=-1).reshape(T, EB)
            full = (dec[:, :, None] * pair[:, None, :]).reshape(T, D)
            tables.append(full.reshape(NC, P, D).transpose(1, 0, 2))
    rope = np.stack(tables, axis=1).astype(f32)
    parity = np.stack([(s // EB) % 2 == 0, (s // EB) % 2 == 1], axis=1).astype(f32)
    head = s // EB
    state_mask = np.zeros((P, KK, P), f32)
    for g in range(KK):
        state_mask[:, g, :] = (head[:, None] == head[None, :]) * (gam.astype(np.float64)[g * 8 + head] ** P)[:, None]
    return dict(ident=np.eye(P, dtype=f32), mask=mask, decay_w=decay_w.astype(f32), rope=rope,
                parity=parity, state_mask=state_mask)


def kernel(x, ctx_1024, L0_attn_Wq, L0_attn_Wk, L0_attn_Wv, L0_attn_Wf, L0_attn_g_norm_w, L0_attn_Wo,
           L0_xattn_W_Q, L0_xattn_W_K, L0_xattn_W_V, L0_xattn_g_w, L0_xattn_g_b, L0_xattn_out_w, L0_xattn_out_b,
           L0_ffn_w1, L0_ffn_b1, L0_ffn_w2, L0_ffn_b2):
    import concourse.bacc as bacc
    from concourse.bass_utils import run_bass_kernel_spmd

    def tokens(a):
        return a.reshape(B, NC, P, D).transpose(0, 2, 1, 3)

    def features(a):
        return a.transpose(0, 2, 1).reshape(B, KK, P, T).transpose(0, 2, 1, 3)

    def weight(w):
        return w.reshape(w.shape[0] // P, P, w.shape[1]).transpose(1, 0, 2)

    def head_weight(w):
        return weight(w.transpose(1, 0, 2).reshape(D, D))

    def row(b):
        return np.broadcast_to(b[None, :], (P, D))

    arrays = dict(
        x_tok=tokens(x), x_feat=features(x), c_feat=features(ctx_1024),
        wq=weight(L0_attn_Wq), wk=weight(L0_attn_Wk), wv=weight(L0_attn_Wv), wf=weight(L0_attn_Wf),
        gcol=np.concatenate([L0_attn_g_norm_w] * 2)[:, None], wo=weight(L0_attn_Wo),
        rq=head_weight(L0_xattn_W_Q), rk=head_weight(L0_xattn_W_K), rv=head_weight(L0_xattn_W_V),
        gw=weight(L0_xattn_g_w.transpose(1, 0)), gb=row(L0_xattn_g_b),
        ow=weight(L0_xattn_out_w.transpose(1, 0)), ob=row(L0_xattn_out_b),
        w1=weight(L0_ffn_w1), b1=L0_ffn_b1.reshape(NF, P).transpose(1, 0), w2=weight(L0_ffn_w2), b2=row(L0_ffn_b2),
        **shape_constants())
    nc = bacc.Bacc("TRN2", target_bir_lowering=False, num_devices=1)
    ins, feed = {}, {}
    for name, a in arrays.items():
        a = np.ascontiguousarray(a)
        feed[f"in_{name}"] = a
        ins[name] = nc.dram_tensor(f"in_{name}", a.shape, mybir.dt.from_np(a.dtype), kind="ExternalInput").ap()
    out = nc.dram_tensor("out_rows", (NT, P, 4, D), F32, kind="ExternalOutput").ap()
    decoder_kernel(nc, out=out, **ins)
    r = run_bass_kernel_spmd(nc, [feed], core_ids=[0])
    got = r.results[0]["out_rows"]
    return got.transpose(0, 2, 1, 3).reshape(B, T, D)
```
